# Optimizing a Trainium2 kernel written in Bass

```python
import numpy as np
import jax
import jax.numpy as jnp

def _softmax(x, axis=-1):
    return jax.nn.softmax(x, axis=axis)

def _gelu(x):
    return jax.nn.gelu(x, approximate=True)

def _silu(x):
    return jax.nn.silu(x)

def _sigmoid(x):
    return jax.nn.sigmoid(x)

def _layernorm(x, axis=-1, eps=1e-05):
    m = jnp.mean(x, axis=axis, keepdims=True)
    v = jnp.var(x, axis=axis, keepdims=True)
    return (x - m) / jnp.sqrt(v + eps)

def _scatter_add(tgt, idx, src, axis=0):
    return tgt.at[idx].add(src)

def _segment_sum(src, seg, n):
    return jax.ops.segment_sum(src, seg, n)
kernel_name = 'mk_flamingo_gated_d1_seqx_r4_7cbdac'

def setup_inputs(seed: int=0):
    np.random.seed(seed)
    _w = jnp.asarray

    def _rec_inputs():
        import jax
        import jax.numpy as jnp
        _rk = jax.random.key(seed)
        x = -0.0002928 + 1 * jax.random.normal(jax.random.fold_in(_rk, 1), (4, 512, 256), jnp.float32)
        _lenS = 512 - jax.random.randint(jax.random.fold_in(_rk, 7), (4,), 0, max(1, 512 // 4) + 1, jnp.int32)
        _lenS2 = 512 - jax.random.randint(jax.random.fold_in(_rk, 8), (4,), 0, max(1, 512 // 4) + 1, jnp.int32)
        _ctx_512P = jax.random.normal(jax.random.fold_in(_rk, 11), (4, 16, 128), jnp.float32)
        _ctx_512c = jax.random.dirichlet(jax.random.fold_in(_rk, 511), 0.3 * jnp.ones((16,), jnp.float32), (4, 512))
        _ctx_512t = jnp.einsum('bsk,bkd->bsd', _ctx_512c, _ctx_512P)
        _ctx_512t = _ctx_512t * jax.lax.rsqrt(jnp.mean(jnp.square(_ctx_512t)) + 1e-12) * 0.953939
        ctx_512 = 0.00222621 + 0.99962 * (_ctx_512t + 0.3 * jax.random.normal(jax.random.fold_in(_rk, 611), (4, 512, 128), jnp.float32))
        _g = jax.random.normal(jax.random.fold_in(_rk, 9001), (2, 1), jnp.float32)
        _g = jnp.sign(_g) * jnp.maximum(jnp.abs(_g), 1.0) + (_g == 0) * 1.0
        g_xattn = _g[0]
        g_ffn = _g[1]
        return (x, ctx_512, g_xattn, g_ffn)
    x, ctx_512, g_xattn, g_ffn = _rec_inputs()

    def _L0_xattn_setup():
        import jax, jax.numpy as jnp
        import numpy as np
        B, T, TC, C, CC, H = (2, 512, 128, 256, 128, 16)
        D = C // H

        def _heads(t):
            b, l, _ = t.shape
            return t.reshape(b, l, H, D).transpose(0, 2, 1, 3)
        key = jax.random.key(seed)
        ks = jax.random.split(key, 18)
        w = lambda k, i, o: jax.random.normal(k, (i, o), jnp.float32) / np.sqrt(i).astype(np.float32)
        return {'x': jax.random.normal(ks[0], (B, T, C), jnp.float32), 'cross_input': jax.random.normal(ks[1], (B, TC, CC), jnp.float32), 'Wk': w(ks[2], C, C), 'bk': jnp.zeros((C,), jnp.float32), 'Wq': w(ks[3], C, C), 'bq': jnp.zeros((C,), jnp.float32), 'Wv': w(ks[4], C, C), 'bv': jnp.zeros((C,), jnp.float32), 'Wck': w(ks[5], CC, C), 'bck': jnp.zeros((C,), jnp.float32), 'Wcq': w(ks[6], C, C), 'bcq': jnp.zeros((C,), jnp.float32), 'Wcv': w(ks[7], CC, C), 'bcv': jnp.zeros((C,), jnp.float32), 'Wp': w(ks[8], C, C), 'bp': jnp.zeros((C,), jnp.float32)}
    _L0_xattn_all = _L0_xattn_setup()
    _L0_xattn_in = {k: v for k, v in _L0_xattn_all.items() if k in ('Wk', 'bk', 'Wq', 'bq', 'Wv', 'bv', 'Wck', 'bck', 'Wcq', 'bcq', 'Wcv', 'bcv', 'Wp', 'bp')}
    del _L0_xattn_all

    def _L0_ffn_setup():
        import jax, jax.numpy as jnp
        import numpy as np
        HIDDEN = 256
        NUM_EXPERTS = 8
        TOP_K = 2
        key = jax.random.key(seed)
        k_x, k_r, k_w1, k_w2 = jax.random.split(key, 4)
        x = jax.random.normal(k_x, (4, 512, HIDDEN), dtype=jnp.float32)
        router_w = jax.random.normal(k_r, (NUM_EXPERTS, HIDDEN), dtype=jnp.float32) * HIDDEN ** (-0.5)
        w1 = jax.random.normal(k_w1, (NUM_EXPERTS, HIDDEN, 2 * HIDDEN), dtype=jnp.float32) * HIDDEN ** (-0.5)
        w2 = jax.random.normal(k_w2, (NUM_EXPERTS, 2 * HIDDEN, HIDDEN), dtype=jnp.float32) * (2 * HIDDEN) ** (-0.5)
        return {'x': x, 'router_w': router_w, 'w1': w1, 'w2': w2}
    _L0_ffn_all = _L0_ffn_setup()
    _L0_ffn_in = {k: v for k, v in _L0_ffn_all.items() if k in ('router_w', 'w1', 'w2')}
    del _L0_ffn_all
    return {'x': x, 'ctx_512': ctx_512, 'g_xattn': g_xattn, 'g_ffn': g_ffn, 'L0_xattn_Wk': _L0_xattn_in['Wk'], 'L0_xattn_bk': _L0_xattn_in['bk'], 'L0_xattn_Wq': _L0_xattn_in['Wq'], 'L0_xattn_bq': _L0_xattn_in['bq'], 'L0_xattn_Wv': _L0_xattn_in['Wv'], 'L0_xattn_bv': _L0_xattn_in['bv'], 'L0_xattn_Wck': _L0_xattn_in['Wck'], 'L0_xattn_bck': _L0_xattn_in['bck'], 'L0_xattn_Wcq': _L0_xattn_in['Wcq'], 'L0_xattn_bcq': _L0_xattn_in['bcq'], 'L0_xattn_Wcv': _L0_xattn_in['Wcv'], 'L0_xattn_bcv': _L0_xattn_in['bcv'], 'L0_xattn_Wp': _L0_xattn_in['Wp'], 'L0_xattn_bp': _L0_xattn_in['bp'], 'L0_ffn_router_w': _L0_ffn_in['router_w'], 'L0_ffn_w1': _L0_ffn_in['w1'], 'L0_ffn_w2': _L0_ffn_in['w2']}

def reference(x, ctx_512, g_xattn, g_ffn, L0_xattn_Wk, L0_xattn_bk, L0_xattn_Wq, L0_xattn_bq, L0_xattn_Wv, L0_xattn_bv, L0_xattn_Wck, L0_xattn_bck, L0_xattn_Wcq, L0_xattn_bcq, L0_xattn_Wcv, L0_xattn_bcv, L0_xattn_Wp, L0_xattn_bp, L0_ffn_router_w, L0_ffn_w1, L0_ffn_w2):
    import jax
    import jax.numpy as jnp

    def _L0_xattn_ref(x, cross_input, Wk, bk, Wq, bq, Wv, bv, Wck, bck, Wcq, bcq, Wcv, bcv, Wp, bp):
        import jax, jax.numpy as jnp
        import numpy as np
        B, T, TC, C, CC, H = (2, 512, 128, 256, 128, 16)
        D = C // H

        def _heads(t):
            b, l, _ = t.shape
            return t.reshape(b, l, H, D).transpose(0, 2, 1, 3)
        scale = np.float32(1.0 / np.sqrt(D))
        q = _heads(x @ Wq + bq)
        k = _heads(x @ Wk + bk)
        v = _heads(x @ Wv + bv)
        att = jnp.einsum('bhqd,bhkd->bhqk', q, k) * scale
        causal = jnp.tril(jnp.ones((T, T), bool))
        att = jnp.where(causal[None, None], att, -jnp.inf)
        y = jnp.einsum('bhqk,bhkd->bhqd', jax.nn.softmax(att, axis=-1), v)
        qc = _heads(x @ Wcq + bcq)
        kc = _heads(cross_input @ Wck + bck)
        vc = _heads(cross_input @ Wcv + bcv)
        attc = jnp.einsum('bhqd,bhkd->bhqk', qc, kc) * scale
        y = y + jnp.einsum('bhqk,bhkd->bhqd', jax.nn.softmax(attc, axis=-1), vc)
        y = y.transpose(0, 2, 1, 3).reshape(x.shape[0], T, C)
        return y @ Wp + bp

    def _L0_ffn_ref(x, router_w, w1, w2):
        import jax, jax.numpy as jnp
        import numpy as np
        HIDDEN = 256
        NUM_EXPERTS = 8
        TOP_K = 2
        bsz, seq, hidden = x.shape
        tokens = x.reshape(-1, hidden)
        logits = tokens @ router_w.T
        topk_vals, topk_idx = jax.lax.top_k(logits, TOP_K)
        weights = jax.nn.softmax(topk_vals, axis=-1)
        h = jnp.einsum('td,edf->etf', tokens, w1)
        h = jax.nn.gelu(h, approximate=False)
        out_all = jnp.einsum('etf,efd->etd', h, w2)
        out_ted = jnp.transpose(out_all, (1, 0, 2))
        gathered = jnp.take_along_axis(out_ted, topk_idx[:, :, None], axis=1)
        output = jnp.sum(weights[:, :, None] * gathered, axis=1)
        return output.reshape(bsz, seq, hidden)
    x = x + jnp.tanh(g_xattn[0]) * _L0_xattn_ref(_layernorm(x, axis=-1), ctx_512, L0_xattn_Wk, L0_xattn_bk, L0_xattn_Wq, L0_xattn_bq, L0_xattn_Wv, L0_xattn_bv, L0_xattn_Wck, L0_xattn_bck, L0_xattn_Wcq, L0_xattn_bcq, L0_xattn_Wcv, L0_xattn_bcv, L0_xattn_Wp, L0_xattn_bp)
    x = x + jnp.tanh(g_ffn[0]) * _L0_ffn_ref(_layernorm(x, axis=-1), L0_ffn_router_w, L0_ffn_w1, L0_ffn_w2)
    return x

_drawn_inputs = setup_inputs


def setup_inputs(seed=0):
    import zlib

    import numpy as np

    out = dict(_drawn_inputs(seed))
    spreads = {'L0_xattn_bk': (0.0, 0.1),
     'L0_xattn_bq': (0.0, 0.1),
     'L0_xattn_bv': (0.0, 0.1),
     'L0_xattn_bck': (0.0, 0.1),
     'L0_xattn_bcq': (0.0, 0.1),
     'L0_xattn_bcv': (0.0, 0.1),
     'L0_xattn_bp': (0.0, 0.1)}
    factors = {}
    for name, (base, spread) in spreads.items():
        noise = np.random.default_rng([zlib.crc32(name.encode()), seed]).standard_normal(out[name].shape)
        drawn = base * np.exp(spread * noise) if base else spread * noise
        out[name] = jnp.asarray(drawn.astype(out[name].dtype))
    for name, factor in factors.items():
        out[name] = (out[name] * factor).astype(out[name].dtype)
    return out
```

```python
from contextlib import ExitStack

import concourse.bass as bass
from concourse import mybir

F32 = mybir.dt.float32
F16 = mybir.dt.float16
BF16 = mybir.dt.bfloat16
U32 = mybir.dt.uint32
ACT = mybir.ActivationFunctionType
ALU = mybir.AluOpType
X = mybir.AxisListType.X

P = 128
EPS = 1e-5
MASKED = -1e30


def flamingo_layer(nc, x, ctx_512, g_xattn, g_ffn, Wk, bk, Wq, bq, Wv, bv, Wck, bck, Wcq, bcq,
                   Wcv, bcv, Wp, bp, router_w, w1, w2, out):
    B, T, C = x.shape
    S, CC = ctx_512.shape[1:]
    H = 16
    D = C // H
    TT = T // P
    KT = C // P
    G = H // 4
    NE, _, F = w1.shape
    FT = F // P
    SCALE = 0.25
    assert D == 16 and SCALE == float(D) ** -0.5 and T == S == 512 and C == 256 and CC == P and F == 512
    CQ, CK, CCQ, CV, CP, CCK, CCV = 0, 2, 4, 6, 8, 10, 11
    NCH = 12
    PROJ = [(CQ, KT), (CK, KT), (CCQ, KT), (CCK, 1)]
    NPT = len(PROJ) * KT
    NPJ = NPT + TT

    proj_dram = nc.dram_tensor("proj_dram", [B, 4, 2, C, T], F16).ap()
    v_dram = nc.dram_tensor("v_dram", [B, TT, P, 2, H * 32], F32).ap()
    x1_dram = nc.dram_tensor("x1_dram", [B, TT, P, C], F32).ap()
    x2t_dram = nc.dram_tensor("x2t_dram", [B, 2, C, T], F16).ap()
    gate_dram = nc.dram_tensor("gate_dram", [B, P, TT * NE], F32).ap()

    x_rows = x.rearrange("b (t p) c -> b t p c", p=P)
    ctx_rows = ctx_512.rearrange("b (t p) c -> b t p c", p=P)
    out_rows = out.rearrange("b (t p) c -> b t p c", p=P)

    with ExitStack() as whole:
        def sem(name):
            return whole.enter_context(nc.semaphore(name))

        def wait(eng, s, value):
            if not (isinstance(value, int) and value <= 0):
                eng.wait_ge(s, value)

        bank = whole.enter_context(nc.psum_tensor("bank", [P, 8, 512], F32))
        ident = whole.enter_context(nc.sbuf_tensor("ident", [P, P], F32))
        ident_bf = whole.enter_context(nc.sbuf_tensor("ident_bf", [P, P], BF16))
        future = whole.enter_context(nc.sbuf_tensor("future", [P, P], BF16))
        w_hi = whole.enter_context(nc.sbuf_tensor("w_hi", [P, NCH, C], F16))
        w_lo = whole.enter_context(nc.sbuf_tensor("w_lo", [P, NCH, C], F16))
        tanh_g = whole.enter_context(nc.sbuf_tensor("tanh_g", [P, 2], F32))
        tick = whole.enter_context(nc.sbuf_tensor("tick", [P, 1], F32))
        pool_tick = whole.enter_context(nc.sbuf_tensor("pool_tick", [P, 1], F32))
        half_neg = whole.enter_context(nc.sbuf_tensor("half_neg", [P, TT], F32))

        s_load = sem("s_load")
        s_consts = sem("s_consts")
        s_wscaled = sem("s_wscaled")
        s_whi = sem("s_whi")
        s_wlo = sem("s_wlo")
        s_tanh = sem("s_tanh")
        s_x = sem("s_x")
        s_ctx = sem("s_ctx")
        s_stats = sem("s_stats")
        s_aggr = sem("s_aggr")
        s_var = sem("s_var")
        s_rstd = sem("s_rstd")
        s_xn = sem("s_xn")
        s_tr = sem("s_tr")
        s_trhi = sem("s_trhi")
        s_trlo = sem("s_trlo")
        s_pj = sem("s_pj")
        s_pjhi = sem("s_pjhi")
        s_pjlo = sem("s_pjlo")
        s_projout = sem("s_projout")
        s_vout = sem("s_vout")

        with ExitStack() as phase:
            def sb(name, shape, dt):
                return phase.enter_context(nc.sbuf_tensor(name, shape, dt))

            wf = sb("wf", [P, NCH, C], F32)
            bias_col = sb("bias_col", [P, 4, KT], F32)
            bias_row = sb("bias_row", [P, 2, C], F32)
            x_in = sb("x_in", [P, TT, C], F32)
            ctx_in = sb("ctx_in", [P, TT, CC], F32)
            stats = sb("stats", [P, TT, 6], F32)
            mean_var = sb("mean_var", [P, TT, 2], F32)
            var_eps = sb("var_eps", [P, TT], F32)
            rstd = sb("rstd", [P, TT], F32)
            xn = sb("xn", [P, TT, C], F32)
            xt_hi = sb("xt_hi", [P, KT + 1, T], F16)
            xt_lo = sb("xt_lo", [P, KT + 1, T], F16)
            pj_out = sb("pj_out", [P, NPT, 2, T], F16)
            v_out = sb("v_out", [P, TT, 2, H, 32], F32)
            g_in = sb("g_in", [P, 2], F32)
            block = phase.enter_context(nc.Block())

            def store(sp, b):
                for n in range(NPT):
                    sp.wait_ge(s_pjlo, b * NPJ + n + 1)
                    sp.dma_start(
                        proj_dram[b, n // KT, :, (n % KT) * P:(n % KT + 1) * P, :].rearrange("l p n -> p l n"),
                        pj_out[:, n]).then_inc(s_projout, 16)
                for t in range(TT):
                    sp.wait_ge(s_pjlo, b * NPJ + NPT + t + 1)
                    sp.dma_start(v_dram[b, t], v_out[:, t].rearrange("p a h e -> p a (h e)")).then_inc(s_vout, 16)

            def last_ring():
                return sum(len(tiles) for g in range(G) for tiles in step_tiles(g, False, True))

            @block.sync
            def _(sp):
                sp.dma_start(x_in[:], x_rows[0].rearrange("t p c -> p t c")).then_inc(s_x, 16)
                sp.dma_start(ctx_in[:], ctx_rows[0].rearrange("t p c -> p t c")).then_inc(s_ctx, 16)
                for w, at, k in ((Wq, CQ, KT), (Wk, CK, KT), (Wcq, CCQ, KT), (Wv, CV, KT), (Wp, CP, KT),
                                 (Wck, CCK, 1), (Wcv, CCV, 1)):
                    sp.dma_start(wf[:, at:at + k, :], w.rearrange("(k p) n -> p k n", p=P)).then_inc(s_load, 16)
                for n, v in enumerate((bq, bk, bcq, bck)):
                    sp.dma_start(bias_col[:, n, :], v.rearrange("(k p) -> p k", p=P),
                                   allow_slow_non_contiguous=True).then_inc(s_load, 16)
                for n, v in enumerate((bv, bcv)):
                    sp.dma_start(bias_row[:, n, :], v.partition_broadcast(P)).then_inc(s_load, 16)
                sp.dma_start(g_in[:, 0:1], g_xattn.partition_broadcast(P)).then_inc(s_load, 16)
                sp.dma_start(g_in[:, 1:2], g_ffn.partition_broadcast(P)).then_inc(s_load, 16)
                def projections(b):
                    sp.wait_ge(s_xn, b + 1)
                    sp.dma_start(x_in[:], x_rows[b + 1].rearrange("t p c -> p t c")).then_inc(s_x, 16)
                    sp.wait_ge(s_tr, b * 3 + 3)
                    sp.dma_start(ctx_in[:], ctx_rows[b + 1].rearrange("t p c -> p t c")).then_inc(s_ctx, 16)
                    store(sp, b)

                projections(0)
                with sp.Fori(1, B - 1) as b:
                    projections(b)
                store(sp, B - 1)
                sp.wait_ge(s_projout, 16 * NPT * B)
                sp.wait_ge(s_vout, 16 * TT * B)

            @block.gpsimd
            def _(pool):
                pool.memset(ident[:], 0.0).then_inc(s_consts, 1)
                pool.memset(ident_bf[:], 0.0).then_inc(s_consts, 1)
                pool.memset(future[:], 0.0).then_inc(s_consts, 1)
                pool.memset(half_neg[:], -0.5).then_inc(s_consts, 1)
                pool.memset(v_out[:], 1.0).then_inc(s_consts, 1)
                pool.wait_ge(s_consts, 5)
                diagonal = dict(pattern=[[-1, P]], base=0, channel_multiplier=1)
                pool.affine_select(out=ident[:], in_=ident[:], compare_op=ALU.not_equal, fill=1.0,
                                   **diagonal).then_inc(s_consts, 1)
                pool.affine_select(out=ident_bf[:], in_=ident_bf[:], compare_op=ALU.not_equal, fill=1.0,
                                   **diagonal).then_inc(s_consts, 1)
                pool.affine_select(out=future[:], in_=future[:], compare_op=ALU.is_ge, fill=MASKED,
                                   **diagonal).then_inc(s_consts, 1)

                def inverse_root(b):
                    pool.wait_ge(s_var, b + 1)
                    pool.tensor_tensor(rstd[:], var_eps[:], half_neg[:], ALU.pow).then_inc(s_rstd, 1)

                inverse_root(0)
                with pool.Fori(0, B - 1) as b:
                    inverse_root(b + 1)

            @block.scalar
            def _(act):
                act.wait_ge(s_load, 16 * 15)
                act.activation(tanh_g[:], g_in[:], ACT.Tanh).then_inc(s_tanh, 1)
                act.wait_ge(s_wscaled, 3)
                def projections(b):
                    for n in range(KT + 1):
                        act.wait_ge(s_tr, b * 3 + n + 1)
                        if n == 0:
                            wait(act, s_pj, b * NPJ)
                        act.activation(xt_hi[:, n, :], bank[:, n, :], ACT.Copy).then_inc(s_trhi, 1)
                    for n in range(NPT):
                        act.wait_ge(s_pj, b * NPJ + n + 1)
                        if n == 0:
                            wait(act, s_projout, b * (16 * NPT))
                        act.activation(pj_out[:, n, 0, :], bank[:, 3 + n % 4, :], ACT.Identity,
                                       bias=bias_col[:, n // KT, n % KT:n % KT + 1]).then_inc(s_pjhi, 1)

                projections(0)
                with act.Fori(1, B) as b:
                    projections(b)

            @block.vector
            def _(dve):
                def layer_norm(b):
                    dve.wait_ge(s_x, (b + 1) * 16)
                    for t in range(TT):
                        last = dve.bn_stats(stats[:, t, :], x_in[:, t, :])
                    last.then_inc(s_stats, 1)
                    dve.wait_ge(s_stats, b + 1)
                    dve.memset(tick[:], 0.0)
                    for t in range(TT):
                        last = dve.bn_aggr(mean_var[:, t, :], stats[:, t, :])
                    last.then_inc(s_aggr, 1)
                    dve.wait_ge(s_aggr, b + 1)
                    dve.tensor_scalar(var_eps[:], mean_var[:, :, 1], EPS, None, ALU.add).then_inc(s_var, 1)
                    dve.wait_ge(s_rstd, b + 1)
                    wait(dve, s_tr, b * 3)
                    for t in range(TT):
                        last = dve.tensor_scalar(xn[:, t, :], x_in[:, t, :], mean_var[:, t, 0:1], rstd[:, t:t + 1],
                                                 ALU.subtract, ALU.mult)
                    last.then_inc(s_xn, 1)

                def transposed_low(b):
                    for n in range(KT + 1):
                        dve.wait_ge(s_trhi, b * 3 + n + 1)
                        dve.tensor_tensor(xt_lo[:, n, :], bank[:, n, :], xt_hi[:, n, :], ALU.subtract).then_inc(s_trlo, 1)

                def projected(b, n):
                    if n < NPT:
                        dve.wait_ge(s_pjhi, b * NPT + n + 1)
                        dve.scalar_tensor_tensor(out=pj_out[:, n, 1, :], in0=bank[:, 3 + n % 4, :],
                                                 scalar=bias_col[:, n // KT, n % KT:n % KT + 1],
                                                 in1=pj_out[:, n, 0, :], op0=ALU.add,
                                                 op1=ALU.subtract).then_inc(s_pjlo, 1)
                    else:
                        dve.wait_ge(s_pj, b * NPJ + n + 1)
                        if n == NPT:
                            wait(dve, s_vout, b * (16 * TT))
                        dve.tensor_tensor(v_out[:, n - NPT, :, :, 0:D],
                                          bank[:, 3 + n % 4, :].rearrange("p (a h d) -> p a h d", a=2, h=H),
                                          bias_row[:].rearrange("p a (h d) -> p a h d", h=H),
                                          ALU.add).then_inc(s_pjlo, 1)

                dve.wait_ge(s_consts, 5)
                layer_norm(0)
                dve.wait_ge(s_load, 16 * 15)
                dve.tensor_scalar(wf[:, CQ:CQ + KT, :], wf[:, CQ:CQ + KT, :], SCALE, None, ALU.mult).then_inc(s_wscaled, 1)
                dve.tensor_scalar(wf[:, CCQ:CCQ + KT, :], wf[:, CCQ:CCQ + KT, :], SCALE, None,
                                  ALU.mult).then_inc(s_wscaled, 1)
                dve.tensor_scalar(bias_col[:, 0:3:2, :], bias_col[:, 0:3:2, :], SCALE, None, ALU.mult).then_inc(s_wscaled, 1)
                dve.wait_ge(s_wscaled, 3)
                dve.tensor_copy(w_hi[:], wf[:]).then_inc(s_whi, 1)
                dve.wait_ge(s_whi, 1)
                dve.tensor_tensor(w_lo[:], wf[:], w_hi[:], ALU.subtract).then_inc(s_wlo, 1)
                def projections(b):
                    transposed_low(b)
                    for n in range(NPJ):
                        projected(b, n)
                        if n == 3:
                            layer_norm(b + 1)

                projections(0)
                with dve.Fori(1, B - 1) as b:
                    projections(b)
                transposed_low(B - 1)
                for n in range(NPJ):
                    projected(B - 1, n)

            @block.tensor
            def _(pe):
                pe.wait_ge(s_consts, 8)
                pe.wait_ge(s_wlo, 1)
                def projections(b):
                    pe.wait_ge(s_xn, b + 1)
                    wait(pe, s_trlo, b * 3)
                    for k in range(KT):
                        for t in range(TT):
                            last = pe.transpose(bank[:, k, t * P:(t + 1) * P], xn[:, t, k * P:(k + 1) * P], ident[:])
                        last.then_inc(s_tr, 1)
                    pe.wait_ge(s_ctx, (b + 1) * 16)
                    for t in range(TT):
                        last = pe.transpose(bank[:, KT, t * P:(t + 1) * P], ctx_in[:, t, :], ident[:])
                    last.then_inc(s_tr, 1)
                    pe.wait_ge(s_trlo, b * 3 + 3)
                    for n in range(NPJ):
                        wait(pe, s_pjlo, b * NPJ + (n - 3))
                        if n < NPT:
                            at, nk = PROJ[n // KT]
                            m = slice((n % KT) * P, (n % KT + 1) * P)
                            for k in range(nk):
                                xk = k if nk > 1 else KT
                                for w, a in ((w_hi, xt_hi), (w_hi, xt_lo), (w_lo, xt_hi)):
                                    last = pe.matmul(bank[:, 3 + n % 4, :], w[:, at + k, m], a[:, xk, :],
                                                     start=(k == 0 and w is w_hi and a is xt_hi),
                                                     stop=(k == nk - 1 and w is w_lo))
                        else:
                            t = slice((n - NPT) * P, (n - NPT + 1) * P)
                            for half, at, xk, nk in ((0, CV, 0, KT), (1, CCV, KT, 1)):
                                for k in range(nk):
                                    for w, a in ((w_hi, xt_hi), (w_lo, xt_hi), (w_hi, xt_lo)):
                                        last = pe.matmul(bank[:, 3 + n % 4, half * C:(half + 1) * C], a[:, xk + k, t],
                                                         w[:, at + k, :],
                                                         start=(k == 0 and w is w_hi and a is xt_hi),
                                                         stop=(k == nk - 1 and a is xt_lo))
                        last.then_inc(s_pj, 1)

                projections(0)
                with pe.Fori(1, B) as b:
                    projections(b)

        NM = 26
        PER_STEP = NM + 3
        FINISH = 4
        RING, RING_BANK = 3, 4
        SUM_BANK = 7
        MT_CROSS = [("cross", j, q) for j in range(4) for q in range(TT)]
        MT_SELF = [("self3", j, 0) for j in range(4)] + [("self02", j, 0) for j in range(4)] + \
                  [("self1", 0, 0), ("self1", 2, 0)]
        MAX_TILES = MT_CROSS + MT_SELF
        assert len(MAX_TILES) == NM

        def step_tiles(g, first, last):
            cuts = [3, 7, 10, 14, 17, 21, 24, 26] if g else [3, 6, 9, 12, 15, 19, 23, 26]
            units, at = [], 0
            for u in range(8):
                tiles = []
                if u == 1 and not (last and g == G - 1):
                    tiles.append(("turn_max", g + 1, len(units[0])))
                if u == 2 and not (g == 0 and first):
                    tiles.append(("turn_cross", g - 1, 0))
                if g == 0 and not first and u == 3:
                    tiles += [("turn_y", 0, 0), ("turn_y", 1, 0)]
                if g == 0 and not first and u == 4:
                    tiles += [("project", 0, 0), ("project", 1, 0)]
                if not (last and g >= G - 2):
                    tiles += MAX_TILES[at:cuts[u]]
                    at = cuts[u]
                if u == 6:
                    tiles.append(("turn_self", g, 0))
                units.append(tiles)
            return units

        AHEAD = 2 * NM + 1
        FIRST_BATCH = AHEAD + G * PER_STEP - 1
        PER_BATCH = G * PER_STEP + FINISH
        assert FIRST_BATCH % RING == 0 and PER_BATCH % RING == 0

        def ring_index(b, n):
            if isinstance(b, int) and b == 0:
                return AHEAD + n, RING_BANK + (AHEAD + n) % RING
            return b * PER_BATCH + (FIRST_BATCH - PER_BATCH + n), RING_BANK + n % RING

        def turned(b, g, half, last):
            tile = ("turn_cross", g, 0) if half else ("turn_self", g, 0)
            n = 0
            for k in range(G):
                for tiles in step_tiles(k, isinstance(b, int) and b == 0, last):
                    for one in tiles:
                        n += 1
                        if one == tile:
                            return ring_index(b, n)[0]
            tile = (tile[0], g % G, 0)
            step = [one for tiles in step_tiles(G - 1, False, False) for one in tiles]
            return ring_index(b, step.index(tile) + 1 - len(step))[0]

        s_zeroed = sem("s_zeroed")
        s_stack = [sem(f"s_stack{g}") for g in range(G)]
        s_scores = sem("s_scores")
        s_exp = sem("s_exp")
        s_causal = sem("s_causal")
        s_pv = sem("s_pv")
        s_oout = sem("s_oout")
        s_full = sem("s_full")
        s_free = sem("s_free")
        s_link = sem("s_link")
        s_maxrow = sem("s_maxrow")
        s_xa = sem("s_xa")
        s_x1out = sem("s_x1out")
        s_tbp = sem("s_tbp")
        s_ones = sem("s_ones")
        LOADS = 18

        with ExitStack() as phase:
            def sb(name, shape, dt):
                return phase.enter_context(nc.sbuf_tensor(name, shape, dt))

            q_st = sb("q_st", [P, G, 2, 4, T], F16)
            k_st = sb("k_st", [P, G, 2, 4, T], F16)
            v_st = sb("v_st", [P, G, 2, TT, 4 * 32], F32)
            probs = sb("probs", [P, 4, 4, T], F32)
            o_sb = sb("o_sb", [P, 2, T], F32)
            negmax = sb("negmax", [P, 2, TT, 8], F32)
            maxrow = sb("maxrow", [8, T], F16)
            ones_row = sb("ones_row", [1, T], F16)
            rec = sb("rec", [P, 2, TT, 4], F32)
            part = sb("part", [P, TT, 4, D], F32)
            y = sb("y", [P, TT, C], F32)
            yt_hi = sb("yt_hi", [P, KT, T], F16)
            yt_lo = sb("yt_lo", [P, KT, T], F16)
            xa = sb("xa", [P, TT, C], F32)
            x1 = sb("x1", [P, TT, C], F32)
            tbp = sb("tbp", [P, C], F32)
            block = phase.enter_context(nc.Block())

            @block.sync
            def _(sp):
                def load_group(b, g):
                    rows = slice(g * 64, (g + 1) * 64)
                    for n, (dst, which) in enumerate(((q_st, 0), (q_st, 2))):
                        for half in range(2):
                            for rep in range(2):
                                r = 32 * half + 16 * rep
                                sp.dma_start(dst[r:r + 16, g, n], proj_dram[b, which, half, rows, :].rearrange(
                                    "(j d) n -> d j n", d=D)).then_inc(s_stack[g], 16)
                    for n, (dst, which) in enumerate(((k_st, 1), (k_st, 3))):
                        for rep in range(2):
                            for half in range(2):
                                r = 32 * rep + 16 * half
                                sp.dma_start(dst[r:r + 16, g, n], proj_dram[b, which, half, rows, :].rearrange(
                                    "(j d) n -> d j n", d=D)).then_inc(s_stack[g], 16)
                    for n in range(2):
                        sp.dma_start(v_st[:, g, n], v_dram[b, :, :, n, g * 128:(g + 1) * 128].rearrange(
                            "t p e -> p t e")).then_inc(s_stack[g], 16)

                def max_rows(g, ring):
                    sp.wait_ge(s_free, ring + 1)
                    for n in range(2):
                        sp.dma_start(q_st[127:128, g, n], maxrow[4 * n:4 * n + 4, :]).then_inc(s_maxrow, 16)

                sp.wait_ge(s_ones, 1)
                for g in range(G):
                    load_group(0, g)
                sp.dma_start(tbp[:], bp.partition_broadcast(P)).then_inc(s_tbp, 16)
                sp.wait_ge(s_zeroed, 2)
                for g in range(G):
                    for n in range(2):
                        for j in range(4):
                            sp.dma_start(k_st[127:128, g, n, j, :], ones_row[:]).then_inc(s_ones, 16)
                max_rows(0, 2 * NM)

                def batch(b, first, last):
                    n = 0
                    for g in range(G):
                        units = step_tiles(g, first, last)
                        if not (last and g == G - 1):
                            max_rows((g + 1) % G, ring_index(b, n + len(units[0]))[0])
                        if not (first and g == 0):
                            if g > 0 and not last:
                                sp.wait_ge(s_pv, b * 32 + 8 * g)
                                load_group(b + 1, g - 1)
                            if g == 0:
                                sp.wait_ge(s_pv, b * 32)
                                load_group(b, G - 1)
                        n += sum(len(tiles) for tiles in units)
                        if g == 0:
                            if not first:
                                store_x1(b - 1, finish_ring(b))
                            sp.dma_start(xa[:], x_rows[b].rearrange("t p c -> p t c")).then_inc(s_xa, 16)

                def finish_ring(b):
                    n = 0
                    for tiles in step_tiles(0, False, False)[:4]:
                        n += len(tiles)
                    return ring_index(b, n + 1)[0]

                def store_x1(b, ring):
                    sp.wait_ge(s_free, ring + 1)
                    sp.dma_start(x1_dram[b].rearrange("t p c -> p t c"), x1[:]).then_inc(s_x1out, 16)

                batch(0, True, False)
                with sp.Fori(1, B - 1) as b:
                    batch(b, False, False)
                batch(B - 1, False, True)
                sp.wait_ge(s_free, ring_index(B - 1, last_ring() + 5)[0])
                sp.dma_start(x1_dram[B - 1].rearrange("t p c -> p t c"), x1[:]).then_inc(s_x1out, 16)
                sp.wait_ge(s_x1out, 16 * B)

            @block.gpsimd
            def _(pool):
                pool.memset(ones_row[:], 1.0).then_inc(s_ones, 1)
                pool.memset(q_st[64:128].bitcast(F32), 0.0).then_inc(s_zeroed, 1)

                def batch(b):
                    for g in range(G):
                        for u in range(4):
                            pool.wait_ge(s_exp, b * 64 + g * 16 + 2 * u + 2)
                            wait(pool, s_causal, b * 16 + g * 4 + u)
                            pool.tensor_tensor(pool_tick[:], half_neg[:, 0:1], half_neg[:, 0:1], ALU.mult)
                            pool.affine_select(out=probs[:, u, :, 0:P], in_=probs[:, u, :, 0:P], pattern=[[0, 4], [1, P]],
                                               compare_op=ALU.is_ge, fill=0.0, base=0,
                                               channel_multiplier=-1).then_inc(s_causal, 1)

                batch(0)
                with pool.Fori(1, B) as b:
                    batch(b)

            @block.scalar
            def _(act):
                def out_of_bank(b, g, half, last=False):
                    act.wait_ge(s_pv, b * 32 + g * 8 + 4 * half + 4)
                    if not (isinstance(b, int) and b == 0 and g == 0):
                        act.wait_ge(s_full, turned(b, g - 1, half, last))
                    act.activation(o_sb[:, half, :], bank[:, SUM_BANK, :], ACT.Copy).then_inc(s_oout, 1)

                def batch(b, first, last):
                    for g in range(G):
                        for u in range(8):
                            n = T - P * u if u < 4 else T
                            wait(act, s_pv, b * 32 + (g * 8 + u - 3))
                            for pair in range(2):
                                act.wait_ge(s_scores, b * 64 + (g * 16 + 2 * u + pair + 1))
                                act.activation(probs[:, u % 4, 2 * pair:2 * pair + 2, 0:n],
                                               bank[:, 2 * pair:2 * pair + 2, 0:n], ACT.Exp).then_inc(s_exp, 1)
                            if u == 0 and not (first and g == 0):
                                out_of_bank(b, g - 1, 1, last)
                            if u == 4:
                                out_of_bank(b, g, 0, last)

                batch(0, True, False)
                with act.Fori(1, B - 1) as b:
                    batch(b, False, False)
                batch(B - 1, False, True)
                out_of_bank(B - 1, G - 1, 1, True)

            @block.vector
            def _(dve):
                links = [0]
                dve.memset(k_st[64:128].bitcast(F32), 0.0).then_inc(s_zeroed, 1)
                dve.wait_ge(s_tbp, 16)
                dve.tensor_scalar(tbp[:], tbp[:], tanh_g[:, 0:1], None, ALU.mult).then_inc(s_tbp, 1)
                dve.wait_ge(s_tbp, 17)

                def consume(b, n, tile, step, link, par=0):
                    kind, a, q = tile
                    ring, at = ring_index(b, n) if n is not None else step
                    dve.wait_ge(s_full, ring + 1)
                    bk_ = bank[:, at, :]
                    if kind == "cross":
                        ins = dve.tensor_reduce(negmax[:, par, q, 4 + a:5 + a], bk_, X, ALU.max, negate=True)
                    elif kind == "self3":
                        ins = dve.tensor_reduce(negmax[:, par, 3, a:a + 1], bk_, X, ALU.max, negate=True)
                    elif kind == "self02":
                        dve.tensor_reduce(negmax[:, par, 0, a:a + 1], bk_[:, 0:P], X, ALU.max, negate=True)
                        ins = dve.tensor_reduce(negmax[:, par, 2, a:a + 1], bk_[:, P:T], X, ALU.max, negate=True)
                    elif kind == "self1":
                        ins = dve.tensor_reduce(negmax[:, par, 1, a:a + 2], bk_.rearrange("p (j n) -> p j n", j=2), X,
                                                ALU.max, negate=True)
                    elif kind == "turn_max":
                        wait(dve, s_maxrow, step_no(b, a) * 32)
                        ins = dve.tensor_copy(maxrow[:], bank[0:8, at, :])
                    elif kind in ("turn_self", "turn_cross"):
                        g = a % G
                        o = bk_.rearrange("p (t j e) -> p t j e", t=TT, j=4)
                        half = int(kind == "turn_cross")
                        dve.reciprocal(rec[:, half], o[:, :, :, D]).then_inc(s_link, 1)
                        link = link + 1
                        dve.wait_ge(s_link, link)
                        r = rec[:, half].unsqueeze(3).broadcast_to([P, TT, 4, D])
                        yg = y[:, :, g * 64:(g + 1) * 64].rearrange("p t (j d) -> p t j d", j=4)
                        if kind == "turn_self":
                            ins = dve.tensor_tensor(yg, o[:, :, :, 0:D], r, ALU.mult)
                        else:
                            dve.tensor_tensor(part[:], o[:, :, :, 0:D], r, ALU.mult).then_inc(s_link, 1)
                            link = link + 1
                            dve.wait_ge(s_link, link)
                            ins = dve.tensor_tensor(yg, yg, part[:], ALU.add)
                    elif kind == "turn_y":
                        dve.tensor_copy(yt_hi[:, a, :], bk_).then_inc(s_link, 1)
                        link = link + 1
                        dve.wait_ge(s_link, link)
                        ins = dve.tensor_tensor(yt_lo[:, a, :], bk_, yt_hi[:, a, :], ALU.subtract)
                    elif kind == "project":
                        if a == 0:
                            dve.wait_ge(s_xa, b_of(b) * 16)
                            wait(dve, s_x1out, b_of(b) * 16 - 16)
                        xs = xa[:, 2 * a:2 * a + 2, :]
                        dve.tensor_tensor(xs, xs, tbp[:].unsqueeze(1).broadcast_to([P, 2, C]), ALU.add).then_inc(s_link, 1)
                        link = link + 1
                        dve.wait_ge(s_link, link)
                        ins = dve.scalar_tensor_tensor(out=x1[:, 2 * a:2 * a + 2, :],
                                                       in0=bk_.rearrange("p (t c) -> p t c", t=2),
                                                       scalar=tanh_g[:, 0:1], in1=xs, op0=ALU.mult, op1=ALU.add)
                    ins.then_inc(s_free, 1)
                    return link

                def b_of(b):
                    return b

                def step_no(b, g):
                    return b * 4 + g

                def batch(b, first, last, link):
                    n = 0
                    for g in range(G):
                        for tiles in step_tiles(g, first, last):
                            for tile in tiles:
                                link = consume(b, n, tile, None, link, g % 2)
                                n += 1
                    return link, n

                for n, tile in enumerate(MAX_TILES + MAX_TILES + [("turn_max", 0, NM)]):
                    consume(0, None, tile, (n, RING_BANK + n % RING), 0, n // NM)
                LINKS = [G + 2 * (G - 1), G * 3 + 4]
                batch(0, True, False, 0)
                with dve.Fori(1, B - 1) as b:
                    batch(b, False, False, b * LINKS[1] + (LINKS[0] - LINKS[1]))
                at = (B - 1) * LINKS[1] + LINKS[0] - LINKS[1]
                at, n = batch(B - 1, False, True, at)
                for k, tile in enumerate((("turn_cross", G - 1, 0), ("turn_y", 0, 0), ("turn_y", 1, 0),
                                          ("project", 0, 0), ("project", 1, 0))):
                    if tile[0] == "project" and tile[1] == 0:
                        dve.wait_ge(s_xa, 16 * B)
                        dve.wait_ge(s_x1out, 16 * (B - 1))
                    at = consume(B - 1, n + k, tile, None, at)

            @block.tensor
            def _(pe):
                def scores_for_max(slot, tile, bk_):
                    kind, a, q = tile

                    def own(j, q, to, width):
                        pe.matmul(bk_[:, to:to + width], q_st[0:96, slot, 0, j, q * P:(q + 1) * P],
                                  k_st[0:96, slot, 0, j, 0:width], start=True, stop=False)
                        return pe.matmul(bk_[:, to + width - P:to + width], ident_bf[:], future[:], start=False, stop=True)

                    if kind == "cross":
                        return pe.matmul(bk_, q_st[0:96, slot, 1, a, q * P:(q + 1) * P], k_st[0:96, slot, 1, a, :],
                                         start=True, stop=True)
                    if kind == "self3":
                        return own(a, 3, 0, T)
                    if kind == "self02":
                        own(a, 0, 0, P)
                        return own(a, 2, P, 3 * P)
                    own(a, 1, 0, 2 * P)
                    return own(a + 1, 1, 2 * P, 2 * P)

                def tile_of(b, ring, at, tile):
                    kind, a, q = tile
                    bk_ = bank[:, at, :]
                    wait(pe, s_free, ring - (RING - 1))
                    if kind in ("cross", "self3", "self02", "self1"):
                        last = scores_for_max(q_slot[0], tile, bk_)
                    elif kind == "turn_max":
                        pe.wait_ge(s_free, ring - q)
                        for t in range(TT):
                            last = pe.transpose(bank[0:8, at, t * P:(t + 1) * P], negmax[:, a % 2, t, :], ident[:])
                    elif kind in ("turn_self", "turn_cross"):
                        half = int(kind == "turn_cross")
                        pe.wait_ge(s_oout, b * 8 + 2 * a + half + 1)
                        for t in range(TT):
                            last = pe.transpose(bk_[:, t * P:(t + 1) * P], o_sb[:, half, t * P:(t + 1) * P], ident[:])
                    elif kind == "turn_y":
                        pe.wait_ge(s_free, ring - a)
                        for t in range(TT):
                            last = pe.transpose(bk_[:, t * P:(t + 1) * P], y[:, t, a * P:(a + 1) * P], ident[:])
                    elif kind == "project":
                        pe.wait_ge(s_free, ring - a)
                        for t in range(2):
                            ts = slice((2 * a + t) * P, (2 * a + t + 1) * P)
                            for k in range(KT):
                                for w, act_ in ((w_hi, yt_hi), (w_lo, yt_hi), (w_hi, yt_lo)):
                                    last = pe.matmul(bk_[:, t * C:(t + 1) * C], act_[:, k, ts], w[:, CP + k, :],
                                                     start=(k == 0 and w is w_hi and act_ is yt_hi),
                                                     stop=(k == KT - 1 and act_ is yt_lo))
                    last.then_inc(s_full, 1)

                q_slot = [0]

                def values(b, g, u):
                    half, kt = u // 4, u % 4
                    q0 = kt * P if half == 0 else 0
                    slot = g % G
                    pe.wait_ge(s_exp, b * 64 + (g * 16 + 2 * u + 2))
                    if half == 0:
                        pe.wait_ge(s_causal, b * 16 + (g * 4 + kt + 1))
                    if kt == 0:
                        wait(pe, s_oout, b * 8 + (2 * g + half))
                    for j in range(4):
                        last = pe.matmul(bank[32 * j:32 * j + 32, SUM_BANK, q0:T],
                                         v_st[:, slot, half, kt, 32 * j:32 * j + 32],
                                         probs[:, kt, j, 0:T - q0], start=(kt == 0), stop=(kt == 3))
                    last.then_inc(s_pv, 1)

                def batch(b, first, last_batch):
                    n = 0
                    for g in range(G):
                        pe.wait_ge(s_maxrow, b * 128 + 32 * (g + 1))
                        units = step_tiles(g, first, last_batch)
                        for u in range(8):
                            half, kt = u // 4, u % 4
                            q0 = kt * P if half == 0 else 0
                            for pair in range(2):
                                wait(pe, s_exp, b * 64 + (g * 16 + 2 * u + pair - 1))
                                for j in (2 * pair, 2 * pair + 1):
                                    last = pe.matmul(bank[:, j, 0:T - q0], k_st[:, g, half, j, kt * P:(kt + 1) * P],
                                                     q_st[:, g, half, j, q0:T], start=True, stop=True)
                                last.then_inc(s_scores, 1)
                            if u == 0 and not (last_batch and g >= G - 2):
                                nb = b + 1 if g < G - 2 else b + 2
                                pe.wait_ge(s_stack[(g + 2) % G], nb * (16 * LOADS))
                            if u > 0 or not (first and g == 0):
                                values(b, g - 1 if u == 0 else g, (u - 1) % 8)
                            q_slot[0] = (g + 2) % G
                            for tile in units[u]:
                                ring, at = ring_index(b, n)
                                tile_of(b, ring, at, tile)
                                n += 1
                    return n

                pe.wait_ge(s_zeroed, 2)
                pe.wait_ge(s_ones, 1 + 16 * 32)
                for n, tile in enumerate(MAX_TILES + MAX_TILES + [("turn_max", 0, NM)]):
                    if n == 0 or n == NM:
                        q_slot[0] = n // NM
                        pe.wait_ge(s_stack[n // NM], 16 * LOADS)
                    tile_of(0, n, RING_BANK + n % RING, tile)
                batch(0, True, False)
                with pe.Fori(1, B - 1) as b:
                    batch(b, False, False)
                n = batch(B - 1, False, True)
                values(B - 1, G - 1, 7)
                for k, tile in enumerate((("turn_cross", G - 1, 0), ("turn_y", 0, 0), ("turn_y", 1, 0),
                                          ("project", 0, 0), ("project", 1, 0))):
                    ring, at = ring_index(B - 1, n + k)
                    tile_of(B - 1, ring, at, tile)

        s_lw = sem("s_lw")
        s_x1in = sem("s_x1in")
        s_wr = sem("s_wr")
        s_stats2 = sem("s_stats2")
        s_aggr2 = sem("s_aggr2")
        s_var2 = sem("s_var2")
        s_rstd2 = sem("s_rstd2")
        s_xn2 = sem("s_xn2")
        s_tr2 = sem("s_tr2")
        s_tr2hi = sem("s_tr2hi")
        s_tr2lo = sem("s_tr2lo")
        s_logit = sem("s_logit")
        s_logitc = sem("s_logitc")
        s_x2out = sem("s_x2out")
        s_lgout = sem("s_lgout")
        s_lg = sem("s_lg")
        s_route = sem("s_route")
        s_gap = sem("s_gap")
        s_gexp = sem("s_gexp")
        s_x2in = sem("s_x2in")
        s_accin = sem("s_accin")
        s_we = [sem(f"s_we{n}") for n in range(2)]
        s_ehi = sem("s_ehi")
        s_elo = sem("s_elo")
        s_h = sem("s_h")
        s_gelu = sem("s_gelu")
        s_hhi = sem("s_hhi")
        s_hlo = sem("s_hlo")
        s_y = sem("s_y")
        s_acc = sem("s_acc")
        s_out = sem("s_out")

        with ExitStack() as phase:
            def sb(name, shape, dt):
                return phase.enter_context(nc.sbuf_tensor(name, shape, dt))

            x_in = sb("x1_in", [P, TT, C], F32)
            stats = sb("stats2", [P, TT, 6], F32)
            mean_var = sb("mean_var2", [P, TT, 2], F32)
            var_eps = sb("var_eps2", [P, TT], F32)
            rstd = sb("rstd2", [P, TT], F32)
            xn = sb("xn2", [P, TT, C], F32)
            xt_st = sb("xt_st", [P, 2, KT, T], F16)
            wr = sb("wr", [P, KT, NE], F32)
            wr_hi = sb("wr_hi", [P, KT, NE], F16)
            wr_lo = sb("wr_lo", [P, KT, NE], F16)
            lg_st = sb("lg_st", [P, TT, NE], F32)
            lg = sb("lg", [P, B, TT, NE], F32)
            top = sb("top", [P, B, TT, 8], F32)
            top_i = sb("top_i", [P, B, TT, 8], U32)
            top_f = sb("top_f", [P, B, TT, 8], F32)
            gap = sb("gap", [P, B, TT], F32)
            gap_e = sb("gap_e", [P, B, TT], F32)
            g_first = sb("g_first", [P, B, TT], F32)
            g_second = sb("g_second", [P, B, TT], F32)
            g_sum = sb("g_sum", [P, B, TT], F32)
            number = sb("number", [P, NE], F32)
            gate = sb("gate", [P, B, TT, NE], F32)
            gate2 = sb("gate2", [P, B, TT, NE], F32)
            x2t = sb("x2t", [P, B, 2, KT, T], F16)
            acc = sb("acc", [P, B, TT, C], F32)
            we = sb("we", [P, 2, KT * F + FT * C], F32)
            we_hi = sb("we_hi", [P, 2, KT * F + FT * C], F16)
            we_lo = sb("we_lo", [P, 2, KT * F + FT * C], F16)
            h32 = sb("h32", [P, 2, FT, T], F32)
            h_hi = sb("h_hi", [P, 2, FT, T], F16)
            h_lo = sb("h_lo", [P, 2, FT, T], F16)
            block = phase.enter_context(nc.Block())

            @block.sync
            def _(sp):
                for k in range(KT):
                    sp.dma_start(wr[:, k, :], router_w[:, k * P:(k + 1) * P].rearrange("e p -> p e"),
                                 allow_slow_non_contiguous=True).then_inc(s_wr, 16)
                def router(b):
                    wait(sp, s_xn2, b)
                    sp.dma_start(x_in[:], x1_dram[b].rearrange("t p c -> p t c")).then_inc(s_x1in, 16)
                    sp.wait_ge(s_tr2lo, b * KT + KT)
                    for half in range(2):
                        sp.dma_start(x2t_dram[b, half].rearrange("(k p) n -> p k n", p=P),
                                     xt_st[:, half]).then_inc(s_x2out, 16)
                    sp.wait_ge(s_logitc, b + 1)
                    sp.dma_start(gate_dram[b], lg_st[:].rearrange("p t e -> p (t e)")).then_inc(s_lgout, 16)

                router(0)
                with sp.Fori(1, B) as b:
                    router(b)
                sp.wait_ge(s_lgout, 16 * B)
                sp.dma_start(lg[:].rearrange("p b t e -> p b (t e)"), gate_dram.rearrange("b p n -> p b n")).then_inc(s_lg, 16)
                sp.wait_ge(s_x2out, 32 * B)
                for b in range(B):
                    for half in range(2):
                        sp.dma_start(x2t[:, b, half], x2t_dram[b, half].rearrange("(k p) n -> p k n",
                                                                                  p=P)).then_inc(s_x2in, 16)
                    sp.dma_start(acc[:, b], x1_dram[b].rearrange("t p c -> p t c")).then_inc(s_accin, 16)
                def load_pair(e):
                    for par in range(2):
                        wait(sp, s_elo, e + (par - 1))
                        sp.dma_start(we[:, par, 0:KT * F].rearrange("p (k f) -> p k f", k=KT),
                                     w1[e + par].rearrange("(k p) f -> p k f", p=P)).then_inc(s_we[par], 16)
                        sp.dma_start(we[:, par, KT * F:].rearrange("p (k c) -> p k c", k=FT),
                                     w2[e + par].rearrange("(k p) c -> p k c", p=P)).then_inc(s_we[par], 16)

                load_pair(0)
                with sp.Fori(1, NE // 2) as half_e:
                    load_pair(half_e * 2)
                sp.wait_ge(s_acc, NE * B * TT)
                for b in range(B):
                    sp.dma_start(out_rows[b].rearrange("t p c -> p t c"), acc[:, b]).then_inc(s_out, 16)
                sp.wait_ge(s_out, 16 * B)

            @block.gpsimd
            def _(pool):
                with pool.Fori(0, B) as b:
                    pool.wait_ge(s_var2, b + 1)
                    pool.tensor_tensor(rstd[:], var_eps[:], half_neg[:], ALU.pow).then_inc(s_rstd2, 1)

            @block.scalar
            def _(act):
                def router(b):
                    for k in range(KT):
                        act.wait_ge(s_tr2, b * KT + k + 1)
                        if k == 0:
                            wait(act, s_x2out, b * 32)
                            wait(act, s_logit, b)
                        act.activation(xt_st[:, 0, k, :], bank[:, k, :], ACT.Copy).then_inc(s_tr2hi, 1)

                router(0)
                with act.Fori(1, B) as b:
                    router(b)
                act.wait_ge(s_gap, 1)
                act.activation(gap_e[:], gap[:], ACT.Exp).then_inc(s_gexp, 1)

                def gelu(e, first):
                    for par in range(2):
                        for b in range(B):
                            for m in range(FT):
                                i = (par * B + b) * FT + m
                                act.wait_ge(s_h, e * (B * FT) + (i + 1))
                                wait(act, s_hlo, e * (B * FT) + (i - 2 * FT + 1))
                                act.activation(h32[:, b % 2, m, :], bank[:, m, :], ACT.Gelu).then_inc(s_gelu, 1)

                gelu(0, True)
                with act.Fori(1, NE // 2) as half_e:
                    e = half_e * 2
                    gelu(e, False)

            @block.vector
            def _(dve):
                for e in range(NE):
                    last = dve.memset(number[:, e:e + 1], float(e))
                last.then_inc(s_route, 1)
                dve.wait_ge(s_wr, 16 * KT)
                dve.tensor_copy(wr_hi[:], wr[:]).then_inc(s_route, 1)
                dve.wait_ge(s_route, 2)
                dve.tensor_tensor(wr_lo[:], wr[:], wr_hi[:], ALU.subtract).then_inc(s_lw, 1)
                def router(b):
                    dve.wait_ge(s_x1in, b * 16 + 16)
                    for t in range(TT):
                        last = dve.bn_stats(stats[:, t, :], x_in[:, t, :])
                    last.then_inc(s_stats2, 1)
                    dve.wait_ge(s_stats2, b + 1)
                    dve.memset(tick[:], 0.0)
                    for t in range(TT):
                        last = dve.bn_aggr(mean_var[:, t, :], stats[:, t, :])
                    last.then_inc(s_aggr2, 1)
                    dve.wait_ge(s_aggr2, b + 1)
                    dve.tensor_scalar(var_eps[:], mean_var[:, :, 1], EPS, None, ALU.add).then_inc(s_var2, 1)
                    dve.wait_ge(s_rstd2, b + 1)
                    for t in range(TT):
                        last = dve.tensor_scalar(xn[:, t, :], x_in[:, t, :], mean_var[:, t, 0:1], rstd[:, t:t + 1],
                                                 ALU.subtract, ALU.mult)
                    last.then_inc(s_xn2, 1)
                    for k in range(KT):
                        dve.wait_ge(s_tr2hi, b * KT + k + 1)
                        dve.tensor_tensor(xt_st[:, 1, k, :], bank[:, k, :], xt_st[:, 0, k, :], ALU.subtract).then_inc(s_tr2lo, 1)
                    dve.wait_ge(s_logit, b + 1)
                    wait(dve, s_lgout, b * 16)
                    dve.tensor_copy(lg_st[:].rearrange("p t e -> p (t e)"), bank[:, 2, 0:TT * NE]).then_inc(s_logitc, 1)

                router(0)
                with dve.Fori(1, B) as b:
                    router(b)
                dve.wait_ge(s_lg, 16)
                for b in range(B):
                    for t in range(TT):
                        last = dve.max(top[:, b, t, :], lg[:, b, t, :])
                last.then_inc(s_route, 1)
                dve.wait_ge(s_route, 3)
                for b in range(B):
                    for t in range(TT):
                        dve.max_index(top_i[:, b, t, :], top[:, b, t, :], lg[:, b, t, :])
                dve.tensor_tensor(gap[:], top[:, :, :, 1], top[:, :, :, 0], ALU.subtract).then_inc(s_gap, 1)
                dve.wait_ge(s_gap, 1)
                dve.tensor_copy(top_f[:], top_i[:]).then_inc(s_route, 1)
                dve.wait_ge(s_gexp, 1)
                dve.tensor_scalar(g_sum[:], gap_e[:], 1.0, None, ALU.add).then_inc(s_route, 1)
                dve.wait_ge(s_route, 5)
                dve.reciprocal(g_first[:], g_sum[:]).then_inc(s_route, 1)
                dve.wait_ge(s_route, 6)
                dve.tensor_scalar(g_first[:], g_first[:], tanh_g[:, 1:2], None, ALU.mult).then_inc(s_route, 1)
                dve.wait_ge(s_route, 7)
                dve.tensor_tensor(g_second[:], g_first[:], gap_e[:], ALU.mult).then_inc(s_route, 1)
                dve.wait_ge(s_route, 8)
                for b in range(B):
                    for t in range(TT):
                        dve.tensor_scalar(gate[:, b, t, :], number[:], top_f[:, b, t, 0:1], g_first[:, b, t:t + 1],
                                          ALU.is_equal, ALU.mult)
                        last = dve.tensor_scalar(gate2[:, b, t, :], number[:], top_f[:, b, t, 1:2],
                                                 g_second[:, b, t:t + 1], ALU.is_equal, ALU.mult)
                last.then_inc(s_route, 1)
                dve.wait_ge(s_route, 9)
                dve.tensor_tensor(gate[:], gate[:], gate2[:], ALU.add).then_inc(s_route, 1)
                dve.wait_ge(s_route, 10)
                dve.wait_ge(s_accin, 16 * B)

                def split_expert(e, par):
                    dve.wait_ge(s_we[par], e * 16 + 32)
                    wait(dve, s_y, e * (B * TT) + (par - 1) * (B * TT))
                    dve.tensor_copy(we_hi[:, par, :], we[:, par, :]).then_inc(s_ehi, 1)
                    dve.wait_ge(s_ehi, e + (par + 1))
                    dve.tensor_tensor(we_lo[:, par, :], we[:, par, :], we_hi[:, par, :], ALU.subtract).then_inc(s_elo, 1)

                def accumulate(e, i, t):
                    b = i % B
                    par = i // B % 2
                    dve.wait_ge(s_y, e * (B * TT) + (i * TT + t + 1))
                    yb = bank[:, 4 + t, 0:C]
                    ex = e + (i // B)
                    dve.scalar_tensor_tensor(out=acc[:, b, t, :], in0=yb, scalar=gate[:, b, t, bass.ds(ex, 1)],
                                             in1=acc[:, b, t, :], op0=ALU.mult, op1=ALU.add).then_inc(s_acc, 1)

                def pair(e, first):
                    for i in range(2 * B):
                        if i % B == 0:
                            pass
                        for m in range(FT):
                            n = e * (B * FT) + (i * FT + m)
                            dve.wait_ge(s_gelu, n + 1)
                            wait(dve, s_y, e * (B * TT) + (i - 1) * TT)
                            dve.tensor_copy(h_hi[:, i % 2, m, :], h32[:, i % 2, m, :]).then_inc(s_hhi, 1)
                            if not (first and i == 0):
                                accumulate(e, i - 1, m)
                            dve.wait_ge(s_hhi, n + 1)
                            dve.tensor_tensor(h_lo[:, i % 2, m, :], h32[:, i % 2, m, :], h_hi[:, i % 2, m, :],
                                              ALU.subtract).then_inc(s_hlo, 1)
                        if i == 0:
                            split_expert(e, 1)
                        if i == B:
                            if first is not None:
                                split_expert(e + 2, 0)

                split_expert(0, 0)
                pair(0, True)
                with dve.Fori(1, NE // 2 - 1) as half_e:
                    e = half_e * 2
                    pair(e, False)
                pair(NE - 2, None)
                for t in range(TT):
                    accumulate(NE - 2, 2 * B - 1, t)

            @block.tensor
            def _(pe):
                pe.wait_ge(s_lw, 1)
                def router(b):
                    pe.wait_ge(s_xn2, b + 1)
                    wait(pe, s_tr2lo, b * KT)
                    for k in range(KT):
                        for t in range(TT):
                            last = pe.transpose(bank[:, k, t * P:(t + 1) * P], xn[:, t, k * P:(k + 1) * P], ident[:])
                        last.then_inc(s_tr2, 1)
                    pe.wait_ge(s_tr2lo, b * KT + KT)
                    wait(pe, s_logitc, b)
                    for t in range(TT):
                        ts = slice(t * P, (t + 1) * P)
                        for k in range(KT):
                            for a, w in ((0, wr_hi), (0, wr_lo), (1, wr_hi)):
                                last = pe.matmul(bank[:, 2, t * NE:(t + 1) * NE], xt_st[:, a, k, ts], w[:, k, :],
                                                 start=(k == 0 and a == 0 and w is wr_hi), stop=(k == KT - 1 and a == 1))
                    last.then_inc(s_logit, 1)

                router(0)
                with pe.Fori(1, B) as b:
                    router(b)
                pe.wait_ge(s_x2in, 32 * B)

                def up(e, i):
                    par, b = i // B, i % B
                    if b == 0:
                        pe.wait_ge(s_elo, e + (par + 1))
                    for m in range(FT):
                        wait(pe, s_gelu, e * (B * FT) + (i * FT + m - FT + 1))
                        for k in range(KT):
                            cols = slice(k * F + m * P, k * F + (m + 1) * P)
                            for w, a in ((we_hi, 0), (we_hi, 1), (we_lo, 0)):
                                last = pe.matmul(bank[:, m, :], w[:, par, cols], x2t[:, b, a, k, :],
                                                 start=(k == 0 and w is we_hi and a == 0),
                                                 stop=(k == KT - 1 and w is we_lo))
                        last.then_inc(s_h, 1)

                def down(e, i):
                    par = i // B % 2
                    for t in range(TT):
                        if t == 0:
                            pe.wait_ge(s_hlo, e * (B * FT) + (i + 1) * FT)
                        wait(pe, s_acc, e * (B * TT) + (i * TT + t - TT + 1))
                        for k in range(FT):
                            cols = slice(KT * F + k * C, KT * F + (k + 1) * C)
                            for h, w in ((h_hi, we_hi), (h_hi, we_lo), (h_lo, we_hi)):
                                last = pe.matmul(bank[:, 4 + t, 0:C], h[:, i % 2, k, t * P:(t + 1) * P], w[:, par, cols],
                                                 start=(k == 0 and h is h_hi and w is we_hi),
                                                 stop=(k == FT - 1 and h is h_lo))
                        last.then_inc(s_y, 1)

                def pair(e, first):
                    for i in range(2 * B):
                        up(e, i)
                        if not (first and i == 0):
                            down(e, i - 1)

                pair(0, True)
                with pe.Fori(1, NE // 2) as half_e:
                    e = half_e * 2
                    pair(e, False)
                down(NE - 2, 2 * B - 1)


_INS = ['x', 'ctx_512', 'g_xattn', 'g_ffn', 'L0_xattn_Wk', 'L0_xattn_bk', 'L0_xattn_Wq', 'L0_xattn_bq',
        'L0_xattn_Wv', 'L0_xattn_bv', 'L0_xattn_Wck', 'L0_xattn_bck', 'L0_xattn_Wcq', 'L0_xattn_bcq',
        'L0_xattn_Wcv', 'L0_xattn_bcv', 'L0_xattn_Wp', 'L0_xattn_bp', 'L0_ffn_router_w', 'L0_ffn_w1', 'L0_ffn_w2']
_OUTS = [((4, 512, 256), 'float32')]


def kernel(**inputs):
    import numpy as _np
    import concourse.bacc as _bacc
    from concourse import mybir as _mybir
    from concourse.bass_utils import run_bass_kernel_spmd as _run

    nc = _bacc.Bacc("TRN2", target_bir_lowering=False, num_devices=1)
    arrays, args = {}, []
    for name in _INS:
        a = _np.ascontiguousarray(inputs[name])
        arrays[f"in_{name}_dram"] = a
        args.append(nc.dram_tensor(f"in_{name}_dram", a.shape, _mybir.dt.from_np(a.dtype), kind="ExternalInput").ap())
    for i, (shape, dtype) in enumerate(_OUTS):
        dt = _mybir.dt.from_np(_np.dtype(dtype))
        args.append(nc.dram_tensor(f"out_{i}_dram", shape, dt, kind="ExternalOutput").ap())
    flamingo_layer(nc, *args)
    r = _run(nc, [arrays], core_ids=[0])
    got = tuple(r.results[0][f"out_{i}_dram"] for i in range(len(_OUTS)))
    return got[0]
```

```python
from contextlib import ExitStack

import concourse.bass as bass
from concourse import mybir
import numpy as np

F32 = mybir.dt.float32
F16 = mybir.dt.float16
BF16 = mybir.dt.bfloat16
U32 = mybir.dt.uint32
ACT = mybir.ActivationFunctionType
ALU = mybir.AluOpType
X = mybir.AxisListType.X

P = 128
EPS = 1e-5
MASKED = -1e30


def flamingo_layer(nc, x, ctx_512, g_xattn, g_ffn, Wk, bk, Wq, bq, Wv, bv, Wck, bck, Wcq, bcq,
                   Wcv, bcv, Wp, bp, router_w, w1, w2, out):
    B, T, C = x.shape
    S, CC = ctx_512.shape[1:]
    H = 16
    D = C // H
    TT = T // P
    KT = C // P
    G = H // 4
    NE, _, F = w1.shape
    FT = F // P
    SCALE = 0.25
    assert D == 16 and SCALE == float(D) ** -0.5 and T == S == 512 and C == 256 and CC == P and F == 512
    CQ, CK, CCQ, CV, CP, CCK, CCV = 0, 2, 4, 6, 8, 10, 11
    NCH = 12
    PROJ = [(CQ, KT), (CK, KT), (CCQ, KT), (CCK, 1)]
    NPT = len(PROJ) * KT
    NPJ = NPT + TT

    proj_dram = nc.dram_tensor("proj_dram", [B, 2, G, 2, 64, 2, T], F16).ap()
    v_dram = nc.dram_tensor("v_dram", [B, P, 2 * TT, H * 32], F32).ap()

    x_rows = x.rearrange("b (t p) c -> b t p c", p=P)
    ctx_rows = ctx_512.rearrange("b (t p) c -> b t p c", p=P)
    out_rows = out.rearrange("b (t p) c -> b t p c", p=P)

    with ExitStack() as whole:
        def sem(name):
            return whole.enter_context(nc.semaphore(name))

        def wait(eng, s, value):
            if not (isinstance(value, int) and value <= 0):
                eng.wait_ge(s, value)

        bank = whole.enter_context(nc.psum_tensor("bank", [P, 8, 512], F32))
        ident = whole.enter_context(nc.sbuf_tensor("ident", [P, P], F32))
        ident_bf = whole.enter_context(nc.sbuf_tensor("ident_bf", [P, P], BF16))
        future = whole.enter_context(nc.sbuf_tensor("future", [P, P], BF16))
        w_hi = whole.enter_context(nc.sbuf_tensor("w_hi", [P, NCH, C], F16))
        w_lo = whole.enter_context(nc.sbuf_tensor("w_lo", [P, NCH, C], F16))
        tanh_g = whole.enter_context(nc.sbuf_tensor("tanh_g", [P, 2], F32))
        x1_all = whole.enter_context(nc.sbuf_tensor("x1_all", [P, B, TT, C], F32))
        arena = whole.enter_context(nc.sbuf_tensor("arena", [P, 16384], F32))
        tick = whole.enter_context(nc.sbuf_tensor("tick", [P, 1], F32))
        pool_tick = whole.enter_context(nc.sbuf_tensor("pool_tick", [P, 1], F32))
        half_neg = whole.enter_context(nc.sbuf_tensor("half_neg", [P, TT], F32))

        s_load = sem("s_load")
        s_consts = sem("s_consts")
        s_wscaled = sem("s_wscaled")
        s_whi = sem("s_whi")
        s_wlo = sem("s_wlo")
        s_tanh = sem("s_tanh")
        s_x = sem("s_x")
        s_ctx = sem("s_ctx")
        s_stats = sem("s_stats")
        s_aggr = sem("s_aggr")
        s_var = sem("s_var")
        s_rstd = sem("s_rstd")
        s_xn = sem("s_xn")
        s_tr = sem("s_tr")
        s_trhi = sem("s_trhi")
        s_trlo = sem("s_trlo")
        s_pj = sem("s_pj")
        s_pjhi = sem("s_pjhi")
        s_pjlo = sem("s_pjlo")
        s_projout = sem("s_projout")
        s_vout = sem("s_vout")


        NM = 26
        PER_STEP = NM + 3
        FINISH = 4
        RING, RING_BANK = 3, 4
        SUM_BANK = 7
        MT_CROSS = [("cross", j, q) for j in range(4) for q in range(TT)]
        MT_SELF = [("self3", j, 0) for j in range(4)] + [("self02", j, 0) for j in range(4)] + \
                  [("self1", 0, 0), ("self1", 2, 0)]
        MAX_TILES = MT_CROSS + MT_SELF
        assert len(MAX_TILES) == NM

        def step_tiles(g, first, last):
            cuts = [3, 7, 10, 14, 17, 21, 24, 26] if g else [3, 6, 9, 12, 15, 19, 23, 26]
            units, at = [], 0
            for u in range(8):
                tiles = []
                if u == 1 and not (last and g == G - 1):
                    tiles.append(("turn_max", g + 1, len(units[0])))
                if u == 2 and not (g == 0 and first):
                    tiles.append(("turn_cross", g - 1, 0))
                if g == 0 and not first and u == 3:
                    tiles += [("turn_y", 0, 0), ("turn_y", 1, 0)]
                if g == 0 and not first and u == 4:
                    tiles += [("project", 0, 0), ("project", 1, 0)]
                if not (last and g >= G - 2):
                    tiles += MAX_TILES[at:cuts[u]]
                    at = cuts[u]
                if u == 6:
                    tiles.append(("turn_self", g, 0))
                units.append(tiles)
            return units

        AHEAD = 2 * NM + 1
        FIRST_BATCH = AHEAD + G * PER_STEP - 1
        PER_BATCH = G * PER_STEP + FINISH
        assert FIRST_BATCH % RING == 0 and PER_BATCH % RING == 0

        def ring_index(b, n):
            if isinstance(b, int) and b == 0:
                return AHEAD + n, RING_BANK + (AHEAD + n) % RING
            return b * PER_BATCH + (FIRST_BATCH - PER_BATCH + n), RING_BANK + n % RING

        def turned(b, g, half, last):
            tile = ("turn_cross", g, 0) if half else ("turn_self", g, 0)
            n = 0
            for k in range(G):
                for tiles in step_tiles(k, isinstance(b, int) and b == 0, last):
                    for one in tiles:
                        n += 1
                        if one == tile:
                            return ring_index(b, n)[0]
            tile = (tile[0], g % G, 0)
            step = [one for tiles in step_tiles(G - 1, False, False) for one in tiles]
            return ring_index(b, step.index(tile) + 1 - len(step))[0]

        s_zeroed = sem("s_zeroed")
        s_stack = [sem(f"s_stack{g}") for g in range(G)]
        s_scores = sem("s_scores")
        s_exp = sem("s_exp")
        s_causal = sem("s_causal")
        s_pv = sem("s_pv")
        s_oout = sem("s_oout")
        s_full = sem("s_full")
        s_free = sem("s_free")
        s_link = sem("s_link")
        s_maxrow = sem("s_maxrow")
        s_xa = sem("s_xa")
        s_x1out = sem("s_x1out")
        s_tbp = sem("s_tbp")
        LOADS = 9

        with ExitStack() as phase:
            def sb(name, shape, dt):
                return phase.enter_context(nc.sbuf_tensor(name, shape, dt))

            taken = [0]

            def view(shape, dt):
                words = int(np.prod(shape[1:])) * (1 if dt == F32 else 2) // (1 if dt == F32 else 4)
                part_ = arena[:, taken[0]:taken[0] + words]
                taken[0] += words
                part_ = part_ if dt == F32 else part_.bitcast(dt)
                names = "abcd"[:len(shape) - 1]
                return part_.rearrange("p (%s) -> p %s" % (" ".join(names), " ".join(names)),
                                       **dict(zip(names, shape[1:])))

            wf = view([P, NCH, C], F32)
            x_in = view([P, TT, C], F32)
            ctx_in = view([P, TT, CC], F32)
            xn = view([P, TT, C], F32)
            xt_hi = view([P, KT + 1, T], F16)
            xt_lo = view([P, KT + 1, T], F16)
            pj_out = view([P, NPT, 2, T], F16)
            v_out = view([P, TT, 2, H, 32], F32)
            assert taken[0] <= 16384
            bias_col = sb("bias_col", [P, 4, KT], F32)
            bias_row = sb("bias_row", [P, 2, C], F32)
            stats = sb("stats", [P, TT, 6], F32)
            mean_var = sb("mean_var", [P, TT, 2], F32)
            var_eps = sb("var_eps", [P, TT], F32)
            rstd = sb("rstd", [P, TT], F32)
            g_in = sb("g_in", [P, 2], F32)
            q_st = sb("q_st", [P, G, 2, 4, T], F16)
            k_st = sb("k_st", [P, G, 2, 4, T], F16)
            v_st = sb("v_st", [P, G, 2, TT, 4 * 32], F32)
            probs = arena[:, 8192:].rearrange("p (a b c) -> p a b c", a=4, b=4)
            o_sb = sb("o_sb", [P, 2, T], F32)
            negmax = sb("negmax", [P, 2, TT, 8], F32)
            maxrow = sb("maxrow", [8, T], F16)
            rec = sb("rec", [P, 2, TT, 4], F32)
            part = sb("part", [P, TT, 4, D], F32)
            y = sb("y", [P, TT, C], F32)
            yt_hi = sb("yt_hi", [P, KT, T], F16)
            yt_lo = sb("yt_lo", [P, KT, T], F16)
            xa = sb("xa", [P, TT, C], F32)
            x1 = sb("x1", [P, TT, C], F32)
            tbp = sb("tbp", [P, C], F32)
            block = phase.enter_context(nc.Block())

            def store(sp, b):
                for n in range(NPT):
                    sp.wait_ge(s_pjlo, b * NPJ + n + 1)
                    sp.dma_start(
                        proj_dram[b, n // KT % 2, n % KT * 2:n % KT * 2 + 2, n // KT // 2].rearrange("g r l n -> g r (l n)"),
                        pj_out[:, n].rearrange("p l n -> p (l n)")).then_inc(s_projout, 16)
                for t in range(TT):
                    sp.wait_ge(s_pjlo, b * NPJ + NPT + t + 1)
                    sp.dma_start(v_dram[b, :, t::TT], v_out[:, t].rearrange("p a h e -> p a (h e)")).then_inc(s_vout, 16)

            def last_ring():
                return sum(len(tiles) for g in range(G) for tiles in step_tiles(g, False, True))

            @block.sync
            def _(sp):
                def load_group(b, g):
                    for half in range(2):
                        for rep in range(2):
                            for dst, which, r in ((q_st, 0, 32 * half + 16 * rep), (k_st, 1, 32 * rep + 16 * half)):
                                sp.dma_start(dst[r:r + 16, g].rearrange("d w j n -> d (w j) n"),
                                             proj_dram[b, which, g, :, :, half, :].rearrange(
                                                 "w (j d) n -> d (w j) n", d=D)).then_inc(s_stack[g], 16)
                    sp.dma_start(v_st[:, g].rearrange("p a t e -> p (a t) e"),
                                 v_dram[b, :, :, g * 128:(g + 1) * 128]).then_inc(s_stack[g], 16)

                sp.dma_start(x_in[:], x_rows[0].rearrange("t p c -> p t c")).then_inc(s_x, 16)
                sp.dma_start(ctx_in[:], ctx_rows[0].rearrange("t p c -> p t c")).then_inc(s_ctx, 16)
                for w, at, k in ((Wq, CQ, KT), (Wk, CK, KT), (Wcq, CCQ, KT), (Wv, CV, KT), (Wp, CP, KT),
                                 (Wck, CCK, 1), (Wcv, CCV, 1)):
                    sp.dma_start(wf[:, at:at + k, :], w.rearrange("(k p) n -> p k n", p=P)).then_inc(s_load, 16)
                for n, v in enumerate((bq, bk, bcq, bck)):
                    sp.dma_start(bias_col[:, n, :], v.rearrange("(k p) -> p k", p=P),
                                   allow_slow_non_contiguous=True).then_inc(s_load, 16)
                for n, v in enumerate((bv, bcv)):
                    sp.dma_start(bias_row[:, n, :], v.partition_broadcast(P)).then_inc(s_load, 16)
                sp.dma_start(g_in[:, 0:1], g_xattn.partition_broadcast(P)).then_inc(s_load, 16)
                sp.dma_start(g_in[:, 1:2], g_ffn.partition_broadcast(P)).then_inc(s_load, 16)
                def projections(b):
                    sp.wait_ge(s_xn, b + 1)
                    sp.dma_start(x_in[:], x_rows[b + 1].rearrange("t p c -> p t c")).then_inc(s_x, 16)
                    sp.wait_ge(s_tr, b * 3 + 3)
                    sp.dma_start(ctx_in[:], ctx_rows[b + 1].rearrange("t p c -> p t c")).then_inc(s_ctx, 16)
                    store(sp, b)

                sp.dma_start(tbp[:], bp.partition_broadcast(P)).then_inc(s_tbp, 16)
                projections(0)
                for b in range(1, B - 1):
                    projections(b)
                    sp.wait_ge(s_projout, 16 * NPT * (b + 1))
                    sp.wait_ge(s_vout, 16 * TT * (b + 1))
                    load_group(0, b - 1)
                store(sp, B - 1)
                sp.wait_ge(s_projout, 16 * NPT * B)
                sp.wait_ge(s_vout, 16 * TT * B)

                def max_rows(g, ring):
                    sp.wait_ge(s_free, ring + 1)
                    for n in range(2):
                        sp.dma_start(q_st[127:128, g, n], maxrow[4 * n:4 * n + 4, :]).then_inc(s_maxrow, 16)

                for g in range(B - 2, G):
                    load_group(0, g)
                max_rows(0, 2 * NM)

                def batch(b, first, last):
                    n = 0
                    for g in range(G):
                        units = step_tiles(g, first, last)
                        if not (last and g == G - 1):
                            max_rows((g + 1) % G, ring_index(b, n + len(units[0]))[0])
                        if not (first and g == 0):
                            if g > 0 and not last:
                                sp.wait_ge(s_pv, b * 32 + 8 * g)
                                load_group(b + 1, g - 1)
                            if g == 0:
                                sp.wait_ge(s_pv, b * 32)
                                load_group(b, G - 1)
                        n += sum(len(tiles) for tiles in units)
                        if g == 0:
                            if not first:
                                store_x1(b - 1, finish_ring(b))
                            sp.dma_start(xa[:], x_rows[b].rearrange("t p c -> p t c")).then_inc(s_xa, 16)

                def finish_ring(b):
                    n = 0
                    for tiles in step_tiles(0, False, False)[:4]:
                        n += len(tiles)
                    return ring_index(b, n + 1)[0]

                def store_x1(b, ring):
                    sp.wait_ge(s_free, ring + 1)
                    sp.dma_start(x1_all[:, bass.ds(b, 1)].rearrange("p a t c -> p (a t) c"), x1[:]).then_inc(s_x1out, 16)

                batch(0, True, False)
                with sp.Fori(1, B - 1) as b:
                    batch(b, False, False)
                batch(B - 1, False, True)
                sp.wait_ge(s_free, ring_index(B - 1, last_ring() + 5)[0])
                sp.dma_start(x1_all[:, B - 1], x1[:]).then_inc(s_x1out, 16)
                sp.wait_ge(s_x1out, 16 * B)

            @block.gpsimd
            def _(pool):
                pool.memset(ident[:], 0.0).then_inc(s_consts, 1)
                pool.memset(ident_bf[:], 0.0).then_inc(s_consts, 1)
                pool.memset(future[:], 0.0).then_inc(s_consts, 1)
                pool.memset(half_neg[:], -0.5).then_inc(s_consts, 1)
                pool.memset(v_out[:], 1.0).then_inc(s_consts, 1)
                pool.wait_ge(s_consts, 5)
                diagonal = dict(pattern=[[-1, P]], base=0, channel_multiplier=1)
                pool.affine_select(out=ident[:], in_=ident[:], compare_op=ALU.not_equal, fill=1.0,
                                   **diagonal).then_inc(s_consts, 1)
                pool.affine_select(out=ident_bf[:], in_=ident_bf[:], compare_op=ALU.not_equal, fill=1.0,
                                   **diagonal).then_inc(s_consts, 1)
                pool.affine_select(out=future[:], in_=future[:], compare_op=ALU.is_ge, fill=MASKED,
                                   **diagonal).then_inc(s_consts, 1)

                def inverse_root(b):
                    pool.wait_ge(s_var, b + 1)
                    pool.tensor_tensor(rstd[:], var_eps[:], half_neg[:], ALU.pow).then_inc(s_rstd, 1)

                inverse_root(0)
                pool.wait_ge(s_rstd, 1)
                pool.memset(k_st[64:128], 1.0).then_inc(s_zeroed, 1)
                pool.wait_ge(s_zeroed, 1)
                pool.memset(q_st[64:128].bitcast(F32), 0.0).then_inc(s_zeroed, 1)
                pool.wait_ge(s_zeroed, 2)
                with pool.Fori(0, B - 1) as b:
                    inverse_root(b + 1)

                def batch(b):
                    for g in range(G):
                        for u in range(4):
                            pool.wait_ge(s_exp, b * 64 + g * 16 + 2 * u + 2)
                            wait(pool, s_causal, b * 16 + g * 4 + u)
                            pool.tensor_tensor(pool_tick[:], half_neg[:, 0:1], half_neg[:, 0:1], ALU.mult)
                            pool.affine_select(out=probs[:, u, :, 0:P], in_=probs[:, u, :, 0:P], pattern=[[0, 4], [1, P]],
                                               compare_op=ALU.is_ge, fill=0.0, base=0,
                                               channel_multiplier=-1).then_inc(s_causal, 1)

                batch(0)
                with pool.Fori(1, B) as b:
                    batch(b)

            @block.scalar
            def _(act):
                act.wait_ge(s_load, 16 * 15)
                act.activation(tanh_g[:], g_in[:], ACT.Tanh).then_inc(s_tanh, 1)
                act.wait_ge(s_wscaled, 3)
                def projections(b):
                    for n in range(KT + 1):
                        act.wait_ge(s_tr, b * 3 + n + 1)
                        if n == 0:
                            wait(act, s_pj, b * NPJ)
                        act.activation(xt_hi[:, n, :], bank[:, n, :], ACT.Copy).then_inc(s_trhi, 1)
                    for n in range(NPT):
                        act.wait_ge(s_pj, b * NPJ + n + 1)
                        if n == 0:
                            wait(act, s_projout, b * (16 * NPT))
                        act.activation(pj_out[:, n, 0, :], bank[:, 3 + n % 4, :], ACT.Identity,
                                       bias=bias_col[:, n // KT, n % KT:n % KT + 1]).then_inc(s_pjhi, 1)

                projections(0)
                with act.Fori(1, B) as b:
                    projections(b)

                act.wait_ge(s_pjlo, B * NPJ)
                act.wait_ge(s_projout, 16 * NPT * B)
                act.wait_ge(s_vout, 16 * TT * B)
                def out_of_bank(b, g, half, last=False):
                    act.wait_ge(s_pv, b * 32 + g * 8 + 4 * half + 4)
                    if not (isinstance(b, int) and b == 0 and g == 0):
                        act.wait_ge(s_full, turned(b, g - 1, half, last))
                    act.activation(o_sb[:, half, :], bank[:, SUM_BANK, :], ACT.Copy).then_inc(s_oout, 1)

                def batch(b, first, last):
                    for g in range(G):
                        for u in range(8):
                            n = T - P * u if u < 4 else T
                            wait(act, s_pv, b * 32 + (g * 8 + u - 3))
                            for pair in range(2):
                                act.wait_ge(s_scores, b * 64 + (g * 16 + 2 * u + pair + 1))
                                act.activation(probs[:, u % 4, 2 * pair:2 * pair + 2, 0:n],
                                               bank[:, 2 * pair:2 * pair + 2, 0:n], ACT.Exp).then_inc(s_exp, 1)
                            if u == 0 and not (first and g == 0):
                                out_of_bank(b, g - 1, 1, last)
                            if u == 4:
                                out_of_bank(b, g, 0, last)

                batch(0, True, False)
                with act.Fori(1, B - 1) as b:
                    batch(b, False, False)
                batch(B - 1, False, True)
                out_of_bank(B - 1, G - 1, 1, True)

            @block.vector
            def _(dve):
                def layer_norm(b):
                    dve.wait_ge(s_x, (b + 1) * 16)
                    for t in range(TT):
                        last = dve.bn_stats(stats[:, t, :], x_in[:, t, :])
                    last.then_inc(s_stats, 1)
                    dve.wait_ge(s_stats, b + 1)
                    dve.memset(tick[:], 0.0)
                    for t in range(TT):
                        last = dve.bn_aggr(mean_var[:, t, :], stats[:, t, :])
                    last.then_inc(s_aggr, 1)
                    dve.wait_ge(s_aggr, b + 1)
                    dve.tensor_scalar(var_eps[:], mean_var[:, :, 1], EPS, None, ALU.add).then_inc(s_var, 1)
                    dve.wait_ge(s_rstd, b + 1)
                    wait(dve, s_tr, b * 3)
                    for t in range(TT):
                        last = dve.tensor_scalar(xn[:, t, :], x_in[:, t, :], mean_var[:, t, 0:1], rstd[:, t:t + 1],
                                                 ALU.subtract, ALU.mult)
                    last.then_inc(s_xn, 1)

                def transposed_low(b):
                    for n in range(KT + 1):
                        dve.wait_ge(s_trhi, b * 3 + n + 1)
                        dve.tensor_tensor(xt_lo[:, n, :], bank[:, n, :], xt_hi[:, n, :], ALU.subtract).then_inc(s_trlo, 1)

                def projected(b, n):
                    if n < NPT:
                        dve.wait_ge(s_pjhi, b * NPT + n + 1)
                        dve.scalar_tensor_tensor(out=pj_out[:, n, 1, :], in0=bank[:, 3 + n % 4, :],
                                                 scalar=bias_col[:, n // KT, n % KT:n % KT + 1],
                                                 in1=pj_out[:, n, 0, :], op0=ALU.add,
                                                 op1=ALU.subtract).then_inc(s_pjlo, 1)
                    else:
                        dve.wait_ge(s_pj, b * NPJ + n + 1)
                        if n == NPT:
                            wait(dve, s_vout, b * (16 * TT))
                        dve.tensor_tensor(v_out[:, n - NPT, :, :, 0:D],
                                          bank[:, 3 + n % 4, :].rearrange("p (a h d) -> p a h d", a=2, h=H),
                                          bias_row[:].rearrange("p a (h d) -> p a h d", h=H),
                                          ALU.add).then_inc(s_pjlo, 1)

                dve.wait_ge(s_consts, 5)
                layer_norm(0)
                dve.wait_ge(s_load, 16 * 15)
                dve.tensor_scalar(wf[:, CQ:CQ + KT, :], wf[:, CQ:CQ + KT, :], SCALE, None, ALU.mult).then_inc(s_wscaled, 1)
                dve.tensor_scalar(wf[:, CCQ:CCQ + KT, :], wf[:, CCQ:CCQ + KT, :], SCALE, None,
                                  ALU.mult).then_inc(s_wscaled, 1)
                dve.tensor_scalar(bias_col[:, 0:3:2, :], bias_col[:, 0:3:2, :], SCALE, None, ALU.mult).then_inc(s_wscaled, 1)
                dve.wait_ge(s_wscaled, 3)
                dve.tensor_copy(w_hi[:], wf[:]).then_inc(s_whi, 1)
                dve.wait_ge(s_whi, 1)
                dve.tensor_tensor(w_lo[:], wf[:], w_hi[:], ALU.subtract).then_inc(s_wlo, 1)
                def projections(b):
                    transposed_low(b)
                    for n in range(NPJ):
                        projected(b, n)
                        if n == 3:
                            layer_norm(b + 1)

                projections(0)
                with dve.Fori(1, B - 1) as b:
                    projections(b)
                transposed_low(B - 1)
                for n in range(NPJ):
                    projected(B - 1, n)

                dve.wait_ge(s_tbp, 16)
                dve.tensor_scalar(tbp[:], tbp[:], tanh_g[:, 0:1], None, ALU.mult).then_inc(s_tbp, 1)
                dve.wait_ge(s_tbp, 17)

                def consume(b, n, tile, step, link, par=0):
                    kind, a, q = tile
                    ring, at = ring_index(b, n) if n is not None else step
                    dve.wait_ge(s_full, ring + 1)
                    bk_ = bank[:, at, :]
                    if kind == "cross":
                        ins = dve.tensor_reduce(negmax[:, par, q, 4 + a:5 + a], bk_, X, ALU.max, negate=True)
                    elif kind == "self3":
                        ins = dve.tensor_reduce(negmax[:, par, 3, a:a + 1], bk_, X, ALU.max, negate=True)
                    elif kind == "self02":
                        dve.tensor_reduce(negmax[:, par, 0, a:a + 1], bk_[:, 0:P], X, ALU.max, negate=True)
                        ins = dve.tensor_reduce(negmax[:, par, 2, a:a + 1], bk_[:, P:T], X, ALU.max, negate=True)
                    elif kind == "self1":
                        ins = dve.tensor_reduce(negmax[:, par, 1, a:a + 2], bk_.rearrange("p (j n) -> p j n", j=2), X,
                                                ALU.max, negate=True)
                    elif kind == "turn_max":
                        wait(dve, s_maxrow, step_no(b, a) * 32)
                        ins = dve.tensor_copy(maxrow[:], bank[0:8, at, :])
                    elif kind in ("turn_self", "turn_cross"):
                        g = a % G
                        o = bk_.rearrange("p (t j e) -> p t j e", t=TT, j=4)
                        half = int(kind == "turn_cross")
                        dve.reciprocal(rec[:, half], o[:, :, :, D]).then_inc(s_link, 1)
                        link = link + 1
                        dve.wait_ge(s_link, link)
                        r = rec[:, half].unsqueeze(3).broadcast_to([P, TT, 4, D])
                        yg = y[:, :, g * 64:(g + 1) * 64].rearrange("p t (j d) -> p t j d", j=4)
                        if kind == "turn_self":
                            ins = dve.tensor_tensor(yg, o[:, :, :, 0:D], r, ALU.mult)
                        else:
                            dve.tensor_tensor(part[:], o[:, :, :, 0:D], r, ALU.mult).then_inc(s_link, 1)
                            link = link + 1
                            dve.wait_ge(s_link, link)
                            ins = dve.tensor_tensor(yg, yg, part[:], ALU.add)
                    elif kind == "turn_y":
                        dve.tensor_copy(yt_hi[:, a, :], bk_).then_inc(s_link, 1)
                        link = link + 1
                        dve.wait_ge(s_link, link)
                        ins = dve.tensor_tensor(yt_lo[:, a, :], bk_, yt_hi[:, a, :], ALU.subtract)
                    elif kind == "project":
                        if a == 0:
                            dve.wait_ge(s_xa, b_of(b) * 16)
                            wait(dve, s_x1out, b_of(b) * 16 - 16)
                        xs = xa[:, 2 * a:2 * a + 2, :]
                        dve.tensor_tensor(xs, xs, tbp[:].unsqueeze(1).broadcast_to([P, 2, C]), ALU.add).then_inc(s_link, 1)
                        link = link + 1
                        dve.wait_ge(s_link, link)
                        ins = dve.scalar_tensor_tensor(out=x1[:, 2 * a:2 * a + 2, :],
                                                       in0=bk_.rearrange("p (t c) -> p t c", t=2),
                                                       scalar=tanh_g[:, 0:1], in1=xs, op0=ALU.mult, op1=ALU.add)
                    ins.then_inc(s_free, 1)
                    return link

                def b_of(b):
                    return b

                def step_no(b, g):
                    return b * 4 + g

                def batch(b, first, last, link):
                    n = 0
                    for g in range(G):
                        for tiles in step_tiles(g, first, last):
                            for tile in tiles:
                                link = consume(b, n, tile, None, link, g % 2)
                                n += 1
                    return link, n

                for n, tile in enumerate(MAX_TILES + MAX_TILES + [("turn_max", 0, NM)]):
                    consume(0, None, tile, (n, RING_BANK + n % RING), 0, n // NM)
                LINKS = [G + 2 * (G - 1), G * 3 + 4]
                batch(0, True, False, 0)
                with dve.Fori(1, B - 1) as b:
                    batch(b, False, False, b * LINKS[1] + (LINKS[0] - LINKS[1]))
                at = (B - 1) * LINKS[1] + LINKS[0] - LINKS[1]
                at, n = batch(B - 1, False, True, at)
                for k, tile in enumerate((("turn_cross", G - 1, 0), ("turn_y", 0, 0), ("turn_y", 1, 0),
                                          ("project", 0, 0), ("project", 1, 0))):
                    if tile[0] == "project" and tile[1] == 0:
                        dve.wait_ge(s_xa, 16 * B)
                        dve.wait_ge(s_x1out, 16 * (B - 1))
                    at = consume(B - 1, n + k, tile, None, at)

            @block.tensor
            def _(pe):
                pe.wait_ge(s_consts, 8)
                pe.wait_ge(s_wlo, 1)
                def projections(b):
                    pe.wait_ge(s_xn, b + 1)
                    wait(pe, s_trlo, b * 3)
                    for k in range(KT):
                        for t in range(TT):
                            last = pe.transpose(bank[:, k, t * P:(t + 1) * P], xn[:, t, k * P:(k + 1) * P], ident[:])
                        last.then_inc(s_tr, 1)
                    pe.wait_ge(s_ctx, (b + 1) * 16)
                    for t in range(TT):
                        last = pe.transpose(bank[:, KT, t * P:(t + 1) * P], ctx_in[:, t, :], ident[:])
                    last.then_inc(s_tr, 1)
                    pe.wait_ge(s_trlo, b * 3 + 3)
                    for n in range(NPJ):
                        wait(pe, s_pjlo, b * NPJ + (n - 3))
                        if n < NPT:
                            at, nk = PROJ[n // KT]
                            m = slice((n % KT) * P, (n % KT + 1) * P)
                            for k in range(nk):
                                xk = k if nk > 1 else KT
                                for w, a in ((w_hi, xt_hi), (w_hi, xt_lo), (w_lo, xt_hi)):
                                    last = pe.matmul(bank[:, 3 + n % 4, :], w[:, at + k, m], a[:, xk, :],
                                                     start=(k == 0 and w is w_hi and a is xt_hi),
                                                     stop=(k == nk - 1 and w is w_lo))
                        else:
                            t = slice((n - NPT) * P, (n - NPT + 1) * P)
                            for half, at, xk, nk in ((0, CV, 0, KT), (1, CCV, KT, 1)):
                                for k in range(nk):
                                    for w, a in ((w_hi, xt_hi), (w_lo, xt_hi), (w_hi, xt_lo)):
                                        last = pe.matmul(bank[:, 3 + n % 4, half * C:(half + 1) * C], a[:, xk + k, t],
                                                         w[:, at + k, :],
                                                         start=(k == 0 and w is w_hi and a is xt_hi),
                                                         stop=(k == nk - 1 and a is xt_lo))
                        last.then_inc(s_pj, 1)

                projections(0)
                with pe.Fori(1, B) as b:
                    projections(b)

                pe.wait_ge(s_pjlo, B * NPJ)
                def scores_for_max(slot, tile, bk_):
                    kind, a, q = tile

                    def own(j, q, to, width):
                        pe.matmul(bk_[:, to:to + width], q_st[0:96, slot, 0, j, q * P:(q + 1) * P],
                                  k_st[0:96, slot, 0, j, 0:width], start=True, stop=False)
                        return pe.matmul(bk_[:, to + width - P:to + width], ident_bf[:], future[:], start=False, stop=True)

                    if kind == "cross":
                        return pe.matmul(bk_, q_st[0:96, slot, 1, a, q * P:(q + 1) * P], k_st[0:96, slot, 1, a, :],
                                         start=True, stop=True)
                    if kind == "self3":
                        return own(a, 3, 0, T)
                    if kind == "self02":
                        own(a, 0, 0, P)
                        return own(a, 2, P, 3 * P)
                    own(a, 1, 0, 2 * P)
                    return own(a + 1, 1, 2 * P, 2 * P)

                def tile_of(b, ring, at, tile):
                    kind, a, q = tile
                    bk_ = bank[:, at, :]
                    wait(pe, s_free, ring - (RING - 1))
                    if kind in ("cross", "self3", "self02", "self1"):
                        last = scores_for_max(q_slot[0], tile, bk_)
                    elif kind == "turn_max":
                        pe.wait_ge(s_free, ring - q)
                        for t in range(TT):
                            last = pe.transpose(bank[0:8, at, t * P:(t + 1) * P], negmax[:, a % 2, t, :], ident[:])
                    elif kind in ("turn_self", "turn_cross"):
                        half = int(kind == "turn_cross")
                        pe.wait_ge(s_oout, b * 8 + 2 * a + half + 1)
                        for t in range(TT):
                            last = pe.transpose(bk_[:, t * P:(t + 1) * P], o_sb[:, half, t * P:(t + 1) * P], ident[:])
                    elif kind == "turn_y":
                        pe.wait_ge(s_free, ring - a)
                        for t in range(TT):
                            last = pe.transpose(bk_[:, t * P:(t + 1) * P], y[:, t, a * P:(a + 1) * P], ident[:])
                    elif kind == "project":
                        pe.wait_ge(s_free, ring - a)
                        for t in range(2):
                            ts = slice((2 * a + t) * P, (2 * a + t + 1) * P)
                            for k in range(KT):
                                for w, act_ in ((w_hi, yt_hi), (w_lo, yt_hi), (w_hi, yt_lo)):
                                    last = pe.matmul(bk_[:, t * C:(t + 1) * C], act_[:, k, ts], w[:, CP + k, :],
                                                     start=(k == 0 and w is w_hi and act_ is yt_hi),
                                                     stop=(k == KT - 1 and act_ is yt_lo))
                    last.then_inc(s_full, 1)

                q_slot = [0]

                def values(b, g, u):
                    half, kt = u // 4, u % 4
                    q0 = kt * P if half == 0 else 0
                    slot = g % G
                    pe.wait_ge(s_exp, b * 64 + (g * 16 + 2 * u + 2))
                    if half == 0:
                        pe.wait_ge(s_causal, b * 16 + (g * 4 + kt + 1))
                    if kt == 0:
                        wait(pe, s_oout, b * 8 + (2 * g + half))
                    for j in range(4):
                        last = pe.matmul(bank[32 * j:32 * j + 32, SUM_BANK, q0:T],
                                         v_st[:, slot, half, kt, 32 * j:32 * j + 32],
                                         probs[:, kt, j, 0:T - q0], start=(kt == 0), stop=(kt == 3))
                    last.then_inc(s_pv, 1)

                def batch(b, first, last_batch):
                    n = 0
                    for g in range(G):
                        pe.wait_ge(s_maxrow, b * 128 + 32 * (g + 1))
                        units = step_tiles(g, first, last_batch)
                        for u in range(8):
                            half, kt = u // 4, u % 4
                            q0 = kt * P if half == 0 else 0
                            for pair in range(2):
                                wait(pe, s_exp, b * 64 + (g * 16 + 2 * u + pair - 1))
                                for j in (2 * pair, 2 * pair + 1):
                                    last = pe.matmul(bank[:, j, 0:T - q0], k_st[:, g, half, j, kt * P:(kt + 1) * P],
                                                     q_st[:, g, half, j, q0:T], start=True, stop=True)
                                last.then_inc(s_scores, 1)
                            if u == 0 and not (last_batch and g >= G - 2):
                                nb = b + 1 if g < G - 2 else b + 2
                                pe.wait_ge(s_stack[(g + 2) % G], nb * (16 * LOADS))
                            if u > 0 or not (first and g == 0):
                                values(b, g - 1 if u == 0 else g, (u - 1) % 8)
                            q_slot[0] = (g + 2) % G
                            for tile in units[u]:
                                ring, at = ring_index(b, n)
                                tile_of(b, ring, at, tile)
                                n += 1
                    return n

                pe.wait_ge(s_zeroed, 2)
                for n, tile in enumerate(MAX_TILES + MAX_TILES + [("turn_max", 0, NM)]):
                    if n == 0 or n == NM:
                        q_slot[0] = n // NM
                        pe.wait_ge(s_stack[n // NM], 16 * LOADS)
                    tile_of(0, n, RING_BANK + n % RING, tile)
                batch(0, True, False)
                with pe.Fori(1, B - 1) as b:
                    batch(b, False, False)
                n = batch(B - 1, False, True)
                values(B - 1, G - 1, 7)
                for k, tile in enumerate((("turn_cross", G - 1, 0), ("turn_y", 0, 0), ("turn_y", 1, 0),
                                          ("project", 0, 0), ("project", 1, 0))):
                    ring, at = ring_index(B - 1, n + k)
                    tile_of(B - 1, ring, at, tile)

        N = B * TT
        NSLOT = 2 * N + NE - 1
        W_COLS = KT * F
        assert W_COLS == FT * C and NSLOT % 2 == 1
        RG = 8
        x2_dram = nc.dram_tensor("x2_dram", [N * P, 2 * C], F16).ap()
        ys_dram = nc.dram_tensor("ys_dram", [NSLOT * P, C], F32).ap()

        s_mask = sem("s_mask")
        s_count = sem("s_count")
        s_countc = sem("s_countc")
        s_wr = sem("s_wr")
        s_wrc = sem("s_wrc")
        s_stats2 = sem("s_stats2")
        s_aggr2 = sem("s_aggr2")
        s_var2 = sem("s_var2")
        s_rstd2 = sem("s_rstd2")
        s_xn2 = sem("s_xn2")
        s_rowhi = sem("s_rowhi")
        s_rowlo = sem("s_rowlo")
        s_rowout = sem("s_rowout")
        s_tr2 = sem("s_tr2")
        s_tr2hi = sem("s_tr2hi")
        s_tr2lo = sem("s_tr2lo")
        s_logit = sem("s_logit")
        s_route = sem("s_route")
        s_chosen = sem("s_chosen")
        s_rank = sem("s_rank")
        s_gap = sem("s_gap")
        s_gexp = sem("s_gexp")
        s_place = sem("s_place")
        s_token = sem("s_token")
        s_expert = sem("s_expert")
        s_inverse = sem("s_inverse")
        s_pos = sem("s_pos")
        s_we = [sem(f"s_we{n}") for n in range(4)]
        s_ehi = sem("s_ehi")
        s_elo = sem("s_elo")
        s_xs = [sem(f"s_xs{n}") for n in range(2)]
        s_st = sem("s_st")
        s_xt = sem("s_xt")
        s_up = sem("s_up")
        s_wup = sem("s_wup")
        s_wdown = sem("s_wdown")
        s_gelu = sem("s_gelu")
        s_hhi = sem("s_hhi")
        s_hlo = sem("s_hlo")
        s_down = sem("s_down")
        s_yev = sem("s_yev")
        s_yout = [sem(f"s_yout{n}") for n in range(2)]
        s_back = [sem(f"s_back{n}") for n in range(RG)]
        s_acc = sem("s_acc")
        s_out = sem("s_out")

        with ExitStack() as phase:
            def sb(name, shape, dt):
                return phase.enter_context(nc.sbuf_tensor(name, shape, dt))

            before = sb("before", [P, P], BF16)
            ones = sb("ones", [P, P], BF16)
            count = sb("count", [P, P + 1], F32)
            half16 = sb("half16", [P, N], F32)
            stats = sb("stats2", [P, N, 6], F32)
            mean_var = sb("mean_var2", [P, N, 2], F32)
            var_eps = sb("var_eps2", [P, N], F32)
            rstd = sb("rstd2", [P, N], F32)
            xn = sb("xn2", [P, N, C], F32)
            rows = sb("rows", [P, N, 2, C], F16)
            xt_st = sb("xt_st", [P, 2, 2, KT, T], F16)
            wr = sb("wr", [P, KT, NE], F32)
            wr_hi = sb("wr_hi", [P, KT, NE], F16)
            wr_lo = sb("wr_lo", [P, KT, NE], F16)
            lg = sb("lg", [P, N, NE], F32)
            top = sb("top", [P, N, 8], F32)
            top_i = sb("top_i", [P, N, 8], U32)
            top_f = sb("top_f", [P, N, 8], F32)
            gap = sb("gap", [P, N], F32)
            gap_e = sb("gap_e", [P, N], F32)
            g_sum = sb("g_sum", [P, N], F32)
            gates = sb("gates", [P, 2, N], F32)
            chosen = sb("chosen", [P, 2, N, NE], F32)
            chosen_bf = sb("chosen_bf", [P, N + 1, NE], BF16)
            rank = sb("rank", [P, N + 1, NE], F32)
            steps = sb("steps", [P, 16], F32)
            fills = sb("fills", [P, NE, 16], F32)
            slots = sb("slots", [P, NE], F32)
            earlier = sb("earlier", [P, NE, NE], F32)
            base_of = sb("base_of", [P, NE, NE], F32)
            base = sb("base", [P, NE], F32)
            at_or_after = sb("at_or_after", [P, NSLOT, NE], F32)
            expert_f = sb("expert_f", [P, NSLOT], F32)
            expert = sb("expert", [P, NSLOT], U32)
            picked = sb("picked", [P, 2, N, NE], F32)
            picked2 = sb("picked2", [P, 2, N, NE], F32)
            my_rank = sb("my_rank", [P, 2, N], F32)
            my_base = sb("my_base", [P, 2, N], F32)
            past = sb("past", [P, 2 * N, 16], F32)
            my_tile = sb("my_tile", [P, 2, N], F32)
            my_row = sb("my_row", [P, 2, N], F32)
            my_slot = sb("my_slot", [P, 2, N], F32)
            my_pos = sb("my_pos", [P, 2, N], U32)
            token = sb("token", [P, N], F32)
            row_hot = sb("row_hot", [P, 2, N, P], F16)
            slot_hot = sb("slot_hot", [P, 2, N, NSLOT], F16)
            source = sb("source", [P, NSLOT], U32)
            w_in = sb("w_in", [P, 4, W_COLS], F32)
            we = arena[:].bitcast(F16).rearrange("p (e a l n) -> p e a l n", e=NE, a=2, l=2)
            w_up = sb("w_up", [P, 2, 2, W_COLS], F16)
            w_down = sb("w_down", [P, 2, 2, W_COLS], F16)
            xs = sb("xs", [P, 2, 2 * C], F16)
            xt = sb("xt", [P, 2, 4, P], F16)
            h32 = sb("h32", [P, 2, FT, P], F32)
            h_hi = sb("h_hi", [P, 2, FT, P], F16)
            h_lo = sb("h_lo", [P, 2, FT, P], F16)
            y_sb = sb("y_sb", [P, 2, C], F32)
            back = w_in[:, 0:2].rearrange("p a (g c) -> p (a g) c", c=C)
            ident_h = sb("ident_h", [P, P], F16)
            block = phase.enter_context(nc.Block())
            PAIRS = (NSLOT - 3) // 2

            def expert_rows(c):
                return (w1, w2)[c % 2][c // 2].rearrange("(k p) n -> p k n", p=P)

            @block.sync
            def _(sp):
                for k in range(KT):
                    sp.dma_start(wr[:, k, :], router_w[:, k * P:(k + 1) * P].rearrange("e p -> p e"),
                                 allow_slow_non_contiguous=True).then_inc(s_wr, 16)
                for c in range(2 * NE):
                    wait(sp, s_elo, c - 3)
                    sp.dma_start(w_in[:, c % 4].rearrange("p (k n) -> p k n", k=(KT, FT)[c % 2]),
                                 expert_rows(c)).then_inc(s_we[c % 4], 16)
                for b in range(B):
                    sp.wait_ge(s_rowlo, b + 1)
                    sp.dma_start(x2_dram[b * T:(b + 1) * T].rearrange("(t p) n -> p t n", p=P),
                                 rows[:, b * TT:(b + 1) * TT].rearrange("p t l c -> p t (l c)")).then_inc(s_rowout, 16)

                def store(s, par):
                    sp.wait_ge(s_yev, s + 1)
                    sp.dma_start(ys_dram[bass.ds(s * P, P), :], y_sb[:, par]).then_inc(s_yout[par], 16)

                with sp.Fori(0, NSLOT // 2) as half_s:
                    for par in range(2):
                        store(half_s * 2 + par, par)
                store(NSLOT - 1, 0)
                for b in range(B):
                    sp.wait_ge(s_acc, (b + 1) * 2 * TT)
                    sp.dma_start(out_rows[b].rearrange("t p c -> p t c"), x1_all[:, b]).then_inc(s_out, 16)
                sp.wait_ge(s_out, 16 * B)

            @block.gpsimd
            def _(pool):
                pool.memset(before[:], 1.0).then_inc(s_mask, 1)
                pool.memset(ones[:], 1.0).then_inc(s_mask, 1)
                pool.memset(half16[:], -0.5).then_inc(s_mask, 1)
                pool.memset(ident_h[:], 0.0).then_inc(s_mask, 1)
                pool.memset(chosen_bf[:, N], 0.0).then_inc(s_mask, 1)
                pool.wait_ge(s_mask, 5)
                pool.affine_select(out=before[:], in_=before[:], compare_op=ALU.is_gt, fill=0.0,
                                   pattern=[[1, P]], base=0, channel_multiplier=-1).then_inc(s_mask, 1)
                pool.affine_select(out=ident_h[:], in_=ident_h[:], compare_op=ALU.not_equal, fill=1.0,
                                   pattern=[[-1, P]], base=0, channel_multiplier=1).then_inc(s_mask, 1)

                def low(c):
                    pool.wait_ge(s_ehi, c + 1)
                    pool.tensor_tensor(we[:, c // 2, c % 2, 1, :], w_in[:, c % 4], we[:, c // 2, c % 2, 0, :],
                                       ALU.subtract).then_inc(s_elo, 1)

                def low_rows(b):
                    pool.wait_ge(s_rowhi, b + 1)
                    t = slice(b * TT, (b + 1) * TT)
                    pool.tensor_tensor(rows[:, t, 1], xn[:, t], rows[:, t, 0], ALU.subtract).then_inc(s_rowlo, 1)

                low(0)
                pool.wait_ge(s_var2, 1)
                pool.tensor_tensor(rstd[:], var_eps[:], half16[:], ALU.pow).then_inc(s_rstd2, 1)
                for b in range(B):
                    for c in range(4 * b, 4 * b + 4):
                        if c > 0:
                            low(c)
                    low_rows(b)
                pool.wait_ge(s_rowout, 16 * B)
                pool.wait_ge(s_inverse, 1)

                for s in range(NSLOT):
                    wait(pool, s_st, s - 1)
                    pool.indirect_dma_start(xs[:, s % 2, :], None, x2_dram[:, :],
                                            bass.IndirectOffsetOnAxis(ap=source[:, s:s + 1], axis=0)
                                            ).then_inc(s_xs[s % 2], 16)
                pool.wait_ge(s_pos, 1)
                for par in range(2):
                    pool.wait_ge(s_yout[par], 16 * ((NSLOT + 1 - par) // 2))
                for i in range(2 * N):
                    wait(pool, s_acc, i - RG + 1)
                    pool.indirect_dma_start(back[:, i % RG, :], None, ys_dram[:, :],
                                            bass.IndirectOffsetOnAxis(ap=my_pos[:, i % 2, i // 2:i // 2 + 1], axis=0)
                                            ).then_inc(s_back[i % RG], 16)

            @block.scalar
            def _(act):
                def high(c):
                    act.wait_ge(s_we[c % 4], 16 * (c // 4 + 1))
                    act.activation(we[:, c // 2, c % 2, 0, :], w_in[:, c % 4], ACT.Copy).then_inc(s_ehi, 1)

                for c in range(4):
                    high(c)
                for b in range(B):
                    t = slice(b * TT, (b + 1) * TT)
                    act.wait_ge(s_xn2, b + 1)
                    act.activation(rows[:, t, 0], xn[:, t], ACT.Copy).then_inc(s_rowhi, 1)
                    for k in range(KT):
                        act.wait_ge(s_tr2, b * KT + k + 1)
                        if k == 0:
                            wait(act, s_logit, b - 1)
                        act.activation(xt_st[:, b % 2, 0, k, :], bank[:, 4 * (b % 2) + k, :], ACT.Copy).then_inc(s_tr2hi, 1)
                    if b < B - 1:
                        for c in range(4 * b + 4, 4 * b + 8):
                            high(c)
                act.wait_ge(s_gap, 1)
                act.activation(gap_e[:], gap[:], ACT.Exp).then_inc(s_gexp, 1)

                def turned_rows(s, par):
                    act.wait_ge(s_st, s + 1)
                    wait(act, s_up, s - 1)
                    act.activation(xt[:, par].rearrange("p a n -> p (a n)"), bank[:, par].bitcast(F16)[:, 0:4 * P],
                                   ACT.Copy).then_inc(s_xt, 1)

                def gelu(s, par):
                    act.wait_ge(s_up, s + 1)
                    wait(act, s_hlo, s - 1)
                    act.activation(h32[:, par].rearrange("p m n -> p (m n)"), bank[:, 2 + par, :], ACT.Gelu).then_inc(s_gelu, 1)

                def output(s, par):
                    act.wait_ge(s_down, s + 1)
                    wait(act, s_yout[par], (s - par) * 8)
                    act.activation(y_sb[:, par], bank[:, 4 + par, 0:C], ACT.Copy).then_inc(s_yev, 1)

                turned_rows(0, 0)
                turned_rows(1, 1)
                gelu(0, 0)

                def pair(s):
                    for par in range(2):
                        turned_rows(s + (par + 2), par)
                        gelu(s + (par + 1), 1 - par)
                        output(s + par, par)

                pair(0)
                with act.Fori(1, PAIRS) as half_s:
                    pair(half_s * 2)
                s = 2 * PAIRS
                turned_rows(s + 2, 0)
                gelu(s + 1, 1)
                output(s, 0)
                gelu(s + 2, 0)
                output(s + 1, 1)
                output(s + 2, 0)

            @block.vector
            def _(dve):
                dve.wait_ge(s_wr, 16 * KT)
                dve.tensor_copy(wr_hi[:], wr[:]).then_inc(s_wrc, 1)
                dve.wait_ge(s_wrc, 1)
                dve.tensor_tensor(wr_lo[:], wr[:], wr_hi[:], ALU.subtract).then_inc(s_wrc, 1)
                tokens = x1_all[:].rearrange("p b t c -> p (b t) c")
                for i in range(N):
                    last = dve.bn_stats(stats[:, i, :], tokens[:, i, :])
                last.then_inc(s_stats2, 1)
                dve.wait_ge(s_stats2, 1)
                dve.memset(tick[:], 0.0)
                for i in range(N):
                    last = dve.bn_aggr(mean_var[:, i, :], stats[:, i, :])
                last.then_inc(s_aggr2, 1)
                dve.wait_ge(s_aggr2, 1)
                dve.tensor_scalar(var_eps[:], mean_var[:, :, 1], EPS, None, ALU.add).then_inc(s_var2, 1)
                dve.wait_ge(s_count, 1)
                dve.tensor_copy(count[:], bank[:, 3, 0:P + 1]).then_inc(s_countc, 1)
                dve.wait_ge(s_countc, 1)
                dve.tensor_scalar(steps[:], count[:, 0:16], float(P), None, ALU.mult).then_inc(s_countc, 1)
                dve.tensor_tensor(earlier[:], count[:, 0:NE].unsqueeze(2).broadcast_to([P, NE, NE]),
                                  count[:, 0:NE].unsqueeze(1).broadcast_to([P, NE, NE]), ALU.is_gt).then_inc(s_countc, 1)
                dve.wait_ge(s_countc, 2)
                dve.tensor_tensor(token[:], steps[:, 0:N], count[:, P:P + 1].broadcast_to([P, N]), ALU.add).then_inc(s_countc, 1)

                def normalise(b):
                    for i in range(b * TT, (b + 1) * TT):
                        last = dve.tensor_scalar(xn[:, i, :], tokens[:, i, :], mean_var[:, i, 0:1], rstd[:, i:i + 1],
                                                 ALU.subtract, ALU.mult)
                    last.then_inc(s_xn2, 1)

                def transposed_low(b):
                    for k in range(KT):
                        dve.wait_ge(s_tr2hi, b * KT + k + 1)
                        dve.tensor_tensor(xt_st[:, b % 2, 1, k, :], bank[:, 4 * (b % 2) + k, :], xt_st[:, b % 2, 0, k, :],
                                          ALU.subtract).then_inc(s_tr2lo, 1)

                dve.wait_ge(s_rstd2, 1)
                normalise(0)
                for b in range(B):
                    if b < B - 1:
                        normalise(b + 1)
                    transposed_low(b)
                dve.wait_ge(s_logit, B)
                dve.tensor_copy(lg[:].rearrange("p i e -> p (i e)"), bank[:, 2, 0:N * NE]).then_inc(s_route, 1)
                dve.wait_ge(s_route, 1)
                for i in range(N):
                    last = dve.max(top[:, i, :], lg[:, i, :])
                last.then_inc(s_route, 1)
                dve.wait_ge(s_route, 2)
                for i in range(N):
                    dve.max_index(top_i[:, i, :], top[:, i, :], lg[:, i, :])
                dve.tensor_tensor(gap[:], top[:, :, 1], top[:, :, 0], ALU.subtract).then_inc(s_gap, 1)
                dve.wait_ge(s_gap, 1)
                dve.tensor_copy(top_f[:], top_i[:]).then_inc(s_route, 1)
                dve.wait_ge(s_route, 3)
                for choice in range(2):
                    last = dve.tensor_tensor(chosen[:, choice], count[:, 0:NE].unsqueeze(1).broadcast_to([P, N, NE]),
                                             top_f[:, :, choice:choice + 1].broadcast_to([P, N, NE]), ALU.is_equal)
                last.then_inc(s_route, 1)
                dve.wait_ge(s_route, 4)
                dve.tensor_tensor(chosen_bf[:, 0:N], chosen[:, 0], chosen[:, 1], ALU.add).then_inc(s_chosen, 1)
                dve.wait_ge(s_gexp, 1)
                dve.tensor_scalar(g_sum[:], gap_e[:], 1.0, None, ALU.add).then_inc(s_route, 1)
                dve.wait_ge(s_route, 5)
                dve.reciprocal(gates[:, 0], g_sum[:]).then_inc(s_route, 1)
                dve.wait_ge(s_route, 6)
                dve.tensor_scalar(gates[:, 0], gates[:, 0], tanh_g[:, 1:2], None, ALU.mult).then_inc(s_route, 1)
                dve.wait_ge(s_route, 7)
                dve.tensor_tensor(gates[:, 1], gates[:, 0], gap_e[:], ALU.mult).then_inc(s_route, 1)
                dve.wait_ge(s_rank, 1)
                dve.tensor_copy(rank[:].rearrange("p i e -> p (i e)"), bank[:, 3, 0:(N + 1) * NE]).then_inc(s_place, 1)
                dve.wait_ge(s_place, 1)
                dve.tensor_tensor(fills[:], rank[:, N, :].unsqueeze(2).broadcast_to([P, NE, 16]),
                                  steps[:].unsqueeze(1).broadcast_to([P, NE, 16]), ALU.is_gt).then_inc(s_place, 1)
                dve.tensor_tensor(picked[:], chosen[:], rank[:, 0:N].unsqueeze(1).broadcast_to([P, 2, N, NE]),
                                  ALU.mult).then_inc(s_place, 1)
                dve.wait_ge(s_place, 3)
                dve.tensor_reduce(slots[:], fills[:], X, ALU.add).then_inc(s_place, 1)
                dve.tensor_reduce(my_rank[:], picked[:], X, ALU.add).then_inc(s_place, 1)
                dve.wait_ge(s_place, 5)
                dve.tensor_tensor(base_of[:], earlier[:], slots[:].unsqueeze(1).broadcast_to([P, NE, NE]),
                                  ALU.mult).then_inc(s_place, 1)
                dve.tensor_tensor(past[:], my_rank[:].rearrange("p a i -> p (a i)").unsqueeze(2).broadcast_to([P, 2 * N, 16]),
                                  steps[:].unsqueeze(1).broadcast_to([P, 2 * N, 16]), ALU.is_ge).then_inc(s_place, 1)
                dve.wait_ge(s_place, 7)
                dve.tensor_reduce(base[:], base_of[:], X, ALU.add).then_inc(s_place, 1)
                dve.tensor_reduce(my_tile[:].rearrange("p a i -> p (a i)"), past[:], X, ALU.add).then_inc(s_place, 1)
                dve.wait_ge(s_place, 9)
                dve.tensor_scalar(my_tile[:], my_tile[:], -1.0, None, ALU.add).then_inc(s_place, 1)
                dve.tensor_tensor(picked2[:], chosen[:], base[:].unsqueeze(1).unsqueeze(1).broadcast_to([P, 2, N, NE]),
                                  ALU.mult).then_inc(s_place, 1)
                dve.wait_ge(s_place, 11)
                dve.tensor_reduce(my_base[:], picked2[:], X, ALU.add).then_inc(s_place, 1)
                dve.scalar_tensor_tensor(out=my_row[:], in0=my_tile[:], scalar=-float(P), in1=my_rank[:],
                                         op0=ALU.mult, op1=ALU.add).then_inc(s_place, 1)
                dve.wait_ge(s_place, 13)
                dve.tensor_tensor(my_slot[:], my_base[:], my_tile[:], ALU.add).then_inc(s_place, 1)
                dve.wait_ge(s_place, 14)
                for i in range(N):
                    for choice in range(2):
                        dve.tensor_scalar(row_hot[:, choice, i, :], count[:, 0:P], my_row[:, choice, i:i + 1], None,
                                          ALU.is_equal)
                        dve.tensor_scalar(slot_hot[:, choice, i, :], count[:, 0:NSLOT], my_slot[:, choice, i:i + 1],
                                          token[:, i:i + 1], ALU.is_equal, ALU.mult).then_inc(s_token, 1)
                dve.tensor_tensor(at_or_after[:], count[:, 0:NSLOT].unsqueeze(2).broadcast_to([P, NSLOT, NE]),
                                  base[:].unsqueeze(1).broadcast_to([P, NSLOT, NE]), ALU.is_ge).then_inc(s_place, 1)
                dve.wait_ge(s_place, 15)
                dve.tensor_reduce(expert_f[:], at_or_after[:], X, ALU.add).then_inc(s_place, 1)
                dve.wait_ge(s_place, 16)
                dve.tensor_scalar(expert[:], expert_f[:], -1.0, None, ALU.add).then_inc(s_expert, 1)
                dve.wait_ge(s_rank, 2)
                dve.tensor_copy(source[:], bank[:, 3, 0:NSLOT]).then_inc(s_inverse, 1)
                dve.scalar_tensor_tensor(out=my_pos[:], in0=my_slot[:], scalar=float(P), in1=my_row[:],
                                         op0=ALU.mult, op1=ALU.add).then_inc(s_pos, 1)

                def split_hidden(s, par):
                    dve.wait_ge(s_gelu, s + 1)
                    wait(dve, s_down, s - 1)
                    dve.tensor_copy(h_hi[:, par], h32[:, par]).then_inc(s_hhi, 1)
                    dve.wait_ge(s_hhi, s + 1)
                    dve.tensor_tensor(h_lo[:, par], h32[:, par], h_hi[:, par], ALU.subtract).then_inc(s_hlo, 1)

                def expert_of(s):
                    return dve.value_load(expert[0:1, bass.ds(s, 1)], min_val=0, max_val=NE - 1)

                def weights(which, e, to, done):
                    dve.tensor_copy(to.rearrange("p l n -> p (l n)"),
                                    we[:, bass.ds(e, 1), which].rearrange("p e l n -> p (e l n)")).then_inc(done, 1)

                def ahead(s, par, e1, e2):
                    dve.wait_ge(s_up, s + 1)
                    wait(dve, s_down, s)
                    dve.memset(tick[:], 0.0)
                    if e2 is not None:
                        weights(0, e2, w_up[:, par], s_wup)
                    weights(1, e1, w_down[:, 1 - par], s_wdown)
                    split_hidden(s + 1, 1 - par)

                dve.wait_ge(s_expert, 1)
                dve.wait_ge(s_elo, 2 * NE)
                dve.memset(tick[:], 0.0)
                e = [expert_of(n) for n in range(2)]
                weights(0, e[0], w_up[:, 0], s_wup)
                weights(0, e[1], w_up[:, 1], s_wup)
                weights(1, e[0], w_down[:, 0], s_wdown)
                split_hidden(0, 0)

                def pair(s):
                    e = [expert_of(s + n) for n in range(1, 4)]
                    ahead(s, 0, e[0], e[1])
                    ahead(s + 1, 1, e[1], e[2])

                pair(0)
                with dve.Fori(1, PAIRS) as half_s:
                    pair(half_s * 2)
                s = 2 * PAIRS
                e = [expert_of(s + n) for n in range(1, 3)]
                ahead(s, 0, e[0], e[1])
                ahead(s + 1, 1, e[1], None)
                for i in range(2 * N):
                    dve.wait_ge(s_back[i % RG], 16 * (i // RG + 1))
                    if i % 2:
                        dve.wait_ge(s_acc, i)
                    dve.scalar_tensor_tensor(out=tokens[:, i // 2, :], in0=back[:, i % RG, :],
                                             scalar=gates[:, i % 2, i // 2:i // 2 + 1], in1=tokens[:, i // 2, :],
                                             op0=ALU.mult, op1=ALU.add).then_inc(s_acc, 1)

            @block.tensor
            def _(pe):
                pe.wait_ge(s_mask, 7)
                pe.matmul(bank[:, 3, 0:P], ones[:], before[:], start=True, stop=True)
                pe.matmul(bank[:, 3, P:P + 1], before[:], ones[:, 0:1], start=True, stop=True).then_inc(s_count, 1)
                pe.wait_ge(s_wrc, 2)
                for b in range(B):
                    pe.wait_ge(s_xn2, b + 1)
                    wait(pe, s_tr2lo, (b - 1) * KT)
                    for k in range(KT):
                        for t in range(TT):
                            last = pe.transpose(bank[:, 4 * (b % 2) + k, t * P:(t + 1) * P],
                                                xn[:, b * TT + t, k * P:(k + 1) * P], ident[:])
                        last.then_inc(s_tr2, 1)
                    pe.wait_ge(s_tr2lo, b * KT + KT)
                    for t in range(TT):
                        ts = slice(t * P, (t + 1) * P)
                        i = b * TT + t
                        for k in range(KT):
                            for a, w in ((0, wr_hi), (0, wr_lo), (1, wr_hi)):
                                last = pe.matmul(bank[:, 2, i * NE:(i + 1) * NE], xt_st[:, b % 2, a, k, ts], w[:, k, :],
                                                 start=(k == 0 and a == 0 and w is wr_hi), stop=(k == KT - 1 and a == 1))
                    last.then_inc(s_logit, 1)
                pe.wait_ge(s_chosen, 1)
                pe.matmul(bank[:, 3, 0:(N + 1) * NE], before[:], chosen_bf[:].rearrange("p i e -> p (i e)"),
                          start=True, stop=False)
                for i in range(N):
                    last = pe.matmul(bank[:, 3, (i + 1) * NE:(N + 1) * NE], ones[:],
                                     chosen_bf[:, i:i + 1, :].broadcast_to([P, N - i, NE]), start=False, stop=(i == N - 1))
                last.then_inc(s_rank, 1)
                for i in range(2 * N):
                    pe.wait_ge(s_token, i + 1)
                    last = pe.matmul(bank[:, 3, 0:NSLOT], row_hot[:, i % 2, i // 2, :], slot_hot[:, i % 2, i // 2, :],
                                     start=(i == 0), stop=(i == 2 * N - 1))
                last.then_inc(s_rank, 1)

                def turn(s, par):
                    pe.wait_ge(s_xs[par], (s - par) * 8 + 16)
                    wait(pe, s_xt, s - 1)
                    to = bank[:, par].bitcast(F16)
                    for a in range(4):
                        last = pe.transpose(to[:, a * P:(a + 1) * P], xs[:, par, a * P:(a + 1) * P], ident_h[:])
                    last.then_inc(s_st, 1)

                def up(s, par):
                    pe.wait_ge(s_xt, s + 1)
                    pe.wait_ge(s_wup, s + 1)
                    wait(pe, s_gelu, s - 1)
                    for m in range(FT):
                        for k in range(KT):
                            for w, a in ((0, 0), (0, 1), (1, 0)):
                                at = k * F + m * P
                                last = pe.matmul(bank[:, 2 + par, m * P:(m + 1) * P],
                                                 w_up[:, par, w, at:at + P], xt[:, par, 2 * a + k, :],
                                                 start=(k == 0 and w == 0 and a == 0), stop=(k == KT - 1 and w == 1))
                    last.then_inc(s_up, 1)

                def down(s, par):
                    pe.wait_ge(s_hlo, s + 1)
                    pe.wait_ge(s_wdown, s + 1)
                    wait(pe, s_yev, s - 1)
                    for m in range(FT):
                        for h, w in ((h_hi, 0), (h_hi, 1), (h_lo, 0)):
                            last = pe.matmul(bank[:, 4 + par, 0:C], h[:, par, m, :], w_down[:, par, w, m * C:(m + 1) * C],
                                             start=(m == 0 and h is h_hi and w == 0), stop=(m == FT - 1 and h is h_lo))
                    last.then_inc(s_down, 1)

                turn(0, 0)
                turn(1, 1)
                up(0, 0)

                def pair(s):
                    for par in range(2):
                        turn(s + (par + 2), par)
                        up(s + (par + 1), 1 - par)
                        down(s + par, par)

                pair(0)
                with pe.Fori(1, PAIRS) as half_s:
                    pair(half_s * 2)
                s = 2 * PAIRS
                turn(s + 2, 0)
                up(s + 1, 1)
                down(s, 0)
                up(s + 2, 0)
                down(s + 1, 1)
                down(s + 2, 0)


_INS = ['x', 'ctx_512', 'g_xattn', 'g_ffn', 'L0_xattn_Wk', 'L0_xattn_bk', 'L0_xattn_Wq', 'L0_xattn_bq',
        'L0_xattn_Wv', 'L0_xattn_bv', 'L0_xattn_Wck', 'L0_xattn_bck', 'L0_xattn_Wcq', 'L0_xattn_bcq',
        'L0_xattn_Wcv', 'L0_xattn_bcv', 'L0_xattn_Wp', 'L0_xattn_bp', 'L0_ffn_router_w', 'L0_ffn_w1', 'L0_ffn_w2']
_OUTS = [((4, 512, 256), 'float32')]


def kernel(**inputs):
    import numpy as _np
    import concourse.bacc as _bacc
    from concourse import mybir as _mybir
    from concourse.bass_utils import run_bass_kernel_spmd as _run

    nc = _bacc.Bacc("TRN2", target_bir_lowering=False, num_devices=1)
    arrays, args = {}, []
    for name in _INS:
        a = _np.ascontiguousarray(inputs[name])
        arrays[f"in_{name}_dram"] = a
        args.append(nc.dram_tensor(f"in_{name}_dram", a.shape, _mybir.dt.from_np(a.dtype), kind="ExternalInput").ap())
    for i, (shape, dtype) in enumerate(_OUTS):
        dt = _mybir.dt.from_np(_np.dtype(dtype))
        args.append(nc.dram_tensor(f"out_{i}_dram", shape, dt, kind="ExternalOutput").ap())
    flamingo_layer(nc, *args)
    r = _run(nc, [arrays], core_ids=[0])
    got = tuple(r.results[0][f"out_{i}_dram"] for i in range(len(_OUTS)))
    return got[0]
```

```python
from contextlib import ExitStack

import concourse.bass as bass
from concourse import mybir
import numpy as np

F32 = mybir.dt.float32
F16 = mybir.dt.float16
BF16 = mybir.dt.bfloat16
U32 = mybir.dt.uint32
ACT = mybir.ActivationFunctionType
ALU = mybir.AluOpType
X = mybir.AxisListType.X

P = 128
EPS = 1e-5
MASKED = -1e30


def flamingo_layer(nc, x, ctx_512, g_xattn, g_ffn, Wk, bk, Wq, bq, Wv, bv, Wck, bck, Wcq, bcq,
                   Wcv, bcv, Wp, bp, router_w, w1, w2, out):
    B, T, C = x.shape
    S, CC = ctx_512.shape[1:]
    H = 16
    D = C // H
    TT = T // P
    KT = C // P
    G = H // 4
    NE, _, F = w1.shape
    FT = F // P
    SCALE = 0.25
    assert D == 16 and SCALE == float(D) ** -0.5 and T == S == 512 and C == 256 and CC == P and F == 512
    CQ, CK, CCQ, CV, CP, CCK, CCV = 0, 2, 4, 6, 8, 10, 11
    NCH = 12
    PROJ = [(CQ, KT), (CK, KT), (CCQ, KT), (CCK, 1)]
    NPT = len(PROJ) * KT
    NPJ = NPT + TT

    proj_dram = nc.dram_tensor("proj_dram", [B, 2, G, 2, 64, 2, T], F16).ap()
    v_dram = nc.dram_tensor("v_dram", [B, P, 2 * TT, H * 32], F32).ap()

    x2_dram = nc.dram_tensor("x2_dram", [B * TT * P, 2 * C], F16).ap()

    x_rows = x.rearrange("b (t p) c -> b t p c", p=P)
    ctx_rows = ctx_512.rearrange("b (t p) c -> b t p c", p=P)
    out_rows = out.rearrange("b (t p) c -> b t p c", p=P)

    def expert_rows(c):
        return (w1, w2)[c % 2][c // 2].rearrange("(k p) n -> p k n", p=P)

    with ExitStack() as whole:
        def sem(name):
            return whole.enter_context(nc.semaphore(name))

        def wait(eng, s, value):
            if not (isinstance(value, int) and value <= 0):
                eng.wait_ge(s, value)

        bank = whole.enter_context(nc.psum_tensor("bank", [P, 8, 512], F32))
        ident = whole.enter_context(nc.sbuf_tensor("ident", [P, P], F32))
        ident_bf = whole.enter_context(nc.sbuf_tensor("ident_bf", [P, P], BF16))
        future = whole.enter_context(nc.sbuf_tensor("future", [P, P], BF16))
        w_hi = whole.enter_context(nc.sbuf_tensor("w_hi", [P, NCH, C], F16))
        w_lo = whole.enter_context(nc.sbuf_tensor("w_lo", [P, NCH, C], F16))
        tanh_g = whole.enter_context(nc.sbuf_tensor("tanh_g", [P, 2], F32))
        x1_all = whole.enter_context(nc.sbuf_tensor("x1_all", [P, B, TT, C], F32))
        arena = whole.enter_context(nc.sbuf_tensor("arena", [P, 16384], F32))
        W_COLS = KT * F
        assert W_COLS == FT * C
        we = arena[:].bitcast(F16).rearrange("p (e a l n) -> p e a l n", e=NE, a=2, l=2)
        lg = whole.enter_context(nc.sbuf_tensor("lg", [P, B, TT * NE], F32))
        wr = whole.enter_context(nc.sbuf_tensor("wr", [P, KT, NE], F32))
        wr_hi = whole.enter_context(nc.sbuf_tensor("wr_hi", [P, KT, NE], F16))
        wr_lo = whole.enter_context(nc.sbuf_tensor("wr_lo", [P, KT, NE], F16))
        tick = whole.enter_context(nc.sbuf_tensor("tick", [P, 1], F32))
        pool_tick = whole.enter_context(nc.sbuf_tensor("pool_tick", [P, 1], F32))
        half_neg = whole.enter_context(nc.sbuf_tensor("half_neg", [P, TT], F32))

        s_wfirst = sem("s_wfirst")
        s_load = sem("s_load")
        s_consts = sem("s_consts")
        s_wscaled = sem("s_wscaled")
        s_whi = sem("s_whi")
        s_wlo = sem("s_wlo")
        s_wlolate = sem("s_wlolate")
        s_tanh = sem("s_tanh")
        s_x = sem("s_x")
        s_ctx = sem("s_ctx")
        s_stats = sem("s_stats")
        s_aggr = sem("s_aggr")
        s_var = sem("s_var")
        s_rstd = sem("s_rstd")
        s_xn = sem("s_xn")
        s_tr = sem("s_tr")
        s_trhi = sem("s_trhi")
        s_trlo = sem("s_trlo")
        s_pj = sem("s_pj")
        s_pjhi = sem("s_pjhi")
        s_pjlo = sem("s_pjlo")
        s_projout = sem("s_projout")
        s_vout = sem("s_vout")

        NM = 26
        PER_STEP = NM + 3
        FINISH = 7
        RING, RING_BANK = 3, 4
        SUM_BANK = 7

        def max_tiles(g):
            return [("cross", j, q, g) for j in range(4) for q in range(TT)] + \
                   [("self3", j, 0, g) for j in range(4)] + [("self02", j, 0, g) for j in range(4)] + \
                   [("self1", 0, 0, g), ("self1", 2, 0, g)]

        assert len(max_tiles(0)) == NM
        FIRST = [[8, 4, 3, 3, 4, 4, 4, 4]] + 3 * [[4, 4, 3, 3, 4, 5, 5, 4]]
        SHARED = [[4, 4, 2, 1, 2, 2, 3, 3], [4, 4, 3, 2, 1, 4, 4, 4], [4, 4, 2, 2, 3, 5, 4, 4], [4, 4, 3, 2, 3, 5, 4, 4]]
        FINAL = SHARED[:2] + [[2, 2, 1, 0, 0, 0, 0, 0], 8 * [0]]

        def step_tiles(g, first, last):
            table = FIRST if first else FINAL if last else SHARED
            stream = [tile for ahead in range(1 if first else 2, 4 if last else 6) for tile in max_tiles(ahead % G)]
            turn_unit = ([6, 5, 3, 3] if first else [1, 3, 3, 3])[g]
            at = sum(sum(row) for row in table[:g])
            units = []
            for u in range(8):
                tiles = stream[at:at + table[g][u]]
                at += table[g][u]
                if u == turn_unit and not (last and g == G - 1):
                    tiles.insert(0 if u == 1 else 2, ("turn_max", g + 1, None))
                if u == 2 and not (g == 0 and first):
                    tiles.insert(0, ("turn_cross", g - 1, 0))
                if g == 0 and not first:
                    tiles[2:2] = {3: [("turn_y", 0, None), ("turn_y", 1, None)], 4: [("project", 0, None)]}.get(u, [])
                    if u == 5:
                        tiles.insert(1, ("project", 1, None))
                if g == 1 and not first:
                    tiles[2:2] = {4: [("turn_x2", 0, 0), ("turn_x2", 1, 0)], 6: [("route", 0, None)]}.get(u, [])
                if u == 6:
                    tiles.append(("turn_self", g, 0))
                units.append(tiles)
            order = [tile for tiles in units for tile in tiles]

            def between(tile, n):
                need = {"turn_y": ("turn_cross", -1, 0), "project": ("turn_y", 1, None), "route": ("turn_x2", 1, 0)}
                if tile[0] == "turn_max":
                    at = [k for k in range(n) if len(order[k]) == 4 and order[k][3] == (g + 1) % G]
                    return n - 1 - (at[-1] if at else -1)
                return n - 1 - order.index(need[tile[0]])

            n = 0
            for tiles in units:
                for k, tile in enumerate(tiles):
                    if tile[2] is None:
                        tiles[k] = (tile[0], tile[1], between(tile, n))
                    n += 1
            return units

        def place(g, first, last, kind, a):
            return [tile[:2] for tiles in step_tiles(g, first, last) for tile in tiles].index((kind, a))

        AHEAD = NM + 1
        FIRST_BATCH = AHEAD + NM + G * PER_STEP - 1
        PER_BATCH = G * PER_STEP + FINISH
        assert FIRST_BATCH % RING == 0 and PER_BATCH % RING == 0

        def ring_index(b, n):
            if isinstance(b, int) and b == 0:
                return AHEAD + n, RING_BANK + (AHEAD + n) % RING
            return b * PER_BATCH + (FIRST_BATCH - PER_BATCH + n), RING_BANK + n % RING

        def turned(b, g, half, last):
            tile = ("turn_cross", g, 0) if half else ("turn_self", g, 0)
            n = 0
            for k in range(G):
                for tiles in step_tiles(k, isinstance(b, int) and b == 0, last):
                    for one in tiles:
                        n += 1
                        if one == tile:
                            return ring_index(b, n)[0]
            tile = (tile[0], g % G, 0)
            step = [one for tiles in step_tiles(G - 1, False, False) for one in tiles]
            return ring_index(b, step.index(tile) + 1 - len(step))[0]

        s_zeroed = sem("s_zeroed")
        s_stack = [sem(f"s_stack{g}") for g in range(G)]
        s_scores = sem("s_scores")
        s_exp = sem("s_exp")
        s_causal = sem("s_causal")
        s_pv = sem("s_pv")
        s_oout = sem("s_oout")
        s_full = sem("s_full")
        s_free = sem("s_free")
        s_link = sem("s_link")
        s_maxrow = sem("s_maxrow")
        s_xa = sem("s_xa")
        s_biased = sem("s_biased")
        s_x1out = sem("s_x1out")
        s_tbp = sem("s_tbp")
        s_wr = sem("s_wr")
        s_wrc = sem("s_wrc")
        s_stats2 = sem("s_stats2")
        s_aggr2 = sem("s_aggr2")
        s_var2 = sem("s_var2")
        s_rstd2 = sem("s_rstd2")
        s_xn2 = sem("s_xn2")
        s_rowhi = sem("s_rowhi")
        s_rowlo = sem("s_rowlo")
        s_rowout = sem("s_rowout")
        s_wload = sem("s_wload")
        s_ehi = sem("s_ehi")
        s_elo = sem("s_elo")
        LOADS = 9

        with ExitStack() as phase:
            def sb(name, shape, dt):
                return phase.enter_context(nc.sbuf_tensor(name, shape, dt))

            taken = [0]

            def view(shape, dt):
                words = int(np.prod(shape[1:])) * (1 if dt == F32 else 2) // (1 if dt == F32 else 4)
                part_ = arena[:, taken[0]:taken[0] + words]
                taken[0] += words
                part_ = part_ if dt == F32 else part_.bitcast(dt)
                names = "abcd"[:len(shape) - 1]
                return part_.rearrange("p (%s) -> p %s" % (" ".join(names), " ".join(names)),
                                       **dict(zip(names, shape[1:])))

            wf = view([P, NCH, C], F32)
            x_in = view([P, TT, C], F32)
            ctx_in = view([P, TT, CC], F32)
            xn = view([P, TT, C], F32)
            xt_hi = view([P, KT + 1, T], F16)
            xt_lo = view([P, KT + 1, T], F16)
            pj_out = view([P, NPT, 2, T], F16)
            v_out = view([P, TT, 2, H, 32], F32)
            assert taken[0] <= 16384
            bias_col = sb("bias_col", [P, 4, KT], F32)
            bias_row = sb("bias_row", [P, 2, C], F32)
            stats = sb("stats", [P, TT, 6], F32)
            mean_var = sb("mean_var", [P, TT, 2], F32)
            var_eps = sb("var_eps", [P, TT], F32)
            rstd = sb("rstd", [P, TT], F32)
            g_in = sb("g_in", [P, 2], F32)
            q_st = sb("q_st", [P, G, 2, 4, T], F16)
            k_st = sb("k_st", [P, G, 2, 4, T], F16)
            v_st = sb("v_st", [P, G, 2, TT, 4 * 32], F32)
            probs = arena[:, 8192:].rearrange("p (a b c) -> p a b c", a=4, b=4)
            o_sb = sb("o_sb", [P, 2, T], F32)
            negmax = sb("negmax", [P, 2, TT, 8], F32)
            maxrow = sb("maxrow", [8, T], F16)
            rec = sb("rec", [P, 2, TT, 4], F32)
            part = sb("part", [P, TT, 4, D], F32)
            y = sb("y", [P, TT, C], F32)
            yt_hi = sb("yt_hi", [P, KT, T], F16)
            yt_lo = sb("yt_lo", [P, KT, T], F16)
            xa = sb("xa", [P, TT, C], F32)
            xn2 = sb("xn2", [P, TT, C], F32)
            rows_hi = yt_hi[:].rearrange("p k n -> p (k n)").rearrange("p (t c) -> p t c", c=C)
            rows_lo = yt_lo[:].rearrange("p k n -> p (k n)").rearrange("p (t c) -> p t c", c=C)
            x2t = sb("x2t", [P, 2, KT, T], F16)
            w_early = sb("w_early", [P, W_COLS], F32)
            tbp = sb("tbp", [P, C], F32)
            block = phase.enter_context(nc.Block())

            def store(sp, b):
                for n in range(NPT):
                    sp.wait_ge(s_pjlo, b * NPJ + n + 1)
                    sp.dma_start(
                        proj_dram[b, n // KT % 2, n % KT * 2:n % KT * 2 + 2, n // KT // 2].rearrange("g r l n -> g r (l n)"),
                        pj_out[:, n].rearrange("p l n -> p (l n)")).then_inc(s_projout, 16)
                for t in range(TT):
                    sp.wait_ge(s_pjlo, b * NPJ + NPT + t + 1)
                    sp.dma_start(v_dram[b, :, t::TT], v_out[:, t].rearrange("p a h e -> p a (h e)")).then_inc(s_vout, 16)

            @block.sync
            def _(sp):
                def load_group(b, g):
                    for half in range(2):
                        for rep in range(2):
                            for dst, which, r in ((q_st, 0, 32 * half + 16 * rep), (k_st, 1, 32 * rep + 16 * half)):
                                sp.dma_start(dst[r:r + 16, g].rearrange("d w j n -> d (w j) n"),
                                             proj_dram[b, which, g, :, :, half, :].rearrange(
                                                 "w (j d) n -> d (w j) n", d=D)).then_inc(s_stack[g], 16)
                    sp.dma_start(v_st[:, g].rearrange("p a t e -> p (a t) e"),
                                 v_dram[b, :, :, g * 128:(g + 1) * 128]).then_inc(s_stack[g], 16)

                sp.dma_start(x_in[:], x_rows[0].rearrange("t p c -> p t c")).then_inc(s_x, 16)
                for w, at in ((Wq, CQ), (Wk, CK), (Wcq, CCQ)):
                    sp.dma_start(wf[:, at:at + KT, :], w.rearrange("(k p) n -> p k n", p=P)).then_inc(s_wfirst, 16)
                sp.dma_start(ctx_in[:], ctx_rows[0].rearrange("t p c -> p t c")).then_inc(s_ctx, 16)
                for w, at, k in ((Wv, CV, KT), (Wp, CP, KT), (Wck, CCK, 1), (Wcv, CCV, 1)):
                    sp.dma_start(wf[:, at:at + k, :], w.rearrange("(k p) n -> p k n", p=P)).then_inc(s_load, 16)
                for n, v in enumerate((bq, bk, bcq, bck)):
                    sp.dma_start(bias_col[:, n, :], v.rearrange("(k p) -> p k", p=P),
                                   allow_slow_non_contiguous=True).then_inc(s_load, 16)
                for n, v in enumerate((bv, bcv)):
                    sp.dma_start(bias_row[:, n, :], v.partition_broadcast(P)).then_inc(s_load, 16)
                sp.dma_start(g_in[:, 0:1], g_xattn.partition_broadcast(P)).then_inc(s_load, 16)
                sp.dma_start(g_in[:, 1:2], g_ffn.partition_broadcast(P)).then_inc(s_load, 16)

                def load_x(b):
                    sp.wait_ge(s_xn, b)
                    sp.dma_start(x_in[:], x_rows[b].rearrange("t p c -> p t c")).then_inc(s_x, 16)

                def projections(b):
                    sp.wait_ge(s_tr, b * 3 + 3)
                    sp.dma_start(ctx_in[:], ctx_rows[b + 1].rearrange("t p c -> p t c")).then_inc(s_ctx, 16)
                    store(sp, b)

                for k in range(KT):
                    sp.dma_start(wr[:, k, :], router_w[:, k * P:(k + 1) * P].rearrange("e p -> p e"),
                                 allow_slow_non_contiguous=True).then_inc(s_wr, 16)
                sp.dma_start(tbp[:], bp.partition_broadcast(P)).then_inc(s_tbp, 16)
                load_x(1)
                projections(0)
                load_x(2)
                for b in range(1, B - 1):
                    projections(b)
                    if b + 2 < B:
                        load_x(b + 2)
                    sp.wait_ge(s_projout, 16 * NPT * (b + 1))
                    sp.wait_ge(s_vout, 16 * TT * (b + 1))
                    load_group(0, b - 1)
                store(sp, B - 1)
                sp.wait_ge(s_projout, 16 * NPT * B)
                sp.wait_ge(s_vout, 16 * TT * B)

                def max_rows(g, ring):
                    sp.wait_ge(s_free, ring + 1)
                    for n in range(2):
                        sp.dma_start(q_st[127:128, g, n], maxrow[4 * n:4 * n + 4, :]).then_inc(s_maxrow, 16)

                for g in range(B - 2, G):
                    load_group(0, g)
                max_rows(0, NM)

                def batch(b, first, last):
                    n = 0
                    for g in range(G):
                        if first or last:
                            c = g + (G if last else 0)
                            wait(sp, s_elo, c)
                            sp.dma_start(w_early[:].rearrange("p (k n) -> p k n", k=(KT, FT)[c % 2]),
                                         expert_rows(c)).then_inc(s_wload, 16)
                        units = step_tiles(g, first, last)
                        if not (first and g == 0):
                            if g > 0 and not last:
                                sp.wait_ge(s_pv, b * 32 + 8 * g)
                                load_group(b + 1, g - 1)
                            if g == 0:
                                sp.wait_ge(s_pv, b * 32)
                                load_group(b, G - 1)
                        if not (last and g == G - 1):
                            max_rows((g + 1) % G, ring_index(b, n + place(g, first, last, "turn_max", g + 1))[0])
                        n += sum(len(tiles) for tiles in units)
                        if g == 0:
                            if not first:
                                store_x1(b - 1, finish_ring(b))
                                sp.wait_ge(s_x1out, b * 16)
                                sp.wait_ge(s_xn2, b)
                            sp.dma_start(xa[:], x_rows[b].rearrange("t p c -> p t c")).then_inc(s_xa, 16)
                        if g == 1 and not first:
                            sp.wait_ge(s_rowlo, b + 1)
                            for half, rows in enumerate((rows_hi, rows_lo)):
                                sp.dma_start(x2_dram[bass.ds(b * T - T, T), half * C:(half + 1) * C].rearrange(
                                    "(t p) n -> p t n", p=P), rows).then_inc(s_rowout, 16)

                def finish_ring(b):
                    return ring_index(b, place(0, False, False, "project", 1))[0]

                def store_x1(b, ring):
                    sp.wait_ge(s_free, ring + 1)
                    sp.dma_start(x1_all[:, bass.ds(b, 1)].rearrange("p a t c -> p (a t) c"), xa[:]).then_inc(s_x1out, 16)

                batch(0, True, False)
                with sp.Fori(1, B - 1) as b:
                    batch(b, False, False)
                batch(B - 1, False, True)
                sp.wait_ge(s_x1out, 16 * (B - 1))

            @block.gpsimd
            def _(pool):
                pool.memset(ident[:], 0.0).then_inc(s_consts, 1)
                pool.memset(ident_bf[:], 0.0).then_inc(s_consts, 1)
                pool.memset(future[:], 0.0).then_inc(s_consts, 1)
                pool.memset(half_neg[:], -0.5).then_inc(s_consts, 1)
                pool.memset(v_out[:], 1.0).then_inc(s_consts, 1)
                pool.wait_ge(s_consts, 5)
                diagonal = dict(pattern=[[-1, P]], base=0, channel_multiplier=1)
                pool.affine_select(out=ident[:], in_=ident[:], compare_op=ALU.not_equal, fill=1.0,
                                   **diagonal).then_inc(s_consts, 1)
                pool.affine_select(out=ident_bf[:], in_=ident_bf[:], compare_op=ALU.not_equal, fill=1.0,
                                   **diagonal).then_inc(s_consts, 1)
                pool.affine_select(out=future[:], in_=future[:], compare_op=ALU.is_ge, fill=MASKED,
                                   **diagonal).then_inc(s_consts, 1)

                def inverse_root(b):
                    pool.wait_ge(s_var, b + 1)
                    pool.tensor_tensor(rstd[:], var_eps[:], half_neg[:], ALU.pow).then_inc(s_rstd, 1)

                inverse_root(0)
                pool.wait_ge(s_whi, 4)
                pool.tensor_tensor(w_lo[:, CV:], wf[:, CV:], w_hi[:, CV:], ALU.subtract).then_inc(s_wlolate, 1)
                pool.wait_ge(s_wlolate, 1)
                with pool.Fori(0, B - 1) as b:
                    inverse_root(b + 1)
                pool.wait_ge(s_rstd, B)
                pool.memset(k_st[64:128], 1.0).then_inc(s_zeroed, 1)
                pool.wait_ge(s_zeroed, 1)
                pool.memset(q_st[64:128].bitcast(F32), 0.0).then_inc(s_zeroed, 1)
                pool.wait_ge(s_zeroed, 2)

                pool.wait_ge(s_tbp, 17)
                pool.memset(pool_tick[:], 0.0).then_inc(s_rowlo, 1)
                pool.wait_ge(s_rowlo, 1)
                pool.memset(pool_tick[:], 0.0).then_inc(s_rowout, 1)
                pool.wait_ge(s_rowout, 1)

                def batch(b, first, last):
                    for g in range(G):
                        for u in range(4):
                            pool.wait_ge(s_exp, b * 64 + g * 16 + 2 * u + 2)
                            wait(pool, s_causal, b * 16 + g * 4 + u)
                            pool.tensor_tensor(pool_tick[:], half_neg[:, 0:1], half_neg[:, 0:1], ALU.mult)
                            pool.affine_select(out=probs[:, u, :, 0:P], in_=probs[:, u, :, 0:P], pattern=[[0, 4], [1, P]],
                                               compare_op=ALU.is_ge, fill=0.0, base=0,
                                               channel_multiplier=-1).then_inc(s_causal, 1)
                        if g == 0 and not first:
                            pool.wait_ge(s_var2, b)
                            pool.tensor_tensor(rstd[:], var_eps[:], half_neg[:], ALU.pow).then_inc(s_rstd2, 1)
                        if g == 1 and not first:
                            pool.wait_ge(s_rowhi, b)
                            pool.tensor_tensor(rows_lo, xn2[:], rows_hi, ALU.subtract).then_inc(s_rowlo, 1)
                        if g == 2:
                            pool.wait_ge(s_xa, b * 16 + 16)
                            pool.tensor_tensor(xa[:], xa[:], tbp[:].unsqueeze(1).broadcast_to([P, TT, C]),
                                               ALU.add).then_inc(s_biased, 1)
                        if first or last:
                            c = g + (G if last else 0)
                            pool.wait_ge(s_ehi, c + 1)
                            pool.tensor_tensor(we[:, c // 2, c % 2, 1, :], w_early[:], we[:, c // 2, c % 2, 0, :],
                                               ALU.subtract).then_inc(s_elo, 1)

                batch(0, True, False)
                with pool.Fori(1, B - 1) as b:
                    batch(b, False, False)
                batch(B - 1, False, True)

            @block.scalar
            def _(act):
                act.wait_ge(s_wfirst, 16 * 3)
                for at, scale in ((CQ, SCALE), (CK, 1.0), (CCQ, SCALE)):
                    act.activation(w_hi[:, at:at + KT], wf[:, at:at + KT], ACT.Copy, scale=scale).then_inc(s_whi, 1)

                def turned_high(b):
                    for n in range(KT + 1):
                        act.wait_ge(s_tr, b * 3 + n + 1)
                        if n == 0:
                            wait(act, s_pj, b * NPJ)
                        act.activation(xt_hi[:, n, :], bank[:, n, :], ACT.Copy).then_inc(s_trhi, 1)

                def projected(b):
                    for n in range(NPT):
                        act.wait_ge(s_pj, b * NPJ + n + 1)
                        if n == 0:
                            wait(act, s_projout, b * (16 * NPT))
                        act.activation(pj_out[:, n, 0, :], bank[:, 3 + n % 4, :], ACT.Identity,
                                       bias=bias_col[:, n // KT, n % KT:n % KT + 1]).then_inc(s_pjhi, 1)

                turned_high(0)
                act.wait_ge(s_load, 16 * 12)
                act.activation(w_hi[:, CV:], wf[:, CV:], ACT.Copy).then_inc(s_whi, 1)
                act.activation(tanh_g[:], g_in[:], ACT.Tanh).then_inc(s_tanh, 1)
                act.wait_ge(s_wscaled, 1)
                projected(0)
                with act.Fori(1, B) as b:
                    turned_high(b)
                    projected(b)

                act.wait_ge(s_pjlo, B * NPJ)
                act.wait_ge(s_projout, 16 * NPT * B)
                act.wait_ge(s_vout, 16 * TT * B)

                def out_of_bank(b, g, half, last=False):
                    act.wait_ge(s_pv, b * 32 + g * 8 + 4 * half + 4)
                    if not (isinstance(b, int) and b == 0 and g == 0):
                        act.wait_ge(s_full, turned(b, g - 1, half, last))
                    act.activation(o_sb[:, half, :], bank[:, SUM_BANK, :], ACT.Copy).then_inc(s_oout, 1)

                def batch(b, first, last):
                    for g in range(G):
                        for u in range(8):
                            n = T - P * u if u < 4 else T
                            wait(act, s_pv, b * 32 + (g * 8 + u - 3))
                            for pair in range(2):
                                act.wait_ge(s_scores, b * 64 + (g * 16 + 2 * u + pair + 1))
                                act.activation(probs[:, u % 4, 2 * pair:2 * pair + 2, 0:n],
                                               bank[:, 2 * pair:2 * pair + 2, 0:n], ACT.Exp).then_inc(s_exp, 1)
                            if u == 0 and not (first and g == 0):
                                out_of_bank(b, g - 1, 1, last)
                            if u == 4:
                                out_of_bank(b, g, 0, last)
                            if g == 1 and u == 2 and not first:
                                act.wait_ge(s_xn2, b)
                                act.activation(rows_hi, xn2[:], ACT.Copy).then_inc(s_rowhi, 1)
                            if u == 5 and (first or last):
                                c = g + (G if last else 0)
                                act.wait_ge(s_wload, 16 * (c + 1))
                                act.activation(we[:, c // 2, c % 2, 0, :], w_early[:], ACT.Copy).then_inc(s_ehi, 1)

                batch(0, True, False)
                with act.Fori(1, B - 1) as b:
                    batch(b, False, False)
                batch(B - 1, False, True)
                out_of_bank(B - 1, G - 1, 1, True)

            @block.vector
            def _(dve):
                def statistics_of_x(b):
                    dve.wait_ge(s_x, (b + 1) * 16)
                    for t in range(TT):
                        last = dve.bn_stats(stats[:, t, :], x_in[:, t, :])
                    last.then_inc(s_stats, 1)
                    dve.wait_ge(s_stats, b + 1)
                    dve.memset(tick[:], 0.0)
                    for t in range(TT):
                        last = dve.bn_aggr(mean_var[:, t, :], stats[:, t, :])
                    last.then_inc(s_aggr, 1)
                    dve.wait_ge(s_aggr, b + 1)
                    dve.tensor_scalar(var_eps[:], mean_var[:, :, 1], EPS, None, ALU.add).then_inc(s_var, 1)

                def normalise_x(b):
                    dve.wait_ge(s_rstd, b + 1)
                    wait(dve, s_tr, b * 3)
                    for t in range(TT):
                        last = dve.tensor_scalar(xn[:, t, :], x_in[:, t, :], mean_var[:, t, 0:1], rstd[:, t:t + 1],
                                                 ALU.subtract, ALU.mult)
                    last.then_inc(s_xn, 1)

                def transposed_low(b):
                    for n in range(KT + 1):
                        dve.wait_ge(s_trhi, b * 3 + n + 1)
                        dve.tensor_tensor(xt_lo[:, n, :], bank[:, n, :], xt_hi[:, n, :], ALU.subtract).then_inc(s_trlo, 1)

                def projected(b, n):
                    if n < NPT:
                        dve.wait_ge(s_pjhi, b * NPT + n + 1)
                        dve.scalar_tensor_tensor(out=pj_out[:, n, 1, :], in0=bank[:, 3 + n % 4, :],
                                                 scalar=bias_col[:, n // KT, n % KT:n % KT + 1],
                                                 in1=pj_out[:, n, 0, :], op0=ALU.add,
                                                 op1=ALU.subtract).then_inc(s_pjlo, 1)
                    else:
                        dve.wait_ge(s_pj, b * NPJ + n + 1)
                        if n == NPT:
                            wait(dve, s_vout, b * (16 * TT))
                        dve.tensor_tensor(v_out[:, n - NPT, :, :, 0:D],
                                          bank[:, 3 + n % 4, :].rearrange("p (a h d) -> p a h d", a=2, h=H),
                                          bias_row[:].rearrange("p a (h d) -> p a h d", h=H),
                                          ALU.add).then_inc(s_pjlo, 1)

                dve.wait_ge(s_consts, 5)
                statistics_of_x(0)
                normalise_x(0)
                for n, (at, scale) in enumerate(((CQ, SCALE), (CK, 1.0), (CCQ, SCALE))):
                    dve.wait_ge(s_whi, n + 1)
                    dve.scalar_tensor_tensor(out=w_lo[:, at:at + KT], in0=wf[:, at:at + KT], scalar=scale,
                                             in1=w_hi[:, at:at + KT], op0=ALU.mult, op1=ALU.subtract).then_inc(s_wlo, 1)
                dve.wait_ge(s_load, 16 * 12)
                dve.tensor_scalar(bias_col[:, 0:3:2, :], bias_col[:, 0:3:2, :], SCALE, None, ALU.mult).then_inc(s_wscaled, 1)

                def projections(b):
                    transposed_low(b)
                    for n in range(NPJ):
                        projected(b, n)
                        if n == 3:
                            statistics_of_x(b + 1)
                        if n == 6:
                            normalise_x(b + 1)

                projections(0)
                with dve.Fori(1, B - 1) as b:
                    projections(b)
                transposed_low(B - 1)
                for n in range(NPJ):
                    projected(B - 1, n)

                dve.wait_ge(s_tbp, 16)
                dve.tensor_scalar(tbp[:], tbp[:], tanh_g[:, 0:1], None, ALU.mult).then_inc(s_tbp, 1)
                dve.wait_ge(s_tbp, 17)
                dve.wait_ge(s_wr, 16 * KT)
                dve.tensor_copy(wr_hi[:], wr[:]).then_inc(s_wrc, 1)
                dve.wait_ge(s_wrc, 1)
                dve.tensor_tensor(wr_lo[:], wr[:], wr_hi[:], ALU.subtract).then_inc(s_wrc, 1)

                def consume(b, n, tile, step, link, par=0):
                    kind, a, q = tile[:3]
                    ring, at = ring_index(b, n) if n is not None else step
                    dve.wait_ge(s_full, ring + 1)
                    bk_ = bank[:, at, :]
                    if kind == "cross":
                        ins = dve.tensor_reduce(negmax[:, par, q, 4 + a:5 + a], bk_, X, ALU.max, negate=True)
                    elif kind == "self3":
                        ins = dve.tensor_reduce(negmax[:, par, 3, a:a + 1], bk_, X, ALU.max, negate=True)
                    elif kind == "self02":
                        dve.tensor_reduce(negmax[:, par, 0, a:a + 1], bk_[:, 0:P], X, ALU.max, negate=True)
                        ins = dve.tensor_reduce(negmax[:, par, 2, a:a + 1], bk_[:, P:T], X, ALU.max, negate=True)
                    elif kind == "self1":
                        ins = dve.tensor_reduce(negmax[:, par, 1, a:a + 2], bk_.rearrange("p (j n) -> p j n", j=2), X,
                                                ALU.max, negate=True)
                    elif kind == "turn_max":
                        wait(dve, s_maxrow, (b * G + a) * 32)
                        ins = dve.tensor_copy(maxrow[:], bank[0:8, at, :])
                    elif kind in ("turn_self", "turn_cross"):
                        g = a % G
                        o = bk_.rearrange("p (t j e) -> p t j e", t=TT, j=4)
                        half = int(kind == "turn_cross")
                        dve.reciprocal(rec[:, half], o[:, :, :, D]).then_inc(s_link, 1)
                        link = link + 1
                        dve.wait_ge(s_link, link)
                        r = rec[:, half].unsqueeze(3).broadcast_to([P, TT, 4, D])
                        yg = y[:, :, g * 64:(g + 1) * 64].rearrange("p t (j d) -> p t j d", j=4)
                        if kind == "turn_self":
                            ins = dve.tensor_tensor(yg, o[:, :, :, 0:D], r, ALU.mult)
                        else:
                            dve.tensor_tensor(part[:], o[:, :, :, 0:D], r, ALU.mult).then_inc(s_link, 1)
                            link = link + 1
                            dve.wait_ge(s_link, link)
                            ins = dve.tensor_tensor(yg, yg, part[:], ALU.add)
                    elif kind == "turn_y":
                        if a == 0:
                            dve.wait_ge(s_rowout, b * 32 - 31)
                            dve.memset(tick[:], 0.0)
                            dve.wait_ge(s_full, ring + 1)
                        dve.tensor_copy(yt_hi[:, a, :], bk_).then_inc(s_link, 1)
                        link = link + 1
                        dve.wait_ge(s_link, link)
                        ins = dve.tensor_tensor(yt_lo[:, a, :], bk_, yt_hi[:, a, :], ALU.subtract)
                    elif kind == "turn_x2":
                        dve.tensor_copy(x2t[:, 0, a, :], bk_).then_inc(s_link, 1)
                        link = link + 1
                        dve.wait_ge(s_link, link)
                        ins = dve.tensor_tensor(x2t[:, 1, a, :], bk_, x2t[:, 0, a, :], ALU.subtract)
                    elif kind == "route":
                        dve.memset(tick[:], 0.0)
                        ins = dve.tensor_copy(lg[:, bass.ds(b - 1, 1), :].rearrange("p a n -> p (a n)"), bk_[:, 0:TT * NE])
                    elif kind == "project":
                        if a == 0:
                            dve.wait_ge(s_biased, b)
                        xs = xa[:, 2 * a:2 * a + 2, :]
                        out_ = xs if par == 0 else x1_all[:, B - 1, 2 * a:2 * a + 2, :]
                        ins = dve.scalar_tensor_tensor(out=out_,
                                                       in0=bk_.rearrange("p (t c) -> p t c", t=2),
                                                       scalar=tanh_g[:, 0:1], in1=xs, op0=ALU.mult, op1=ALU.add)
                    ins.then_inc(s_free, 1)
                    return link

                def statistics(b, ring):
                    dve.wait_ge(s_free, ring + 1)
                    for t in range(TT):
                        last = dve.bn_stats(stats[:, t, :], xa[:, t, :])
                    last.then_inc(s_stats2, 1)
                    dve.wait_ge(s_stats2, b)
                    dve.memset(tick[:], 0.0)
                    for t in range(TT):
                        last = dve.bn_aggr(mean_var[:, t, :], stats[:, t, :])
                    last.then_inc(s_aggr2, 1)
                    dve.wait_ge(s_aggr2, b)
                    dve.tensor_scalar(var_eps[:], mean_var[:, :, 1], EPS, None, ALU.add).then_inc(s_var2, 1)

                def normalise(b):
                    dve.wait_ge(s_rstd2, b)
                    dve.wait_ge(s_rowlo, b)
                    for t in range(TT):
                        last = dve.tensor_scalar(xn2[:, t, :], xa[:, t, :], mean_var[:, t, 0:1], rstd[:, t:t + 1],
                                                 ALU.subtract, ALU.mult)
                    last.then_inc(s_xn2, 1)

                def batch(b, first, last, link):
                    n = 0
                    for g in range(G):
                        for u, tiles in enumerate(step_tiles(g, first, last)):
                            for tile in tiles:
                                link = consume(b, n, tile, None, link, tile[3] % 2 if len(tile) == 4 else 0)
                                n += 1
                                if tile[:2] == ("project", 1):
                                    statistics(b, ring_index(b, n - 1)[0])
                            if g == 0 and u == 6 and not first:
                                normalise(b)
                    return link, n

                for n, tile in enumerate(max_tiles(0) + [("turn_max", 0, 0)]):
                    consume(0, None, tile, (n, RING_BANK + n % RING), 0)
                LINKS = [G + 2 * (G - 1), G * 3 + 4]
                batch(0, True, False, 0)
                with dve.Fori(1, B - 1) as b:
                    batch(b, False, False, b * LINKS[1] + (LINKS[0] - LINKS[1]))
                at = (B - 1) * LINKS[1] + LINKS[0] - LINKS[1]
                at, n = batch(B - 1, False, True, at)
                for k, tile in enumerate((("turn_cross", G - 1, 0), ("turn_y", 0, 0), ("turn_y", 1, 1),
                                          ("project", 0, 0), ("project", 1, 1))):
                    if tile[0] == "project" and tile[1] == 0:
                        dve.wait_ge(s_biased, B)
                    if tile == ("turn_y", 0, 0):
                        dve.wait_ge(s_rowout, 32 * (B - 1) + 1)
                    at = consume(B - 1, n + k, tile, None, at, 1)

            @block.tensor
            def _(pe):
                pe.wait_ge(s_consts, 8)

                def turn(b):
                    pe.wait_ge(s_xn, b + 1)
                    wait(pe, s_trlo, b * 3)
                    for k in range(KT):
                        for t in range(TT):
                            last = pe.transpose(bank[:, k, t * P:(t + 1) * P], xn[:, t, k * P:(k + 1) * P], ident[:])
                        last.then_inc(s_tr, 1)
                    pe.wait_ge(s_ctx, (b + 1) * 16)
                    for t in range(TT):
                        last = pe.transpose(bank[:, KT, t * P:(t + 1) * P], ctx_in[:, t, :], ident[:])
                    last.then_inc(s_tr, 1)

                def projections(b, last_batch):
                    for n in range(NPJ):
                        if n == 3 * KT:
                            pe.wait_ge(s_trlo, b * 3 + 3)
                            pe.wait_ge(s_wlolate, 1)
                        if n == NPT + 3 and not last_batch:
                            turn(b + 1)
                        wait(pe, s_pjlo, b * NPJ + (n - 3))
                        if n < NPT:
                            at, nk = PROJ[n // KT]
                            m = slice((n % KT) * P, (n % KT + 1) * P)
                            passes = [(k, w, xt_hi) for k in range(nk) for w in (w_hi, w_lo)] + \
                                     [(k, w_hi, xt_lo) for k in range(nk)]
                            for i, (k, w, a) in enumerate(passes):
                                if n == 0 and w is w_hi:
                                    pe.wait_ge(s_trhi if a is xt_hi else s_trlo, b * 3 + (k + 1))
                                if n == 0 and i == 0:
                                    pe.wait_ge(s_wlo, 3)
                                last = pe.matmul(bank[:, 3 + n % 4, :], w[:, at + k, m], a[:, k if nk > 1 else KT, :],
                                                 start=(i == 0), stop=(i == len(passes) - 1))
                        else:
                            t = slice((n - NPT) * P, (n - NPT + 1) * P)
                            for half, at, xk, nk in ((0, CV, 0, KT), (1, CCV, KT, 1)):
                                for k in range(nk):
                                    for w, a in ((w_hi, xt_hi), (w_lo, xt_hi), (w_hi, xt_lo)):
                                        last = pe.matmul(bank[:, 3 + n % 4, half * C:(half + 1) * C], a[:, xk + k, t],
                                                         w[:, at + k, :],
                                                         start=(k == 0 and w is w_hi and a is xt_hi),
                                                         stop=(k == nk - 1 and a is xt_lo))
                        last.then_inc(s_pj, 1)

                turn(0)
                projections(0, False)
                with pe.Fori(1, B - 1) as b:
                    projections(b, False)
                projections(B - 1, True)

                pe.wait_ge(s_pjlo, B * NPJ)
                pe.wait_ge(s_wrc, 2)

                def scores_for_max(tile, bk_):
                    kind, a, q, slot = tile

                    def own(j, q, to, width):
                        pe.matmul(bk_[:, to:to + width], q_st[0:96, slot, 0, j, q * P:(q + 1) * P],
                                  k_st[0:96, slot, 0, j, 0:width], start=True, stop=False)
                        return pe.matmul(bk_[:, to + width - P:to + width], ident_bf[:], future[:], start=False, stop=True)

                    if kind == "cross":
                        return pe.matmul(bk_, q_st[0:96, slot, 1, a, q * P:(q + 1) * P], k_st[0:96, slot, 1, a, :],
                                         start=True, stop=True)
                    if kind == "self3":
                        return own(a, 3, 0, T)
                    if kind == "self02":
                        own(a, 0, 0, P)
                        return own(a, 2, P, 3 * P)
                    own(a, 1, 0, 2 * P)
                    return own(a + 1, 1, 2 * P, 2 * P)

                def tile_of(b, ring, at, tile):
                    kind, a, q = tile[:3]
                    bk_ = bank[:, at, :]
                    wait(pe, s_free, ring - (RING - 1))
                    if kind in ("cross", "self3", "self02", "self1"):
                        last = scores_for_max(tile, bk_)
                    elif kind == "turn_max":
                        pe.wait_ge(s_free, ring - q)
                        for t in range(TT):
                            last = pe.transpose(bank[0:8, at, t * P:(t + 1) * P], negmax[:, a % 2, t, :], ident[:])
                    elif kind in ("turn_self", "turn_cross"):
                        half = int(kind == "turn_cross")
                        pe.wait_ge(s_oout, b * 8 + 2 * a + half + 1)
                        for t in range(TT):
                            last = pe.transpose(bk_[:, t * P:(t + 1) * P], o_sb[:, half, t * P:(t + 1) * P], ident[:])
                    elif kind == "turn_y":
                        pe.wait_ge(s_free, ring - q)
                        for t in range(TT):
                            last = pe.transpose(bk_[:, t * P:(t + 1) * P], y[:, t, a * P:(a + 1) * P], ident[:])
                    elif kind == "turn_x2":
                        pe.wait_ge(s_xn2, b)
                        for t in range(TT):
                            last = pe.transpose(bk_[:, t * P:(t + 1) * P], xn2[:, t, a * P:(a + 1) * P], ident[:])
                    elif kind == "route":
                        pe.wait_ge(s_free, ring - q)
                        last = logits(bk_, x2t)
                    elif kind == "project":
                        pe.wait_ge(s_free, ring - q)
                        for t in range(2):
                            ts = slice((2 * a + t) * P, (2 * a + t + 1) * P)
                            for k in range(KT):
                                for w, act_ in ((w_hi, yt_hi), (w_lo, yt_hi), (w_hi, yt_lo)):
                                    last = pe.matmul(bk_[:, t * C:(t + 1) * C], act_[:, k, ts], w[:, CP + k, :],
                                                     start=(k == 0 and w is w_hi and act_ is yt_hi),
                                                     stop=(k == KT - 1 and act_ is yt_lo))
                    last.then_inc(s_full, 1)

                def logits(to, x2t):
                    for t in range(TT):
                        ts = slice(t * P, (t + 1) * P)
                        for k in range(KT):
                            for a, w in ((0, wr_hi), (0, wr_lo), (1, wr_hi)):
                                last = pe.matmul(to[:, t * NE:(t + 1) * NE], x2t[:, a, k, ts], w[:, k, :],
                                                 start=(k == 0 and a == 0 and w is wr_hi), stop=(k == KT - 1 and a == 1))
                    return last

                def values(b, g, u):
                    half, kt = u // 4, u % 4
                    q0 = kt * P if half == 0 else 0
                    slot = g % G
                    pe.wait_ge(s_exp, b * 64 + (g * 16 + 2 * u + 2))
                    if half == 0:
                        pe.wait_ge(s_causal, b * 16 + (g * 4 + kt + 1))
                    if kt == 0:
                        wait(pe, s_oout, b * 8 + (2 * g + half))
                    for j in range(4):
                        last = pe.matmul(bank[32 * j:32 * j + 32, SUM_BANK, q0:T],
                                         v_st[:, slot, half, kt, 32 * j:32 * j + 32],
                                         probs[:, kt, j, 0:T - q0], start=(kt == 0), stop=(kt == 3))
                    last.then_inc(s_pv, 1)

                def batch(b, first, last_batch):
                    n = 0
                    for g in range(G):
                        units = step_tiles(g, first, last_batch)

                        def ring_tiles(tiles, n):
                            for tile in tiles:
                                if tile[:3] == ("cross", 0, 0):
                                    loads = b + 1 if tile[3] > 1 or (first and g == 0) else b + 2
                                    pe.wait_ge(s_stack[tile[3]], loads * (16 * LOADS))
                                ring, at = ring_index(b, n)
                                tile_of(b, ring, at, tile)
                                n += 1
                            return n

                        if first and g == 0:
                            n = ring_tiles(units[0], n)
                            units[0] = []
                        pe.wait_ge(s_maxrow, b * 128 + 32 * (g + 1))
                        for u in range(8):
                            half, kt = u // 4, u % 4
                            q0 = kt * P if half == 0 else 0
                            count = len(units[u])
                            cuts = [0, 0, 1, count] if count < 3 else [0, 1, 2, count] if count == 3 else [0, 1, 3, count] if count == 4 else [0, 2, 3, count]
                            for piece in range(3):
                                if piece < 2:
                                    wait(pe, s_exp, b * 64 + (g * 16 + 2 * u + piece - 1))
                                    for j in (2 * piece, 2 * piece + 1):
                                        last = pe.matmul(bank[:, j, 0:T - q0], k_st[:, g, half, j, kt * P:(kt + 1) * P],
                                                         q_st[:, g, half, j, q0:T], start=True, stop=True)
                                    last.then_inc(s_scores, 1)
                                elif u > 0 or not (first and g == 0):
                                    values(b, g - 1 if u == 0 else g, (u - 1) % 8)
                                n = ring_tiles(units[u][cuts[piece]:cuts[piece + 1]], n)
                    return n

                pe.wait_ge(s_zeroed, 2)
                pe.wait_ge(s_stack[0], 16 * LOADS)
                for n, tile in enumerate(max_tiles(0) + [("turn_max", 0, 0)]):
                    tile_of(0, n, RING_BANK + n % RING, tile)
                batch(0, True, False)
                with pe.Fori(1, B - 1) as b:
                    batch(b, False, False)
                n = batch(B - 1, False, True)
                values(B - 1, G - 1, 7)
                for k, tile in enumerate((("turn_cross", G - 1, 0), ("turn_y", 0, 0), ("turn_y", 1, 1),
                                          ("project", 0, 0), ("project", 1, 1))):
                    ring, at = ring_index(B - 1, n + k)
                    tile_of(B - 1, ring, at, tile)

        N = B * TT
        NSLOT = 2 * N + NE - 1
        assert NSLOT % 2 == 1
        RB, YB = 4, 4
        QUADS = (NSLOT - 3) // YB
        assert YB * QUADS + 3 == NSLOT
        ys_dram = nc.dram_tensor("ys_dram", [2 * N * P + NSLOT * P, C], F32).ap()

        s_mask = sem("s_mask")
        s_count = sem("s_count")
        s_countc = sem("s_countc")
        s_tr2 = sem("s_tr2")
        s_tr2hi = sem("s_tr2hi")
        s_tr2lo = sem("s_tr2lo")
        s_logit = sem("s_logit")
        s_top = sem("s_top")
        s_route = sem("s_route")
        s_chosen = sem("s_chosen")
        s_rank = sem("s_rank")
        s_gap = sem("s_gap")
        s_gexp = sem("s_gexp")
        s_place = sem("s_place")
        s_rowhot = sem("s_rowhot")
        s_slotat = sem("s_slotat")
        s_slot = sem("s_slot")
        s_expert = sem("s_expert")
        s_inverse = sem("s_inverse")
        s_we = [sem(f"s_we{n}") for n in range(4)]
        s_xs = [sem(f"s_xs{n}") for n in range(RB)]
        s_st = sem("s_st")
        s_xt = sem("s_xt")
        s_up = sem("s_up")
        s_wslot = sem("s_wslot")
        s_gelu = sem("s_gelu")
        s_hlo = sem("s_hlo")
        s_down = sem("s_down")
        s_yev = sem("s_yev")
        s_yout = [sem(f"s_yout{n}") for n in range(YB)]
        s_back = [sem(f"s_back{b}") for b in range(B)]
        s_acc = sem("s_acc")
        s_out = sem("s_out")

        with ExitStack() as phase:
            def sb(name, shape, dt):
                return phase.enter_context(nc.sbuf_tensor(name, shape, dt))

            before = sb("before", [P, P], BF16)
            ones = sb("ones", [P, P], BF16)
            count = sb("count", [P, P + 1], F32)
            stats = sb("stats2", [P, TT, 6], F32)
            mean_var = sb("mean_var2", [P, TT, 2], F32)
            var_eps = sb("var_eps2", [P, TT], F32)
            rstd = sb("rstd2", [P, TT], F32)
            xn = sb("xn3", [P, TT, C], F32)
            rows = sb("rows", [P, TT, 2, C], F16)
            xt_st = sb("xt_st", [P, 2, KT, T], F16)
            top = sb("top", [P, N, 8], F32)
            top_i = sb("top_i", [P, N, 8], U32)
            top_f = sb("top_f", [P, N, 8], F32)
            gap = sb("gap", [P, N], F32)
            gap_e = sb("gap_e", [P, N], F32)
            g_sum = sb("g_sum", [P, N], F32)
            gates = sb("gates", [P, 2, N], F32)
            chosen = sb("chosen", [P, 2, N, NE], F32)
            chosen_bf = sb("chosen_bf", [P, N + 1, NE], BF16)
            rank = sb("rank", [P, N + 1, NE], F32)
            steps = sb("steps", [P, 16], F32)
            fills = sb("fills", [P, NE, 16], F32)
            slots = sb("slots", [P, NE], F32)
            earlier = sb("earlier", [P, NE, NE], F32)
            base_of = sb("base_of", [P, NE, NE], F32)
            base = sb("base", [P, NE], F32)
            at_or_after = sb("at_or_after", [P, NSLOT, NE], F32)
            expert_f = sb("expert_f", [P, NSLOT], F32)
            expert = sb("expert", [P, NSLOT], U32)
            picked = sb("picked", [P, 2, N, NE], F32)
            picked2 = sb("picked2", [P, 2, N, NE], F32)
            my_rank = sb("my_rank", [P, 2, N], F32)
            my_base = sb("my_base", [P, 2, N], F32)
            past = sb("past", [P, 2 * N, 16], F32)
            my_tile = sb("my_tile", [P, 2, N], F32)
            my_row = sb("my_row", [P, 2, N], F16)
            my_slot = sb("my_slot", [P, 2, N], F16)
            unused = sb("unused", [P, NSLOT], F32)
            unfilled = sb("unfilled", [P, NSLOT], F32)
            filled = sb("filled", [P, NSLOT], F32)
            target = sb("target", [P, NSLOT], U32)
            count_h = sb("count_h", [P, P], F16)
            token = sb("token", [P, N], F32)
            row_hot = sb("row_hot", [P, 2, N, P], F16)
            slot_at = sb("slot_at", [P, 2, N, NSLOT], F16)
            slot_hot = sb("slot_hot", [P, 2, N, NSLOT], F16)
            source = sb("source", [P, NSLOT], U32)
            w_in = sb("w_in", [P, 4, W_COLS], F32)
            w_slot = sb("w_slot", [P, RB, 2, 2, W_COLS], F16)
            ticks = sb("ticks", [P, RB], F32)
            xs = sb("xs", [P, RB, 2 * C], F16)
            xt = sb("xt", [P, 2, 4, P], F16)
            h32 = sb("h32", [P, 2, FT, P], F32)
            h_hi = sb("h_hi", [P, 2, FT, P], F16)
            h_lo = sb("h_lo", [P, 2, FT, P], F16)
            y_sb = sb("y_sb", [P, YB, C], F32)
            back = arena[:, 0:2 * N * C].rearrange("p (a b t c) -> p a b t c", a=2, b=B, t=TT)
            ident_h = sb("ident_h", [P, P], F16)
            block = phase.enter_context(nc.Block())
            PAIRS = (NSLOT - 3) // 2

            @block.sync
            def _(sp):
                for c in range(NE, 2 * NE):
                    if c >= NE + 4:
                        sp.wait_ge(s_elo, c - 3)
                    sp.dma_start(w_in[:, c % 4].rearrange("p (k n) -> p k n", k=(KT, FT)[c % 2]),
                                 expert_rows(c)).then_inc(s_we[c % 4], 16)
                sp.wait_ge(s_rowlo, B + 1)
                sp.dma_start(x2_dram[(B - 1) * T:B * T].rearrange("(t p) n -> p t n", p=P),
                             rows[:].rearrange("p t l c -> p t (l c)")).then_inc(s_rowout, 16)

                for n in range(YB):
                    sp.wait_ge(s_yout[n], 16 * ((NSLOT + YB - 1 - n) // YB))
                sp.wait_ge(s_wslot, NSLOT)
                for b in range(B):
                    for choice in range(2):
                        at = choice * N * P + b * T
                        sp.dma_start(back[:, choice, b], ys_dram[at:at + T].rearrange("(t p) c -> p t c", p=P)
                                     ).then_inc(s_back[b], 16)
                for b in range(B):
                    sp.wait_ge(s_acc, (b + 1) * 2 * TT)
                    sp.dma_start(out_rows[b].rearrange("t p c -> p t c"), x1_all[:, b]).then_inc(s_out, 16)
                sp.wait_ge(s_out, 16 * B)

            @block.gpsimd
            def _(pool):
                pool.memset(before[:], 1.0).then_inc(s_mask, 1)
                pool.memset(ones[:], 1.0).then_inc(s_mask, 1)
                pool.memset(ident_h[:], 0.0).then_inc(s_mask, 1)
                pool.memset(chosen_bf[:, N], 0.0).then_inc(s_mask, 1)
                pool.wait_ge(s_mask, 4)
                pool.affine_select(out=before[:], in_=before[:], compare_op=ALU.is_gt, fill=0.0,
                                   pattern=[[1, P]], base=0, channel_multiplier=-1).then_inc(s_mask, 1)
                pool.affine_select(out=ident_h[:], in_=ident_h[:], compare_op=ALU.not_equal, fill=1.0,
                                   pattern=[[-1, P]], base=0, channel_multiplier=1).then_inc(s_mask, 1)

                def low(c):
                    pool.wait_ge(s_ehi, c + 1)
                    pool.tensor_tensor(we[:, c // 2, c % 2, 1, :], w_in[:, c % 4], we[:, c // 2, c % 2, 0, :],
                                       ALU.subtract).then_inc(s_elo, 1)

                pool.wait_ge(s_var2, B)
                pool.tensor_tensor(rstd[:], var_eps[:], half_neg[:], ALU.pow).then_inc(s_rstd2, 1)
                low(NE)
                low(NE + 1)
                low(NE + 2)
                pool.wait_ge(s_rowhi, B)
                pool.tensor_tensor(rows[:, :, 1], xn[:], rows[:, :, 0], ALU.subtract).then_inc(s_rowlo, 1)
                for c in range(NE + 3, 2 * NE):
                    low(c)
                for choice in range(2):
                    pool.wait_ge(s_slotat, choice + 1)
                    pool.tensor_tensor(slot_hot[:, choice], slot_at[:, choice],
                                       token[:].unsqueeze(2).broadcast_to([P, N, NSLOT]), ALU.mult).then_inc(s_slot, 1)
                pool.wait_ge(s_rowout, 32 * (B - 1) + 17)
                pool.wait_ge(s_inverse, 1)

                def gather(s):
                    wait(pool, s_st, s - RB + 1)
                    pool.indirect_dma_start(xs[:, s % RB, :], None, x2_dram[:, :],
                                            bass.IndirectOffsetOnAxis(ap=source[:, s:s + 1], axis=0)
                                            ).then_inc(s_xs[s % RB], 16)

                for s in range(RB):
                    gather(s)
                pool.wait_ge(s_inverse, 2)
                for s in range(NSLOT):
                    if s + RB < NSLOT:
                        gather(s + RB)
                    pool.wait_ge(s_yev, s + 1)
                    pool.indirect_dma_start(ys_dram[:, :], bass.IndirectOffsetOnAxis(ap=target[:, s:s + 1], axis=0),
                                            y_sb[:, s % YB, :], None).then_inc(s_yout[s % YB], 16)

            @block.scalar
            def _(act):
                def high(c):
                    act.wait_ge(s_we[c % 4], 16 * ((c - NE) // 4 + 1))
                    act.activation(we[:, c // 2, c % 2, 0, :], w_in[:, c % 4], ACT.Copy).then_inc(s_ehi, 1)

                for c in range(NE, NE + 3):
                    high(c)
                for k in range(KT):
                    act.wait_ge(s_tr2, k + 1)
                    act.activation(xt_st[:, 0, k, :], bank[:, k, :], ACT.Copy).then_inc(s_tr2hi, 1)
                act.wait_ge(s_xn2, B)
                act.activation(rows[:, :, 0], xn[:], ACT.Copy).then_inc(s_rowhi, 1)
                for c in range(NE + 3, 2 * NE):
                    high(c)
                act.wait_ge(s_gap, 1)
                act.activation(gap_e[:], gap[:], ACT.Exp).then_inc(s_gexp, 1)

                def turned_rows(s, par):
                    act.wait_ge(s_st, s + 1)
                    wait(act, s_up, s - 1)
                    act.activation(xt[:, par].rearrange("p a n -> p (a n)"), bank[:, par].bitcast(F16)[:, 0:4 * P],
                                   ACT.Copy).then_inc(s_xt, 1)

                def gelu(s, par):
                    act.wait_ge(s_up, s + 1)
                    wait(act, s_down, s - 1)
                    act.activation(h32[:, par].rearrange("p m n -> p (m n)"), bank[:, 2 + par, :], ACT.Gelu)
                    act.activation(h_hi[:, par].rearrange("p m n -> p (m n)"), bank[:, 2 + par, :],
                                   ACT.Gelu).then_inc(s_gelu, 1)

                def output(s, n):
                    act.wait_ge(s_down, s + 1)
                    wait(act, s_yout[n], (s - n) * (16 // YB))
                    act.activation(y_sb[:, n], bank[:, 4 + n % 2, 0:C], ACT.Copy).then_inc(s_yev, 1)

                act.activation(h32[:, 0, 0, 0:N], gap[:], ACT.Gelu)
                turned_rows(0, 0)
                turned_rows(1, 1)
                gelu(0, 0)

                def quad(s):
                    for n in range(YB):
                        turned_rows(s + (n + 2), n % 2)
                        gelu(s + (n + 1), (n + 1) % 2)
                        output(s + n, n)

                quad(0)
                with act.Fori(1, QUADS) as quarter_s:
                    quad(quarter_s * YB)
                s = YB * QUADS
                turned_rows(s + 2, 0)
                gelu(s + 1, 1)
                output(s, 0)
                gelu(s + 2, 0)
                output(s + 1, 1)
                output(s + 2, 2)

            @block.vector
            def _(dve):
                tokens = x1_all[:].rearrange("p b t c -> p (b t) c")
                for t in range(TT):
                    last = dve.bn_stats(stats[:, t, :], x1_all[:, B - 1, t, :])
                last.then_inc(s_stats2, 1)
                dve.wait_ge(s_stats2, B)
                dve.memset(tick[:], 0.0)
                for t in range(TT):
                    last = dve.bn_aggr(mean_var[:, t, :], stats[:, t, :])
                last.then_inc(s_aggr2, 1)
                dve.wait_ge(s_aggr2, B)
                dve.tensor_scalar(var_eps[:], mean_var[:, :, 1], EPS, None, ALU.add).then_inc(s_var2, 1)
                dve.wait_ge(s_count, 1)
                dve.tensor_copy(count[:], bank[:, 3, 0:P + 1]).then_inc(s_countc, 1)
                dve.wait_ge(s_countc, 1)
                dve.tensor_copy(count_h[:], count[:, 0:P]).then_inc(s_countc, 1)
                dve.tensor_scalar(steps[:], count[:, 0:16], float(P), None, ALU.mult).then_inc(s_countc, 1)
                dve.tensor_tensor(earlier[:], count[:, 0:NE].unsqueeze(2).broadcast_to([P, NE, NE]),
                                  count[:, 0:NE].unsqueeze(1).broadcast_to([P, NE, NE]), ALU.is_gt).then_inc(s_countc, 1)
                dve.wait_ge(s_countc, 3)
                dve.scalar_tensor_tensor(out=token[:], in0=steps[:, 0:N], scalar=1.0,
                                         in1=count[:, P:P + 1].broadcast_to([P, N]), op0=ALU.add,
                                         op1=ALU.add).then_inc(s_countc, 1)
                dve.scalar_tensor_tensor(out=unused[:], in0=count[:, 0:NSLOT], scalar=float(P),
                                         in1=count[:, P:P + 1].broadcast_to([P, NSLOT]), op0=ALU.mult,
                                         op1=ALU.add).then_inc(s_countc, 1)
                dve.wait_ge(s_countc, 6)
                dve.tensor_scalar(unused[:], unused[:], float(2 * N * P + 1), None, ALU.add).then_inc(s_countc, 1)

                logits = lg[:].rearrange("p b (t e) -> p (b t) e", e=NE)
                for i in range(N - TT):
                    last = dve.max(top[:, i, :], logits[:, i, :])
                last.then_inc(s_top, 1)
                dve.wait_ge(s_top, 1)
                for i in range(N - TT):
                    dve.max_index(top_i[:, i, :], top[:, i, :], logits[:, i, :])
                dve.wait_ge(s_rstd2, B)
                for t in range(TT):
                    last = dve.tensor_scalar(xn[:, t, :], x1_all[:, B - 1, t, :], mean_var[:, t, 0:1], rstd[:, t:t + 1],
                                             ALU.subtract, ALU.mult)
                last.then_inc(s_xn2, 1)
                for k in range(KT):
                    dve.wait_ge(s_tr2hi, k + 1)
                    dve.tensor_tensor(xt_st[:, 1, k, :], bank[:, k, :], xt_st[:, 0, k, :], ALU.subtract).then_inc(s_tr2lo, 1)
                dve.wait_ge(s_logit, 1)
                dve.tensor_copy(lg[:, B - 1, :], bank[:, 2, 0:TT * NE]).then_inc(s_route, 1)
                dve.wait_ge(s_route, 1)
                for i in range(N - TT, N):
                    last = dve.max(top[:, i, :], logits[:, i, :])
                last.then_inc(s_route, 1)
                dve.wait_ge(s_route, 2)
                for i in range(N - TT, N):
                    dve.max_index(top_i[:, i, :], top[:, i, :], logits[:, i, :])
                dve.tensor_tensor(gap[:], top[:, :, 1], top[:, :, 0], ALU.subtract).then_inc(s_gap, 1)
                dve.wait_ge(s_gap, 1)
                dve.tensor_copy(top_f[:], top_i[:]).then_inc(s_route, 1)
                dve.wait_ge(s_route, 3)
                for choice in range(2):
                    last = dve.tensor_tensor(chosen[:, choice], count[:, 0:NE].unsqueeze(1).broadcast_to([P, N, NE]),
                                             top_f[:, :, choice:choice + 1].broadcast_to([P, N, NE]), ALU.is_equal)
                last.then_inc(s_route, 1)
                dve.wait_ge(s_route, 4)
                dve.tensor_tensor(chosen_bf[:, 0:N], chosen[:, 0], chosen[:, 1], ALU.add).then_inc(s_chosen, 1)
                dve.wait_ge(s_rank, 1)
                dve.tensor_copy(rank[:].rearrange("p i e -> p (i e)"), bank[:, 3, 0:(N + 1) * NE]).then_inc(s_place, 1)
                dve.wait_ge(s_place, 1)
                dve.tensor_tensor(fills[:], rank[:, N, :].unsqueeze(2).broadcast_to([P, NE, 16]),
                                  steps[:].unsqueeze(1).broadcast_to([P, NE, 16]), ALU.is_gt).then_inc(s_place, 1)
                dve.tensor_tensor(picked[:], chosen[:], rank[:, 0:N].unsqueeze(1).broadcast_to([P, 2, N, NE]),
                                  ALU.mult).then_inc(s_place, 1)
                dve.wait_ge(s_place, 3)
                dve.tensor_reduce(slots[:], fills[:], X, ALU.add).then_inc(s_place, 1)
                dve.tensor_reduce(my_rank[:], picked[:], X, ALU.add).then_inc(s_place, 1)
                dve.wait_ge(s_place, 5)
                dve.tensor_tensor(base_of[:], earlier[:], slots[:].unsqueeze(1).broadcast_to([P, NE, NE]),
                                  ALU.mult).then_inc(s_place, 1)
                dve.tensor_tensor(past[:], my_rank[:].rearrange("p a i -> p (a i)").unsqueeze(2).broadcast_to([P, 2 * N, 16]),
                                  steps[:].unsqueeze(1).broadcast_to([P, 2 * N, 16]), ALU.is_ge).then_inc(s_place, 1)
                dve.wait_ge(s_place, 7)
                dve.tensor_reduce(base[:], base_of[:], X, ALU.add).then_inc(s_place, 1)
                dve.tensor_reduce(my_tile[:].rearrange("p a i -> p (a i)"), past[:], X, ALU.add).then_inc(s_place, 1)
                dve.wait_ge(s_place, 9)
                dve.tensor_scalar(my_tile[:], my_tile[:], -1.0, None, ALU.add).then_inc(s_place, 1)
                dve.tensor_tensor(picked2[:], chosen[:], base[:].unsqueeze(1).unsqueeze(1).broadcast_to([P, 2, N, NE]),
                                  ALU.mult).then_inc(s_place, 1)
                dve.wait_ge(s_place, 11)
                dve.tensor_reduce(my_base[:], picked2[:], X, ALU.add).then_inc(s_place, 1)
                dve.scalar_tensor_tensor(out=my_row[:], in0=my_tile[:], scalar=-float(P), in1=my_rank[:],
                                         op0=ALU.mult, op1=ALU.add).then_inc(s_place, 1)
                dve.wait_ge(s_place, 13)
                dve.tensor_tensor(my_slot[:], my_base[:], my_tile[:], ALU.add).then_inc(s_place, 1)
                dve.wait_ge(s_place, 14)
                for choice in range(2):
                    dve.tensor_tensor(slot_at[:, choice], count_h[:, 0:NSLOT].unsqueeze(1).broadcast_to([P, N, NSLOT]),
                                      my_slot[:, choice].unsqueeze(2).broadcast_to([P, N, NSLOT]),
                                      ALU.is_equal).then_inc(s_slotat, 1)
                    for part_ in range(2):
                        i = slice(part_ * (N // 2), (part_ + 1) * (N // 2))
                        dve.tensor_tensor(row_hot[:, choice, i, :], count_h[:].unsqueeze(1).broadcast_to([P, N // 2, P]),
                                          my_row[:, choice, i].unsqueeze(2).broadcast_to([P, N // 2, P]),
                                          ALU.is_equal).then_inc(s_rowhot, 1)
                dve.tensor_tensor(at_or_after[:], count[:, 0:NSLOT].unsqueeze(2).broadcast_to([P, NSLOT, NE]),
                                  base[:].unsqueeze(1).broadcast_to([P, NSLOT, NE]), ALU.is_ge).then_inc(s_place, 1)
                dve.wait_ge(s_place, 15)
                dve.tensor_reduce(expert_f[:], at_or_after[:], X, ALU.add).then_inc(s_place, 1)
                dve.wait_ge(s_place, 16)
                dve.tensor_scalar(expert[:], expert_f[:], -1.0, None, ALU.add).then_inc(s_expert, 1)
                dve.wait_ge(s_rank, 2)
                dve.tensor_scalar(source[:], bank[:, 3, 0:NSLOT], -1.0, 0.0, ALU.add, ALU.max).then_inc(s_inverse, 1)
                dve.tensor_copy(filled[:], bank[:, 3, 0:NSLOT]).then_inc(s_place, 1)
                dve.wait_ge(s_place, 17)
                dve.scalar_tensor_tensor(out=unfilled[:], in0=filled[:], scalar=0.0, in1=unused[:], op0=ALU.is_equal,
                                         op1=ALU.mult).then_inc(s_place, 1)
                dve.wait_ge(s_place, 18)
                dve.tensor_tensor(filled[:], filled[:], unfilled[:], ALU.add).then_inc(s_place, 1)
                dve.wait_ge(s_place, 19)
                dve.scalar_tensor_tensor(out=unfilled[:], in0=bank[:, 3, P:P + NSLOT], scalar=float(N * P), in1=filled[:],
                                         op0=ALU.mult, op1=ALU.add).then_inc(s_place, 1)
                dve.wait_ge(s_place, 20)
                dve.tensor_scalar(target[:], unfilled[:], -1.0, None, ALU.add).then_inc(s_inverse, 1)

                def weights(s, n):
                    e = dve.value_load(expert[0:1, bass.ds(s, 1)], min_val=0, max_val=NE - 1)
                    if not (isinstance(s, int) and s < RB):
                        dve.wait_ge(s_down, s - RB + 1)
                        dve.memset(ticks[:, n:n + 1], 0.0)
                    dve.tensor_copy(w_slot[:, n].rearrange("p a l n -> p (a l n)"),
                                    we[:, bass.ds(e, 1)].rearrange("p e a l n -> p (e a l n)")).then_inc(s_wslot, 1)

                def hidden_low(s, par):
                    dve.wait_ge(s_gelu, s + 1)
                    dve.tensor_tensor(h_lo[:, par], h32[:, par], h_hi[:, par], ALU.subtract).then_inc(s_hlo, 1)

                dve.wait_ge(s_expert, 1)
                dve.wait_ge(s_elo, 2 * NE)
                dve.memset(tick[:], 0.0)
                weights(0, 0)
                weights(1, 1)
                dve.wait_ge(s_gexp, 1)
                dve.tensor_scalar(g_sum[:], gap_e[:], 1.0, None, ALU.add).then_inc(s_route, 1)
                dve.wait_ge(s_route, 5)
                dve.reciprocal(gates[:, 0], g_sum[:]).then_inc(s_route, 1)
                dve.wait_ge(s_route, 6)
                dve.tensor_scalar(gates[:, 0], gates[:, 0], tanh_g[:, 1:2], None, ALU.mult).then_inc(s_route, 1)
                dve.wait_ge(s_route, 7)
                dve.tensor_tensor(gates[:, 1], gates[:, 0], gap_e[:], ALU.mult).then_inc(s_route, 1)
                hidden_low(0, 0)

                def quad(s):
                    for n in range(RB):
                        weights(s + (n + 2), (n + 2) % RB)
                        hidden_low(s + (n + 1), (n + 1) % 2)

                quad(0)
                with dve.Fori(1, QUADS) as quarter_s:
                    quad(quarter_s * RB)
                s = RB * QUADS
                weights(s + 2, 2)
                hidden_low(s + 1, 1)
                hidden_low(s + 2, 0)
                for b in range(B):
                    dve.wait_ge(s_back[b], 32)
                    for choice in range(2):
                        if choice:
                            dve.wait_ge(s_acc, (2 * b + 1) * TT)
                        for t in range(TT):
                            i = b * TT + t
                            dve.scalar_tensor_tensor(out=tokens[:, i, :], in0=back[:, choice, b, t, :],
                                                     scalar=gates[:, choice, i:i + 1], in1=tokens[:, i, :],
                                                     op0=ALU.mult, op1=ALU.add).then_inc(s_acc, 1)

            @block.tensor
            def _(pe):
                pe.wait_ge(s_mask, 6)
                pe.matmul(bank[:, 3, 0:P], ones[:], before[:], start=True, stop=True)
                pe.matmul(bank[:, 3, P:P + 1], before[:], ones[:, 0:1], start=True, stop=True).then_inc(s_count, 1)
                pe.wait_ge(s_xn2, B)
                for k in range(KT):
                    for t in range(TT):
                        last = pe.transpose(bank[:, k, t * P:(t + 1) * P], xn[:, t, k * P:(k + 1) * P], ident[:])
                    last.then_inc(s_tr2, 1)
                pe.wait_ge(s_tr2lo, KT)
                for t in range(TT):
                    ts = slice(t * P, (t + 1) * P)
                    for k in range(KT):
                        for a, w in ((0, wr_hi), (0, wr_lo), (1, wr_hi)):
                            last = pe.matmul(bank[:, 2, t * NE:(t + 1) * NE], xt_st[:, a, k, ts], w[:, k, :],
                                             start=(k == 0 and a == 0 and w is wr_hi), stop=(k == KT - 1 and a == 1))
                last.then_inc(s_logit, 1)
                pe.wait_ge(s_chosen, 1)
                pe.matmul(bank[:, 3, 0:(N + 1) * NE], before[:], chosen_bf[:].rearrange("p i e -> p (i e)"),
                          start=True, stop=False)
                for i in range(N):
                    last = pe.matmul(bank[:, 3, (i + 1) * NE:(N + 1) * NE], ones[:],
                                     chosen_bf[:, i:i + 1, :].broadcast_to([P, N - i, NE]), start=False, stop=(i == N - 1))
                last.then_inc(s_rank, 1)
                for choice in range(2):
                    pe.wait_ge(s_slot, choice + 1)
                    for i in range(N):
                        if i % (N // 2) == 0:
                            pe.wait_ge(s_rowhot, 2 * choice + i // (N // 2) + 1)
                        last = pe.matmul(bank[:, 3, 0:NSLOT], row_hot[:, choice, i, :], slot_hot[:, choice, i, :],
                                         start=(choice == 0 and i == 0), stop=(choice == 1 and i == N - 1))
                for i in range(N):
                    last = pe.matmul(bank[:, 3, P:P + NSLOT], row_hot[:, 1, i, :], slot_at[:, 1, i, :],
                                     start=(i == 0), stop=(i == N - 1))
                last.then_inc(s_rank, 1)

                def turn(s, n):
                    par = n % 2
                    pe.wait_ge(s_xs[n], (s - n) * (16 // RB) + 16)
                    wait(pe, s_xt, s - 1)
                    to = bank[:, par].bitcast(F16)
                    for a in range(4):
                        last = pe.transpose(to[:, a * P:(a + 1) * P], xs[:, n, a * P:(a + 1) * P], ident_h[:])
                    last.then_inc(s_st, 1)

                def up(s, n):
                    par = n % 2
                    pe.wait_ge(s_xt, s + 1)
                    pe.wait_ge(s_wslot, s + 1)
                    wait(pe, s_gelu, s - 1)
                    for m in range(FT):
                        for k in range(KT):
                            for w, a in ((0, 0), (0, 1), (1, 0)):
                                at = k * F + m * P
                                last = pe.matmul(bank[:, 2 + par, m * P:(m + 1) * P],
                                                 w_slot[:, n, 0, w, at:at + P], xt[:, par, 2 * a + k, :],
                                                 start=(k == 0 and w == 0 and a == 0), stop=(k == KT - 1 and w == 1))
                    last.then_inc(s_up, 1)

                def down(s, n):
                    par = n % 2
                    pe.wait_ge(s_hlo, s + 1)
                    wait(pe, s_yev, s - 1)
                    for m in range(FT):
                        for h, w in ((h_hi, 0), (h_hi, 1), (h_lo, 0)):
                            last = pe.matmul(bank[:, 4 + par, 0:C], h[:, par, m, :], w_slot[:, n, 1, w, m * C:(m + 1) * C],
                                             start=(m == 0 and h is h_hi and w == 0), stop=(m == FT - 1 and h is h_lo))
                    last.then_inc(s_down, 1)

                turn(0, 0)
                turn(1, 1)
                up(0, 0)

                def quad(s):
                    for n in range(RB):
                        turn(s + (n + 2), (n + 2) % RB)
                        up(s + (n + 1), (n + 1) % RB)
                        down(s + n, n)

                quad(0)
                with pe.Fori(1, QUADS) as quarter_s:
                    quad(quarter_s * RB)
                s = RB * QUADS
                turn(s + 2, 2)
                up(s + 1, 1)
                down(s, 0)
                up(s + 2, 2)
                down(s + 1, 1)
                down(s + 2, 2)


_INS = ['x', 'ctx_512', 'g_xattn', 'g_ffn', 'L0_xattn_Wk', 'L0_xattn_bk', 'L0_xattn_Wq', 'L0_xattn_bq',
        'L0_xattn_Wv', 'L0_xattn_bv', 'L0_xattn_Wck', 'L0_xattn_bck', 'L0_xattn_Wcq', 'L0_xattn_bcq',
        'L0_xattn_Wcv', 'L0_xattn_bcv', 'L0_xattn_Wp', 'L0_xattn_bp', 'L0_ffn_router_w', 'L0_ffn_w1', 'L0_ffn_w2']
_OUTS = [((4, 512, 256), 'float32')]


def kernel(**inputs):
    import numpy as _np
    import concourse.bacc as _bacc
    from concourse import mybir as _mybir
    from concourse.bass_utils import run_bass_kernel_spmd as _run

    nc = _bacc.Bacc("TRN2", target_bir_lowering=False, num_devices=1)
    arrays, args = {}, []
    for name in _INS:
        a = _np.ascontiguousarray(inputs[name])
        arrays[f"in_{name}_dram"] = a
        args.append(nc.dram_tensor(f"in_{name}_dram", a.shape, _mybir.dt.from_np(a.dtype), kind="ExternalInput").ap())
    for i, (shape, dtype) in enumerate(_OUTS):
        dt = _mybir.dt.from_np(_np.dtype(dtype))
        args.append(nc.dram_tensor(f"out_{i}_dram", shape, dt, kind="ExternalOutput").ap())
    flamingo_layer(nc, *args)
    r = _run(nc, [arrays], core_ids=[0])
    got = tuple(r.results[0][f"out_{i}_dram"] for i in range(len(_OUTS)))
    return got[0]
```
